# Optimizing a Trainium2 kernel written in Bass

```python
import numpy as np
import jax
import jax.numpy as jnp

def _softmax(x, axis=-1):
    return jax.nn.softmax(x, axis=axis)

def _gelu(x):
    return jax.nn.gelu(x, approximate=True)

def _silu(x):
    return jax.nn.silu(x)

def _sigmoid(x):
    return jax.nn.sigmoid(x)

def _layernorm(x, axis=-1, eps=1e-05):
    m = jnp.mean(x, axis=axis, keepdims=True)
    v = jnp.var(x, axis=axis, keepdims=True)
    return (x - m) / jnp.sqrt(v + eps)

def _scatter_add(tgt, idx, src, axis=0):
    return tgt.at[idx].add(src)

def _segment_sum(src, seg, n):
    return jax.ops.segment_sum(src, seg, n)
kernel_name = 'mk_perceiver_d1_seqx_r4_2c56cd'

def setup_inputs(seed: int=0):
    np.random.seed(seed)
    _w = jnp.asarray

    def _rec_inputs():
        import jax
        import jax.numpy as jnp
        _rk = jax.random.key(seed)
        x = -0.0002928 + 1 * jax.random.normal(jax.random.fold_in(_rk, 1), (32, 64, 256), jnp.float32)
        _lenS = 64 - jax.random.randint(jax.random.fold_in(_rk, 7), (32,), 0, max(1, 64 // 4) + 1, jnp.int32)
        _lenS2 = 1601 - jax.random.randint(jax.random.fold_in(_rk, 8), (32,), 0, max(1, 1601 // 4) + 1, jnp.int32)
        _ctx_1024P = jax.random.normal(jax.random.fold_in(_rk, 11), (32, 16, 256), jnp.float32)
        _ctx_1024c = jax.random.dirichlet(jax.random.fold_in(_rk, 511), 0.3 * jnp.ones((16,), jnp.float32), (32, 1601))
        _ctx_1024t = jnp.einsum('bsk,bkd->bsd', _ctx_1024c, _ctx_1024P)
        _ctx_1024t = _ctx_1024t * jax.lax.rsqrt(jnp.mean(jnp.square(_ctx_1024t)) + 1e-12) * 0.953939
        ctx_1024 = -1.39393e-06 + 0.999914 * (_ctx_1024t + 0.3 * jax.random.normal(jax.random.fold_in(_rk, 611), (32, 1601, 256), jnp.float32))
        _validS = jnp.arange(64)[None, :] < _lenS[:, None]
        _validS2 = jnp.arange(1601)[None, :] < _lenS2[:, None]
        _causal = jnp.tril(jnp.ones((64, 64), dtype=bool))
        mask_1x1xSxS2_bf1 = jnp.ones((1, 1, 64, 1601), dtype=bool)
        return (x, ctx_1024, mask_1x1xSxS2_bf1)
    x, ctx_1024, mask_1x1xSxS2_bf1 = _rec_inputs()

    def _L0_xattn_setup():
        import jax, jax.numpy as jnp
        import numpy as np
        D_MODEL = 256
        H = 16
        D_K = D_MODEL // H
        B, S = (2, 512)

        def _split_heads(x):
            b, s, _ = x.shape
            return x.reshape(b, s, H, D_K).transpose(0, 2, 1, 3)
        key = jax.random.key(seed)
        ks = jax.random.split(key, 11)
        sc = 1.0 / np.sqrt(D_MODEL)
        inp = {'q': jax.random.normal(ks[0], (B, S, D_MODEL), jnp.float32), 'k': jax.random.normal(ks[1], (B, S, D_MODEL), jnp.float32), 'v': jax.random.normal(ks[2], (B, S, D_MODEL), jnp.float32), 'mask': jnp.ones((1, 1, S, S), dtype=bool), 'wq_w': jax.random.normal(ks[3], (D_MODEL, D_MODEL), jnp.float32) * sc, 'wq_b': jnp.zeros((D_MODEL,), jnp.float32), 'wk_w': jax.random.normal(ks[4], (D_MODEL, D_MODEL), jnp.float32) * sc, 'wk_b': jnp.zeros((D_MODEL,), jnp.float32), 'wv_w': jax.random.normal(ks[5], (D_MODEL, D_MODEL), jnp.float32) * sc, 'wv_b': jnp.zeros((D_MODEL,), jnp.float32), 'wo_w': jax.random.normal(ks[6], (D_MODEL, D_MODEL), jnp.float32) * sc, 'wo_b': jnp.zeros((D_MODEL,), jnp.float32)}
        return inp
    _L0_xattn_all = _L0_xattn_setup()
    _L0_xattn_in = {k: v for k, v in _L0_xattn_all.items() if k in ('wq_w', 'wq_b', 'wk_w', 'wk_b', 'wv_w', 'wv_b', 'wo_w', 'wo_b')}
    del _L0_xattn_all

    def _L0_attn_setup():
        import jax, jax.numpy as jnp
        import numpy as np
        B, M, HS, K = (2, 512, 256, 16)
        D = HS // K

        def _head_reshape(x, d):
            b, m, _ = x.shape
            return x.reshape(b, m, K, d).transpose(0, 2, 1, 3).reshape(b * K, m, d)
        key = jax.random.key(seed)
        k1, k2, k3, k4 = jax.random.split(key, 4)
        s = 1.0 / np.sqrt(HS)
        return {'h': jax.random.normal(k1, (B, M, HS), jnp.float32), 'W_span': jax.random.normal(k2, (2 * K, HS), jnp.float32) * s, 'W_val': jax.random.normal(k3, (HS, HS), jnp.float32) * s, 'W_out': jax.random.normal(k4, (HS, HS), jnp.float32) * s}
    _L0_attn_all = _L0_attn_setup()
    _L0_attn_in = {k: v for k, v in _L0_attn_all.items() if k in ('W_span', 'W_val', 'W_out')}
    del _L0_attn_all

    def _L0_ffn_setup():
        import jax, jax.numpy as jnp
        import numpy as np
        E = 8
        TOPK = 2
        PRIME = 11
        HASH_OFF = 7919
        N_SHARED = 1
        key = jax.random.key(seed)
        ks = jax.random.split(key, 8)
        B, T, C, Hs, Hr = (4, 2048, 256, 512, 256)
        sc = lambda k, shape, fan: jax.random.normal(k, shape, jnp.float32) * fan ** (-0.5)
        return {'x': jax.random.normal(ks[0], (B, T, C), jnp.float32), 't_emb': jax.random.normal(ks[1], (B, C), jnp.float32), 'sw1': sc(ks[2], (C, Hs), C), 'sb1': jnp.zeros((Hs,), jnp.float32), 'sw3': sc(ks[3], (C, Hs), C), 'sb3': jnp.zeros((Hs,), jnp.float32), 'sw2': sc(ks[4], (Hs, C), Hs), 'sb2': jnp.zeros((C,), jnp.float32), 'w1': sc(ks[5], (E, C, Hr), C), 'b1': jnp.zeros((E, Hr), jnp.float32), 'w2': sc(ks[6], (E, Hr, C), Hr), 'b2': jnp.zeros((E, C), jnp.float32)}
    _L0_ffn_all = _L0_ffn_setup()
    _L0_ffn_in = {k: v for k, v in _L0_ffn_all.items() if k in ('t_emb', 'sw1', 'sb1', 'sw3', 'sb3', 'sw2', 'sb2', 'w1', 'b1', 'w2', 'b2')}
    del _L0_ffn_all
    return {'x': x, 'ctx_1024': ctx_1024, 'mask_1x1xSxS2_bf1': mask_1x1xSxS2_bf1, 'L0_xattn_wq_w': _L0_xattn_in['wq_w'], 'L0_xattn_wq_b': _L0_xattn_in['wq_b'], 'L0_xattn_wk_w': _L0_xattn_in['wk_w'], 'L0_xattn_wk_b': _L0_xattn_in['wk_b'], 'L0_xattn_wv_w': _L0_xattn_in['wv_w'], 'L0_xattn_wv_b': _L0_xattn_in['wv_b'], 'L0_xattn_wo_w': _L0_xattn_in['wo_w'], 'L0_xattn_wo_b': _L0_xattn_in['wo_b'], 'L0_attn_W_span': _L0_attn_in['W_span'], 'L0_attn_W_val': _L0_attn_in['W_val'], 'L0_attn_W_out': _L0_attn_in['W_out'], 'L0_ffn_t_emb': _L0_ffn_in['t_emb'], 'L0_ffn_sw1': _L0_ffn_in['sw1'], 'L0_ffn_sb1': _L0_ffn_in['sb1'], 'L0_ffn_sw3': _L0_ffn_in['sw3'], 'L0_ffn_sb3': _L0_ffn_in['sb3'], 'L0_ffn_sw2': _L0_ffn_in['sw2'], 'L0_ffn_sb2': _L0_ffn_in['sb2'], 'L0_ffn_w1': _L0_ffn_in['w1'], 'L0_ffn_b1': _L0_ffn_in['b1'], 'L0_ffn_w2': _L0_ffn_in['w2'], 'L0_ffn_b2': _L0_ffn_in['b2']}

def reference(x, ctx_1024, mask_1x1xSxS2_bf1, L0_xattn_wq_w, L0_xattn_wq_b, L0_xattn_wk_w, L0_xattn_wk_b, L0_xattn_wv_w, L0_xattn_wv_b, L0_xattn_wo_w, L0_xattn_wo_b, L0_attn_W_span, L0_attn_W_val, L0_attn_W_out, L0_ffn_t_emb, L0_ffn_sw1, L0_ffn_sb1, L0_ffn_sw3, L0_ffn_sb3, L0_ffn_sw2, L0_ffn_sb2, L0_ffn_w1, L0_ffn_b1, L0_ffn_w2, L0_ffn_b2):
    import jax
    import jax.numpy as jnp

    def _L0_xattn_ref(q, k, v, mask, wq_w, wq_b, wk_w, wk_b, wv_w, wv_b, wo_w, wo_b):
        import jax, jax.numpy as jnp
        import numpy as np
        D_MODEL = 256
        H = 16
        D_K = D_MODEL // H
        B, S = (2, 512)

        def _split_heads(x):
            b, s, _ = x.shape
            return x.reshape(b, s, H, D_K).transpose(0, 2, 1, 3)
        qh = _split_heads(q @ wq_w.T + wq_b)
        kh = _split_heads(k @ wk_w.T + wk_b)
        vh = _split_heads(v @ wv_w.T + wv_b)
        scores = jnp.einsum('bhqd,bhkd->bhqk', qh, kh) / jnp.sqrt(jnp.float32(D_K))
        scores = jnp.where(mask, scores, jnp.float32(-1000000000.0))
        attn = jax.nn.softmax(scores, axis=-1)
        out = jnp.einsum('bhqk,bhkd->bhqd', attn, vh)
        out = out.transpose(0, 2, 1, 3).reshape(q.shape[0], q.shape[1], D_MODEL)
        return out @ wo_w.T + wo_b

    def _L0_attn_ref(h, W_span, W_val, W_out):
        import jax, jax.numpy as jnp
        import numpy as np
        B, M, HS, K = (2, 512, 256, 16)
        D = HS // K

        def _head_reshape(x, d):
            b, m, _ = x.shape
            return x.reshape(b, m, K, d).transpose(0, 2, 1, 3).reshape(b * K, m, d)
        b, m, hs = h.shape
        span = _head_reshape(h @ W_span.T, 2)
        value = _head_reshape(h @ W_val.T, D)
        pos = jnp.arange(m, dtype=h.dtype)
        mean = jax.nn.sigmoid(span[..., 0]) * m
        soft = jax.nn.softplus(span[..., 1])
        diff = pos[None, None, :] - mean[..., None]
        scores = -soft[..., None] * (diff * diff)
        attn = jax.nn.softmax(scores, axis=-1)
        out = jnp.matmul(attn, value)
        out = out.reshape(b, K, m, D).transpose(0, 2, 1, 3).reshape(b, m, hs)
        return out @ W_out.T

    def _L0_ffn_ref(x, t_emb, sw1, sb1, sw3, sb3, sw2, sb2, w1, b1, w2, b2):
        import jax, jax.numpy as jnp
        import numpy as np
        E = 8
        TOPK = 2
        PRIME = 11
        HASH_OFF = 7919
        N_SHARED = 1
        B, T, C = x.shape
        N = B * T
        xf = x.reshape(N, C)
        shared = jax.nn.silu(xf @ sw1 + sb1) * (xf @ sw3 + sb3) @ sw2 + sb2
        tok = jnp.arange(N)
        out = jnp.zeros((N, C), x.dtype)
        for k in range(TOPK):
            exp_ids = (tok * PRIME + k * HASH_OFF) % E
            sort_idx = jnp.argsort(exp_ids)
            xs = xf[sort_idx].reshape(E, N // E, C)
            h = jax.nn.gelu(jnp.einsum('enc,ech->enh', xs, w1) + b1[:, None, :], approximate=False)
            y = jnp.einsum('enh,ehc->enc', h, w2) + b2[:, None, :]
            out = out.at[sort_idx].add(y.reshape(N, C))
        out = out / TOPK
        return ((shared + out) / (N_SHARED + 1)).reshape(B, T, C)
    x = x + _L0_xattn_ref(_layernorm(x, axis=-1), ctx_1024, ctx_1024, mask_1x1xSxS2_bf1, L0_xattn_wq_w, L0_xattn_wq_b, L0_xattn_wk_w, L0_xattn_wk_b, L0_xattn_wv_w, L0_xattn_wv_b, L0_xattn_wo_w, L0_xattn_wo_b)
    x = x + _L0_attn_ref(_layernorm(x, axis=-1), L0_attn_W_span, L0_attn_W_val, L0_attn_W_out)
    x = x + _L0_ffn_ref(_layernorm(x, axis=-1), L0_ffn_t_emb, L0_ffn_sw1, L0_ffn_sb1, L0_ffn_sw3, L0_ffn_sb3, L0_ffn_sw2, L0_ffn_sb2, L0_ffn_w1, L0_ffn_b1, L0_ffn_w2, L0_ffn_b2)
    return x

_drawn_inputs = setup_inputs


def setup_inputs(seed=0):
    import zlib

    import numpy as np

    out = dict(_drawn_inputs(seed))
    spreads = {'L0_xattn_wq_b': (0.0, 0.1),
     'L0_xattn_wk_b': (0.0, 0.8),
     'L0_xattn_wv_b': (0.0, 0.1),
     'L0_xattn_wo_b': (0.0, 0.1),
     'L0_ffn_sb1': (0.0, 0.354),
     'L0_ffn_sb3': (0.0, 0.365),
     'L0_ffn_sb2': (0.0, 0.1),
     'L0_ffn_b1': (0.0, 0.469),
     'L0_ffn_b2': (0.0, 0.318)}
    factors = {}
    for name, (base, spread) in spreads.items():
        noise = np.random.default_rng([zlib.crc32(name.encode()), seed]).standard_normal(out[name].shape)
        drawn = base * np.exp(spread * noise) if base else spread * noise
        out[name] = jnp.asarray(drawn.astype(out[name].dtype))
    for name, factor in factors.items():
        out[name] = (out[name] * factor).astype(out[name].dtype)
    return out
```

```python
from contextlib import ExitStack

import numpy as np

import concourse.bass as bass
from concourse import mybir

F32 = mybir.dt.float32
F32R = mybir.dt.float32r
BF16 = mybir.dt.bfloat16
F16 = mybir.dt.float16
U8 = mybir.dt.uint8
ALU = mybir.AluOpType
ACT = mybir.ActivationFunctionType
AX = mybir.AxisListType

P = 128
B, S, S2, D = 32, 64, 1601, 256
H = 16
DK = D // H
NTOK = B * S
NK = D // P
PAIRS = H // 2
GROUPS = 4
PW = 2 * S
KT = -(-S2 // P)
S2P = S2 + 1
KC = 4
CHUNKS = [(0, 400), (400, 400), (800, 400), (1200, 402)]
MAXCH = [(0, 400), (400, 400), (800, 400), (1200, 401)]
NCK = NK * KC
NMX = PAIRS * KC
NST = 2 * KT
NACC = KT - 1
NP = 5
SPLIT = NK * KC
UP = 32.0
SEL = 1024.0
MASKED = -float(2 ** 25)
KSTACK = 3 * 32
KROWS = KSTACK + PAIRS
EPS = 1e-5
HS = 512
E = 8
PRIME, HASH = 11, 7919
NCH = 4
CW = NTOK // NCH
CB = CW // S
ROUND = 1.5 * 2.0 ** 23

CLASS_EXPERTS = [[(c * PRIME + k * HASH) % E for k in range(2)] for c in range(E)]


def keys_of(kt):
    return min(P, S2 - kt * P)


class Batch:

    def __init__(self, n, slot, used):
        self.n, self.slot, self.used = n, slot, used


def at(n):
    return Batch(n, n % 2, n // 2 + 1)


def loop_batch(t, offset):
    return Batch(2 * t + offset, offset % 2, t + offset // 2 + 1)


def first(b):
    return isinstance(b.n, int) and b.n == 0


def before(b):
    return Batch(b.n - 1, 1 - b.slot, None)


def need(eng, sem, value):
    if not isinstance(value, int) or value > 0:
        eng.wait_ge(sem, value)


def build(nc, ins, out_dram):
    ctx = ExitStack()
    with ctx:
        def sem(name):
            return ctx.enter_context(nc.semaphore(name))

        bank = [ctx.enter_context(nc.psum_tensor(f"bank{i}", [P, 512], F32)) for i in range(8)]
        attn_out = ctx.enter_context(nc.sbuf_tensor("attn_out", [P, NK, NTOK], F32))
        ident = ctx.enter_context(nc.sbuf_tensor("ident", [P, P], F32))
        mean_w = ctx.enter_context(nc.sbuf_tensor("mean_w", [P, P], F32))
        eps_col = ctx.enter_context(nc.sbuf_tensor("eps_col", [P, 1], F32))
        q_parts = nc.dram_tensor("q_parts", (2, D, NTOK), F16).ap()
        with ExitStack() as cross:
            def sb(name, shape, dt):
                return cross.enter_context(nc.sbuf_tensor(name, shape, dt))
            w = dict(
                wk_hi=sb("wk_hi", [P, NK, D], F32R), wk_lo=sb("wk_lo", [P, NK, D], F32R),
                wv_hi=sb("wv_hi", [P, NK, D], F32R), wv_lo=sb("wv_lo", [P, NK, D], F32R),
                bk=sb("bk", [P, NK], F32), bv=sb("bv", [P, NK], F32),
                even_rows=sb("even_rows", [P, 2], F32),
                mask_q=sb("mask_q", [P, S2], BF16), mask_k=sb("mask_k", [P, KT, S], BF16),
                rows_all=sb("rows_all", [1, 1], mybir.dt.int32),
                ident_h=sb("ident_h", [P, P], BF16), ones=sb("ones", [P, 32], F32),
            )
            queries(nc, ctx, ins, bank, w, ident, mean_w, eps_col, q_parts, sem)
            cross_attention(nc, sb, ins, bank, w, ident, attn_out, q_parts, sem)
        tail(nc, ctx, ins, bank, attn_out, mean_w, eps_col, out_dram, sem)


def queries(nc, ctx, ins, bank, w, ident, mean_w, eps_col, q_parts, sem):
    with ExitStack() as own:
        def sb(name, shape, dt):
            return own.enter_context(nc.sbuf_tensor(name, shape, dt))

        x = sb("x0", [P, NK, NTOK], F32)
        wq = sb("wq", [P, NK, D], F32)
        wk = sb("wk", [P, NK, D], F32)
        wv = sb("wv", [P, NK, D], F32)
        bq = sb("bq", [P, NK], F32)
        bk_raw = sb("bk_raw", [P, NK], F32)
        mask_u8 = sb("mask_u8", [P, S2], U8)
        maskT_u8 = sb("maskT_u8", [P, KT, S], U8)
        row_ok = sb("row_ok", [S, 1], F32)
        row_all = sb("row_all", [S, 1], F32)
        row_diag = sb("row_diag", [S, S], F32)
        row_live = sb("row_live", [P, S], F32)
        ones_q = sb("ones_q", [S, P], F32)
        xc = sb("xc0", [P, NK, CW], F32)
        sq = sb("sq0", [P, NK, CW], F32)
        std = sb("std0", [P, CW], F32)
        rstd = sb("rstd0", [P, CW], F32)
        xn = sb("xn0", [P, NK, CW], F32)
        q = sb("q0", [P, NK, CW], F32)
        q_hi = sb("q_hi", [P, NK, NTOK], F16)
        q_lo = sb("q_lo", [P, NK, NTOK], F16)

        const_in = sem("const_in")
        x_in = sem("x_in")
        w_in = sem("w_in")
        mask_in = sem("mask_in")
        vec = sem("q_vec")
        consts = sem("q_consts")
        mean = sem("q_mean")
        xc_ready = sem("q_xc")
        sq_ready = sem("q_sq")
        var = sem("q_var")
        std_ready = sem("q_std")
        xn_ready = sem("q_xn")
        proj = sem("q_proj")
        q_done = sem("q_done")
        all_ready = sem("q_all")
        diag_ready = sem("q_diag")
        live_ready = sem("q_live")
        q_out = sem("q_out")

        with nc.Block() as block:
            @block.sync
            def _(sp):
                sp.dma_start(x[:], ins["xT"].rearrange("(k p) t -> p k t", p=P)).then_inc(x_in, 16)
                sp.dma_start(ident[:], ins["c_ident"]).then_inc(const_in, 16)
                sp.dma_start(w["even_rows"][:], ins["c_even"]).then_inc(const_in, 16)
                for name, tile in (("wqT", wq), ("wkT", wk), ("wvT", wv)):
                    sp.dma_start(tile[:], ins[name].rearrange("(k p) n -> p k n", p=P)).then_inc(w_in, 16)
                for name, tile in (("bq", bq), ("bk", bk_raw), ("bv", w["bv"])):
                    sp.dma_start(tile[:], ins[name]).then_inc(w_in, 16)
                for e in range(2):
                    sp.dma_start(mask_u8[S * e:S * e + S, :], ins["maskQ"]).then_inc(mask_in, 16)
                sp.dma_start(maskT_u8[:], ins["maskT"].rearrange("(n p) q -> p n q", p=P)).then_inc(mask_in, 16)
                sp.wait_ge(q_done, 2 * NCH)
                for i, part in enumerate((q_hi, q_lo)):
                    sp.dma_start(q_parts[i].rearrange("(k p) t -> p k t", p=P), part[:]).then_inc(q_out, 16)
                sp.wait_ge(q_out, 32)

            @block.vector
            def _(dve):
                steps = [0]

                def step(instruction):
                    instruction.then_inc(vec, 1)
                    steps[0] += 1
                    dve.wait_ge(vec, steps[0])

                nc.vector.memset(mean_w[:], 1.0 / D).then_inc(consts, 1)
                nc.vector.memset(eps_col[:], EPS).then_inc(consts, 1)
                nc.vector.memset(w["ones"][:], 1.0).then_inc(consts, 1)
                nc.vector.memset(ones_q[:], 1.0).then_inc(consts, 1)
                dve.wait_ge(const_in, 32)
                nc.vector.tensor_copy(w["ident_h"][:], ident[:]).then_inc(consts, 1)
                dve.wait_ge(mask_in, 48)
                nc.vector.tensor_scalar(w["mask_q"][:], mask_u8[:], -1.0, -MASKED, ALU.add, ALU.mult).then_inc(consts, 1)
                nc.vector.tensor_scalar(w["mask_k"][:], maskT_u8[:], -1.0, -MASKED, ALU.add, ALU.mult).then_inc(consts, 1)
                nc.vector.tensor_reduce(row_all[:], mask_u8[0:S, :], AX.X, ALU.min).then_inc(all_ready, 1)
                step(nc.vector.tensor_reduce(row_ok[:], mask_u8[0:S, :], AX.X, ALU.max))
                nc.vector.tensor_scalar(row_diag[:], ident[0:S, 0:S], row_ok[:, 0:1], None, ALU.mult).then_inc(diag_ready, 1)
                dve.wait_ge(w_in, 6 * 16)
                step(nc.vector.tensor_scalar(w["wk_hi"][:], wk[:], UP, None, ALU.mult))
                nc.vector.scalar_tensor_tensor(w["wk_lo"][:], wk[:], UP, w["wk_hi"][:].bitcast(F32),
                                               ALU.mult, ALU.subtract).then_inc(consts, 1)
                step(nc.vector.tensor_copy(w["wv_hi"][:], wv[:]))
                nc.vector.tensor_tensor(w["wv_lo"][:], wv[:], w["wv_hi"][:].bitcast(F32), ALU.subtract).then_inc(consts, 1)
                nc.vector.tensor_scalar(w["bk"][:], bk_raw[:], UP, None, ALU.mult).then_inc(consts, 1)
                dve.wait_ge(live_ready, 1)
                nc.vector.tensor_copy(row_live[:], bank[7][:, 0:S]).then_inc(consts, 1)
                nc.vector.tensor_copy(w["rows_all"][:], bank[7][0:1, S:S + 1]).then_inc(consts, 1)
                dve.wait_ge(consts, 12)
                for c in range(NCH):
                    tok = slice(c * CW, (c + 1) * CW)
                    dve.wait_ge(mean, c + 1)
                    for k in range(NK):
                        i = nc.vector.tensor_tensor(xc[:, k, :], x[:, k, tok], bank[0][:, :], ALU.subtract)
                    i.then_inc(xc_ready, 1)
                    dve.wait_ge(std_ready, c + 1)
                    step(nc.vector.reciprocal(rstd[:], std[:]))
                    for k in range(NK):
                        i = nc.vector.tensor_tensor(xn[:, k, :], xc[:, k, :], rstd[:], ALU.mult)
                    i.then_inc(xn_ready, 1)
                    dve.wait_ge(proj, c + 1)
                    for k in range(NK):
                        step(nc.vector.tensor_scalar(q[:, k, :], bank[2 + k][:, :], bq[:, k:k + 1], UP, ALU.add, ALU.mult))
                        live = row_live[:, :].unsqueeze(1).to_broadcast([P, CB, S])
                        qv = q[:, k, :].rearrange("p (b s) -> p b s", s=S)
                        step(nc.vector.tensor_tensor(qv, qv, live, ALU.mult))
                        step(nc.vector.tensor_copy(q_hi[:, k, tok], q[:, k, :]))
                        nc.vector.tensor_tensor(q_lo[:, k, tok], q[:, k, :], q_hi[:, k, tok], ALU.subtract).then_inc(q_done, 1)

            @block.scalar
            def _(act):
                act.wait_ge(consts, 2)
                for c in range(NCH):
                    act.wait_ge(xc_ready, c + 1)
                    nc.scalar.activation(sq[:], xc[:], ACT.Square).then_inc(sq_ready, 1)
                    act.wait_ge(var, c + 1)
                    nc.scalar.activation(std[:], bank[1][:, :], ACT.Sqrt, bias=eps_col[:, 0:1]).then_inc(std_ready, 1)

            @block.tensor
            def _(pe):
                pe.wait_ge(diag_ready, 1)
                pe.wait_ge(consts, 4)
                pe.wait_ge(all_ready, 1)
                nc.tensor.matmul(bank[7][:, 0:S], ones_q[:], row_diag[:], start=True, stop=True, skip_group_check=True)
                nc.tensor.matmul(bank[7][0:1, S:S + 1], row_all[:], ones_q[:, 0:1], start=False, stop=True,
                                 skip_group_check=True).then_inc(live_ready, 1)
                pe.wait_ge(x_in, 16)
                pe.wait_ge(w_in, 6 * 16)
                for c in range(NCH):
                    tok = slice(c * CW, (c + 1) * CW)
                    if c:
                        pe.wait_ge(xc_ready, c)
                    for k in range(NK):
                        i = nc.tensor.matmul(bank[0][:, :], mean_w[:], x[:, k, tok], start=k == 0, stop=k == NK - 1)
                    i.then_inc(mean, 1)
                    pe.wait_ge(sq_ready, c + 1)
                    if c:
                        pe.wait_ge(std_ready, c)
                    for k in range(NK):
                        i = nc.tensor.matmul(bank[1][:, :], mean_w[:], sq[:, k, :], start=k == 0, stop=k == NK - 1)
                    i.then_inc(var, 1)
                    pe.wait_ge(xn_ready, c + 1)
                    if c:
                        pe.wait_ge(q_done, 2 * c)
                    for m in range(NK):
                        for k in range(NK):
                            i = nc.tensor.matmul(bank[2 + m][:, :], wq[:, k, m * P:(m + 1) * P], xn[:, k, :],
                                                 start=k == 0, stop=k == NK - 1)
                    i.then_inc(proj, 1)


def cross_attention(nc, sb, ins, bank, w, ident, attn_out, q_parts, sem):
    raw = sb("ctx_raw", [P, NK, S2P], F32)
    c_hi = sb("ctx_hi", [P, NK, S2P], F32R)
    c_lo = sb("ctx_lo", [P, NK, S2P], F32R)
    k_hi = sb("k_hi", [P, NK, S2P], F16)
    k_lo = sb("k_lo", [P, NK, S2P], F16)
    kstack = [sb(f"kstack{i}", [P, PAIRS, S2P], F16) for i in range(2)]
    qstack = [sb(f"qstack{i}", [P, PAIRS, PW], F16) for i in range(2)]
    v = [sb(f"v{i}", [P, KT, D], F32) for i in range(2)]
    probs = [sb(f"probs{i}", [P, PAIRS, PW], F32) for i in range(NP)]
    acc = [sb(f"acc{i}", [P, PAIRS, PW], F32) for i in range(2)]
    junk = [sb(f"junk{i}", [P, 402], BF16) for i in range(2)]
    lead = sb("lead", [P, NMX], F32)
    part_max = sb("part_max", [P, PAIRS, KC], F32)
    row_max = sb("row_max", [P, PAIRS], F32)
    shift = sb("shift", [P, PAIRS], F32)
    rsum = sb("rsum", [P, NK, PW], F32)
    o_norm = sb("o_norm", [P, NK, PW], F32)
    o_even = sb("o_even", [P, NK, S], F32)

    pj = bank[0:2]
    st = bank[2:4]
    sm = bank[4:6]
    ob = bank[6:8]

    ctx_in = sem("ctx_in")
    ctx_hi = sem("ctx_hi")
    ctx_lo = sem("ctx_lo")
    k_proj = sem("k_proj")
    v_proj = sem("v_proj")
    khi_done = sem("khi_done")
    klo_done = sem("klo_done")
    v_done = sem("v_done")
    kstack_in = [[sem(f"kstack_in{i}{p}") for p in range(PAIRS)] for i in range(2)]
    qstack_in = [sem(f"qstack_in{i}") for i in range(2)]
    const_in = sem("stack_const_in")
    stack_zero = sem("stack_zero")
    sm_ready = sem("sm_ready")
    sm_done = sem("sm_done")
    max_found = sem("max_found")
    shift_ready = sem("shift_ready")
    shift_rows = sem("shift_rows")
    shift_done = sem("shift_done")
    st_ready = sem("st_ready")
    exp_done = sem("exp_done")
    pv_done = sem("pv_done")
    acc_done = sem("acc_done")
    sums_ready = sem("sums_ready")
    rsum_done = sem("rsum_done")
    o_read = sem("o_read")
    even_done = sem("even_done")
    out_done = sem("out_done")

    STACK_DMAS = 3
    QSTACK_DMAS = 6

    def acc_count(n, kt):
        return NACC * n + max(kt, 1)

    SLOTS = ["S0 K S1 K", "S0 K S1 K P R", "S0 N K S1 K O P", "S0 K S1 K P",
             "S0 M V M S1 M V M P M", "S0 M V M S1 M V M P M", "S0 M V M S1 M X V M P M", "S0 M V M S1 M X V M P M",
             "S0 M V S1 M V M X P M", "S0 M X V S1 M V M X P M", "S0 M V M S1 M P M X G", "S0 S1 X P", "S0 T S1 P P X"]
    slots, counts = [], {}
    for slot in SLOTS:
        slots.append([])
        for step in slot.split():
            if step in ("S0", "S1"):
                slots[-1].append(("S", int(step[1])))
            else:
                slots[-1].append((step, counts.get(step, 0)))
                counts[step] = counts.get(step, 0) + 1
    assert (counts["K"], counts["V"], counts["M"], counts["X"], counts["P"]) == (NCK, KT, NMX, SPLIT, KT)

    def turns(eng, emit):
        def turn(n):
            def or_none(m):
                return at(m) if 0 <= m < B else None
            emit(or_none(n), or_none(n + 1), or_none(n + 2), or_none(n + 3))
        for n in (-1, 0, 1):
            turn(n)
        with eng.Fori(1, (B - 4) // 2) as t:
            for u in range(2):
                emit(loop_batch(t, u), loop_batch(t, u + 1), loop_batch(t, u + 2), loop_batch(t, u + 3))
        for n in range(B - 4, B):
            turn(n)

    with nc.Block() as block:
        @block.sync
        def _(sp):
            def load(b):
                need(sp, ctx_lo, SPLIT * b.n)
                src = ins["ctxT"][b.n] if isinstance(b.n, int) else ins["ctxT"][bass.ds(b.n, 1)].rearrange("a d s -> (a d) s")
                sp.dma_start(raw[:], src.rearrange("(k p) s -> p k s", p=P)).then_inc(ctx_in, 16)

            def lay_out_queries(b):
                need(sp, st_ready, NST * (b.n - 1))
                for i, part in enumerate((0, 0, 1)):
                    for e in range(2):
                        tok = bass.ds(b.n * S, S)
                        src = q_parts[part, :, tok].rearrange("(p e d) s -> e d p s", e=2, d=DK)[e]
                        sp.dma_start(qstack[b.slot][32 * i + DK * e:32 * i + DK * (e + 1), :, S * e:S * (e + 1)],
                                     src).then_inc(qstack_in[b.slot], 16)

            def lay_out_keys(b, t):
                sp.wait_ge(klo_done, NCK * b.n + KC * (t + 1))
                for g in range(GROUPS):
                    p = GROUPS * t + g
                    for i, part in enumerate((k_hi, k_lo, k_hi)):
                        sp.dma_start(kstack[b.slot][32 * i:32 * i + 32, p, :],
                                     part[32 * g:32 * g + 32, t, :]).then_inc(kstack_in[b.slot][p], 16)

            load(at(0))
            for i in range(2):
                sp.dma_start(kstack[i][KSTACK:KROWS, :, :], ins["c_select"].rearrange("r (p s) -> r p s", s=S2P)).then_inc(const_in, 16)
            sp.wait_ge(stack_zero, 2)
            load(at(1))

            def turn(cur, nxt, split, third):
                if nxt:
                    lay_out_queries(nxt)
                    for t in range(NK):
                        lay_out_keys(nxt, t)
                if third:
                    load(third)
            turns(sp, turn)

        @block.gpsimd
        def _(pool):
            def turn(cur, nxt, split, third):
                if not cur:
                    return
                sums = acc[cur.slot]
                for kt in range(1, KT):
                    m = keys_of(kt)
                    pool.wait_ge(exp_done, NST * cur.n + 2 * kt + 2)
                    if kt == 1:
                        need(pool, sums_ready, cur.n - 1)
                        nc.gpsimd.tensor_tensor(sums[:], probs[0][:], probs[1][:], ALU.add).then_inc(acc_done, 1)
                    else:
                        pool.wait_ge(acc_done, acc_count(cur.n, kt - 1))
                        nc.gpsimd.tensor_tensor(sums[0:m], sums[0:m], probs[kt % NP][0:m], ALU.add).then_inc(acc_done, 1)
            turns(pool, turn)

        @block.scalar
        def _(act):
            def split_hi(b, i):
                k, (s0, n) = i % NK, CHUNKS[i // NK]
                if i == 0:
                    act.wait_ge(ctx_in, 16 * (b.n + 1))
                if k == 0 and not first(b):
                    act.wait_ge(v_proj, KT * (b.n - 1) + -(-min(s0 + n, S2) // P))
                nc.scalar.activation(c_hi[:, k, s0:s0 + n], raw[:, k, s0:s0 + n], ACT.Copy).then_inc(ctx_hi, 1)

            def exponentials(b, kt, h):
                m = keys_of(kt)
                if h == 0:
                    if kt >= NP:
                        act.wait_ge(pv_done, KT * b.n + kt - NP + 1)
                        act.wait_ge(acc_done, acc_count(b.n, kt - NP))
                    else:
                        old = max(x for x in range(KT) if x % NP == kt)
                        need(act, pv_done, KT * (b.n - 1) + old + 1)
                        need(act, acc_done, acc_count(b.n - 1, old))
                act.wait_ge(st_ready, NST * b.n + 2 * kt + h + 1)
                nc.scalar.activation(probs[kt % NP][0:m, GROUPS * h:GROUPS * (h + 1), :], st[h][0:m, :], ACT.Exp,
                                     scale=DK ** -0.5 / (UP * UP)).then_inc(exp_done, 1)

            def keys_hi(b, c):
                t, (s0, n) = c // KC, CHUNKS[c % KC]
                if c % KC == 0:
                    for p in range(GROUPS * t, GROUPS * (t + 1)):
                        need(act, kstack_in[1 - b.slot][p], 16 * STACK_DMAS * (b.used - 1 + b.slot))
                act.wait_ge(k_proj, NCK * b.n + c + 1)
                nc.scalar.activation(k_hi[:, t, s0:s0 + n], pj[(b.slot + c) % 2][:, 0:n], ACT.Identity,
                                     bias=w["bk"][:, t:t + 1]).then_inc(khi_done, 1)

            def values(b, i):
                m = keys_of(i)
                if i == 0:
                    need(act, pv_done, KT * (b.n - 1))
                act.wait_ge(v_proj, KT * b.n + i + 1)
                nc.scalar.activation(v[b.slot][0:m, i, :], pj[(b.slot + NCK + i) % 2][0:m, 0:D], ACT.Copy).then_inc(v_done, 1)

            for i in range(SPLIT):
                split_hi(at(0), i)

            def turn(cur, nxt, split, third):
                for kt in range(KT):
                    for what, i in slots[kt]:
                        if what == "S" and cur:
                            exponentials(cur, kt, i)
                        if what == "K" and nxt:
                            keys_hi(nxt, i)
                        if what == "V" and nxt:
                            values(nxt, i)
                        if what == "X" and split:
                            split_hi(split, i)
            turns(act, turn)

        @block.vector
        def _(dve):
            def split_lo(b, i):
                k, (s0, n) = i % NK, CHUNKS[i // NK]
                dve.wait_ge(ctx_hi, SPLIT * b.n + i + 1)
                nc.vector.tensor_tensor(c_lo[:, k, s0:s0 + n], raw[:, k, s0:s0 + n],
                                        c_hi[:, k, s0:s0 + n].bitcast(F32), ALU.subtract).then_inc(ctx_lo, 1)

            def keys_lo(b, c):
                t, (s0, n) = c // KC, CHUNKS[c % KC]
                dve.wait_ge(khi_done, NCK * b.n + c + 1)
                nc.vector.scalar_tensor_tensor(k_lo[:, t, s0:s0 + n], pj[(b.slot + c) % 2][:, 0:n], w["bk"][:, t:t + 1],
                                               k_hi[:, t, s0:s0 + n], ALU.add, ALU.subtract).then_inc(klo_done, 1)

            def chunk_max(b, i):
                p, c = i // KC, i % KC
                s0, n = MAXCH[c]
                dve.wait_ge(sm_ready, NMX * b.n + i + 1)
                nc.vector.memset(lead[:, i:i + 1], 0.0)
                nc.vector.tensor_tensor_reduce(junk[(b.slot + i) % 2][:, 0:n], sm[(b.slot + i) % 2][:, 0:n], w["mask_q"][:, s0:s0 + n],
                                               1.0, -3.0e38, ALU.add, ALU.max, part_max[:, p, c:c + 1]).then_inc(sm_done, 1)

            def maxima(b):
                dve.wait_ge(sm_done, NMX * (b.n + 1))
                nc.vector.tensor_reduce(row_max[:], part_max[:], AX.X, ALU.max).then_inc(max_found, 1)
                dve.wait_ge(max_found, b.n + 1)
                nc.vector.tensor_scalar(shift[:], row_max[:], -1.0 / SEL, None, ALU.mult).then_inc(shift_ready, 1)

            def shift_in(b):
                dve.wait_ge(shift_rows, b.n + 1)
                rows = sm[b.slot][0:PAIRS, 0:PW].unsqueeze(1).to_broadcast([PAIRS, PAIRS, PW])
                nc.vector.tensor_copy(qstack[b.slot][KSTACK:KROWS, :, :], rows).then_inc(shift_done, 1)

            def normalizers(b):
                o = ob[b.slot]
                dve.wait_ge(sums_ready, b.n + 1)
                nc.vector.reciprocal(rsum[:], o[:, NK * PW:2 * NK * PW].rearrange("p (t c) -> p t c", t=NK)).then_inc(rsum_done, 1)

            def outputs(b):
                o = ob[b.slot]
                dve.wait_ge(rsum_done, b.n + 1)
                nc.vector.tensor_tensor(o_norm[:], o[:, 0:NK * PW].rearrange("p (t c) -> p t c", t=NK), rsum[:],
                                        ALU.mult).then_inc(o_read, 1)
                dve.wait_ge(o_read, b.n + 1)
                for t in range(NK):
                    nc.vector.tensor_scalar(o_even[:, t, :], o_norm[:, t, 0:S], w["even_rows"][:, 0:1], w["bv"][:, t:t + 1],
                                            ALU.mult, ALU.add).then_inc(even_done, 1)
                dve.wait_ge(even_done, NK * (b.n + 1))
                nc.vector.scalar_tensor_tensor(attn_out[:, :, bass.ds(b.n * S, S)], o_norm[:, :, S:2 * S], w["even_rows"][:, 1:2],
                                               o_even[:], ALU.mult, ALU.add).then_inc(out_done, 1)

            for i in range(2):
                nc.vector.memset(qstack[i][:], 0.0).then_inc(stack_zero, 1)
            for i in range(SPLIT):
                split_lo(at(0), i)

            def turn(cur, nxt, split, third):
                for kt in range(KT):
                    for what, i in slots[kt]:
                        if what == "K" and nxt:
                            keys_lo(nxt, i)
                        if what == "M" and nxt:
                            chunk_max(nxt, i)
                        if what == "G" and nxt:
                            maxima(nxt)
                        if what == "T" and nxt:
                            shift_in(nxt)
                        if what == "X" and split:
                            split_lo(split, i)
                        if what == "N" and cur and not first(cur):
                            normalizers(before(cur))
                        if what == "O" and cur and not first(cur):
                            outputs(before(cur))
            turns(dve, turn)
            normalizers(at(B - 1))
            outputs(at(B - 1))

        @block.tensor
        def _(pe):
            def piece_free(b, j):
                if j < 2:
                    need(pe, v_done, KT * (b.n - 1) + KT - 1 + j)
                elif j - 2 < NCK:
                    pe.wait_ge(klo_done, NCK * b.n + j - 1)
                else:
                    pe.wait_ge(v_done, KT * b.n + j - 1 - NCK)

            def keys(b, c):
                t, (s0, n) = c // KC, CHUNKS[c % KC]
                if c < KC:
                    pe.wait_ge(ctx_lo, SPLIT * b.n + NK * (c + 1))
                piece_free(b, c)
                o = pj[(b.slot + c) % 2][:, 0:n]
                terms = [(wp, cp, k) for k in range(NK) for wp, cp in (("wk_hi", c_hi), ("wk_lo", c_hi), ("wk_hi", c_lo))]
                for i, (wp, cp, k) in enumerate(terms):
                    mm = nc.tensor.matmul(o, w[wp][:, k, t * P:(t + 1) * P], cp[:, k, s0:s0 + n],
                                          start=i == 0, stop=i == len(terms) - 1)
                mm.then_inc(k_proj, 1)

            def values(b, j):
                m = keys_of(j)
                piece_free(b, NCK + j)
                o = pj[(b.slot + NCK + j) % 2][0:m, 0:D]
                terms = [(wp, cp, k) for k in range(NK) for wp, cp in (("wv_hi", c_hi), ("wv_lo", c_hi), ("wv_hi", c_lo))]
                for i, (wp, cp, k) in enumerate(terms):
                    mm = nc.tensor.matmul(o, cp[:, k, j * P:j * P + m], w[wp][:, k, :],
                                          start=i == 0, stop=i == len(terms) - 1)
                mm.then_inc(v_proj, 1)

            def chunk_scores(b, i):
                p, (s0, n) = i // KC, MAXCH[i % KC]
                if i == 0:
                    pe.wait_ge(qstack_in[b.slot], 16 * QSTACK_DMAS * b.used)
                if i % KC == 0:
                    pe.wait_ge(kstack_in[b.slot][p], 16 * STACK_DMAS * b.used)
                if i == 1:
                    need(pe, shift_done, b.n)
                elif i == 0:
                    need(pe, sm_done, NMX * b.n)
                else:
                    pe.wait_ge(sm_done, NMX * b.n + i - 1)
                nc.tensor.matmul(sm[(b.slot + i) % 2][:, 0:n], qstack[b.slot][0:KSTACK, p, :],
                                 kstack[b.slot][0:KSTACK, p, s0:s0 + n], start=True, stop=True).then_inc(sm_ready, 1)

            def turn_shift(b):
                pe.wait_ge(shift_ready, b.n + 1)
                nc.tensor.transpose(sm[b.slot][0:PAIRS, 0:P], shift[:], ident[:]).then_inc(shift_rows, 1)

            def scores(b, kt, h, masked):
                m = keys_of(kt)
                if kt == 0 and h == 0:
                    pe.wait_ge(shift_done, b.n + 1)
                need(pe, exp_done, NST * b.n + 2 * kt + h - 1)
                if masked:
                    mask = w["mask_k"][0:m, kt, :].unsqueeze(1).to_broadcast([m, 2 * GROUPS, S])
                    nc.tensor.matmul(st[h][0:m, :], w["ident_h"][0:m, 0:m], mask, start=True, stop=True, skip_group_check=True)
                for g in range(GROUPS):
                    p = GROUPS * h + g
                    mm = nc.tensor.matmul(st[h][0:m, g * PW:(g + 1) * PW], kstack[b.slot][0:KROWS, p, kt * P:kt * P + m],
                                          qstack[b.slot][0:KROWS, p, :], start=not masked and g == 0, stop=True, skip_group_check=True)
                mm.then_inc(st_ready, 1)

            def products(b, kt):
                m = keys_of(kt)
                if kt == 0:
                    pe.wait_ge(v_done, KT * (b.n + 1))
                    need(pe, o_read, b.n - 1)
                pe.wait_ge(exp_done, NST * b.n + 2 * kt + 2)
                for t in range(NK):
                    for g in range(GROUPS):
                        p = GROUPS * t + g
                        mm = nc.tensor.matmul(ob[b.slot][32 * g:32 * g + 32, t * PW:(t + 1) * PW],
                                              v[b.slot][0:m, kt, 32 * p:32 * p + 32], probs[kt % NP][0:m, p, :],
                                              start=kt == 0 and t == 0, stop=kt == KT - 1, skip_group_check=True)
                mm.then_inc(pv_done, 1)

            def row_sums(b):
                pe.wait_ge(acc_done, NACC * (b.n + 1))
                for t in range(NK):
                    for g in range(GROUPS):
                        c0 = (NK + t) * PW
                        mm = nc.tensor.matmul(ob[b.slot][32 * g:32 * g + 32, c0:c0 + PW], w["ones"][:],
                                              acc[b.slot][:, GROUPS * t + g, :], start=False, stop=True, skip_group_check=True)
                mm.then_inc(sums_ready, 1)

            pe.wait_ge(const_in, 32)

            def run(masked):
                def turn(cur, nxt, split, third):
                    for kt in range(KT):
                        for what, i in slots[kt]:
                            if cur:
                                if what == "S":
                                    scores(cur, kt, i, masked)
                                if what == "P":
                                    products(cur, i)
                                if what == "R" and not first(cur):
                                    row_sums(before(cur))
                            if nxt:
                                if what == "K":
                                    keys(nxt, i)
                                if what == "V":
                                    values(nxt, i)
                                if what == "M":
                                    chunk_scores(nxt, i)
                                if what == "T":
                                    turn_shift(nxt)
                turns(pe, turn)
                row_sums(at(B - 1))

            rows_all = pe.value_load(w["rows_all"][0:1, 0:1], min_val=0, max_val=S)
            with pe.If(rows_all == S):
                run(masked=False)
            with pe.Else():
                run(masked=True)


def tail(nc, ctx, ins, bank, attn_out, mean_w, eps_col, out_dram, sem):
    with ExitStack() as own:
        def sb(name, shape, dt=F32):
            return own.enter_context(nc.sbuf_tensor(name, shape, dt))

        x = sb("x", [P, NK, NTOK])
        h2 = sb("h2", [P, NK, NTOK])
        wo, wval, wout = (sb(n, [P, NK, D]) for n in ("wo", "wval", "wout"))
        wspan = sb("wspan", [P, NK, 2 * H])
        bo = sb("bo", [P, NK])
        sel_a, sel_b = sb("sel_a", [33, PAIRS, P]), sb("sel_b", [48, PAIRS, P])
        head_cols, head_ones = sb("head_cols", [P, D]), sb("head_ones", [P, 32])
        sw1, sw3 = sb("sw1", [P, NK, HS]), sb("sw3", [P, NK, HS])
        sw2 = sb("sw2", [P, HS // P, D])
        w1, w2 = sb("w1", [P, E, NK, D]), sb("w2", [P, E, NK, D])
        sb1, sb3 = sb("sb1", [P, HS // P]), sb("sb3", [P, HS // P])
        sb2, b1, b2 = sb("sb2", [P, NK]), sb("b1", [P, E, NK]), sb("b2", [P, E, NK])
        class_bias = sb("class_bias", [P, E, NK])
        bias_a, bias_b = sb("bias_a", [P, NK]), sb("bias_b", [P, NK])
        xc, sq = sb("xc", [P, NK, CW]), sb("sq", [P, NK, CW])
        h = sb("h", [P, NK, CB, 2, S])
        std, rstd = sb("std", [P, CW]), sb("rstd", [P, CW])
        e0, e1, absx, ln1 = (sb(n, [H, CW]) for n in ("e0", "e1", "absx", "ln1"))
        mean, near = sb("mean", [H, CW]), sb("near", [H, CW])
        rows_a, rows_b = sb("rows_a", [33, CW]), sb("rows_b", [48, CW])
        b_copy = [sb(f"b_copy{i}", [P, CW]) for i in range(2)]
        dist = [sb(f"dist{i}", [P, CW]) for i in range(2)]
        ex = sb("ex", [P, PAIRS, CW])
        vbd = [sb(f"vbd{i}", [P, D]) for i in range(2)]
        rs, o2 = sb("rs", [P, NK, CW]), sb("o2", [P, NK, CW])
        NC = NTOK // E
        silu = [sb(f"silu{i}", [P, HS // P, NC]) for i in range(2)]
        gate = [sb(f"gate{i}", [P, HS // P, NC]) for i in range(2)]
        gelu = [sb(f"gelu{i}", [P, 2, NK, NC]) for i in range(2)]
        xb = [sb(f"xb{i}", [P, NK, NC]) for i in range(2)]

        names = ("x1_proj x1_done ln_mean ln_xc ln_sq ln_var ln_std ln_rstd ln_done span e0_done ab_done e1_done ln1_done "
                 "vec rows_done ab_ready b_copied dist_done ex_done sums val_ready vbd_done pv rs_done o2_done x2_proj x2_done "
                 "f1 f3 fe silu_done gate_done gelu_done f_out f_done xb_done").split()
        s = {n: sem("t_" + n) for n in names}
        w_in, c_in, x_in, f_in, y_out, prep = (sem("t_" + n) for n in ("w_in", "c_in", "x_in", "f_in", "y_out", "prep"))

        def toks(c):
            return slice(c * CW, (c + 1) * CW)

        def cls(tile, k, c):
            return tile[:, k, :].rearrange("p (b c n) -> p b c n", c=E, n=S // E)[:, :, c, :]

        def flat(ap):
            return ap.rearrange("p (b n) -> p b n", n=S // E)

        with nc.Block() as block:
            @block.sync
            def _(sp):
                sp.dma_start(x[:], ins["xT"].rearrange("(k p) t -> p k t", p=P)).then_inc(x_in, 16)
                for name, tile in (("woT", wo), ("wspanT", wspan), ("wvalT", wval), ("woutT", wout)):
                    sp.dma_start(tile[:], ins[name].rearrange("(k p) n -> p k n", p=P)).then_inc(w_in, 16)
                sp.dma_start(bo[:], ins["bo"]).then_inc(w_in, 16)
                for name, tile in (("c_sel_a", sel_a), ("c_sel_b", sel_b)):
                    sp.dma_start(tile[:], ins[name].rearrange("r (p m) -> r p m", m=P)).then_inc(c_in, 16)
                for name, tile in (("c_head_cols", head_cols), ("c_head_ones", head_ones)):
                    sp.dma_start(tile[:], ins[name]).then_inc(c_in, 16)
                for name, tile in (("sw1", sw1), ("sw3", sw3), ("sw2", sw2)):
                    sp.dma_start(tile[:], ins[name].rearrange("(k p) n -> p k n", p=P)).then_inc(f_in, 16)
                for name, tile in (("w1", w1), ("w2", w2)):
                    sp.dma_start(tile[:], ins[name].rearrange("e (k p) n -> p e k n", p=P)).then_inc(f_in, 16)
                for name, tile in (("sb1", sb1), ("sb3", sb3), ("sb2", sb2)):
                    sp.dma_start(tile[:], ins[name]).then_inc(f_in, 16)
                for name, tile in (("b1", b1), ("b2", b2)):
                    sp.dma_start(tile[:], ins[name].rearrange("p (e k) -> p e k", k=NK)).then_inc(f_in, 16)
                sp.wait_ge(s["f_done"], NK * E)
                sp.dma_start(out_dram.rearrange("(k p) t -> p k t", p=P), x[:]).then_inc(y_out, 16)
                sp.wait_ge(y_out, 16)

            @block.scalar
            def _(act):
                def norm(l):
                    act.wait_ge(s["ln_xc"], l + 1)
                    nc.scalar.activation(sq[:], xc[:], ACT.Square).then_inc(s["ln_sq"], 1)
                    act.wait_ge(s["ln_var"], l + 1)
                    nc.scalar.activation(std[:], bank[3][:, :], ACT.Sqrt, bias=eps_col[:, 0:1]).then_inc(s["ln_std"], 1)

                for c in range(NCH):
                    norm(2 * c)
                    act.wait_ge(s["span"], c + 1)
                    nc.scalar.activation(e0[:], bank[0][0:H, :], ACT.Exp, scale=-1.0).then_inc(s["e0_done"], 1)
                    nc.scalar.activation(absx[:], bank[1][0:H, :], ACT.Abs).then_inc(s["ab_done"], 1)
                    act.wait_ge(s["ab_done"], c + 1)
                    nc.scalar.activation(e1[:], absx[:], ACT.Exp, scale=-1.0).then_inc(s["e1_done"], 1)
                    act.wait_ge(s["e1_done"], c + 1)
                    nc.scalar.activation(ln1[:], e1[:], ACT.Ln, bias=1.0).then_inc(s["ln1_done"], 1)
                    for p in range(PAIRS + 1):
                        n = PAIRS * c + p
                        if p < PAIRS:
                            act.wait_ge(s["ab_ready"], n + 1)
                            if n >= 2:
                                act.wait_ge(s["dist_done"], n - 1)
                            nc.scalar.activation(b_copy[p % 2][:], bank[5 + 2 * (p % 2)][:, :], ACT.Copy).then_inc(s["b_copied"], 1)
                        if p:
                            act.wait_ge(s["dist_done"], n)
                            if p == 1 and c:
                                act.wait_ge(s["pv"], CB * c)
                            nc.scalar.activation(ex[:, p - 1, :], dist[(p - 1) % 2][:], ACT.Exp, scale=-1.0).then_inc(s["ex_done"], 1)
                    norm(2 * c + 1)
                for c in range(E):
                    act.wait_ge(s["f1"], c + 1)
                    if c >= 2:
                        act.wait_ge(s["gate_done"], c - 1)
                    for m in range(HS // P):
                        i = nc.scalar.activation(silu[c % 2][:, m, :], bank[m // 2][:, (m % 2) * NC:(m % 2 + 1) * NC], ACT.Silu,
                                                 bias=sb1[:, m:m + 1])
                    i.then_inc(s["silu_done"], 1)
                    act.wait_ge(s["fe"], c + 1)
                    if c >= 2:
                        act.wait_ge(s["f_out"], c - 1)
                    for k in range(2):
                        for m in range(NK):
                            e = CLASS_EXPERTS[c][k]
                            i = nc.scalar.activation(gelu[c % 2][:, k, m, :], bank[4 + k][:, m * NC:(m + 1) * NC], ACT.Gelu,
                                                     bias=b1[:, e, m:m + 1])
                    i.then_inc(s["gelu_done"], 1)

            @block.vector
            def _(dve):
                steps = [0]

                def step(instruction):
                    instruction.then_inc(s["vec"], 1)
                    steps[0] += 1
                    dve.wait_ge(s["vec"], steps[0])

                def norm(l, src, dst):
                    dve.wait_ge(s["ln_mean"], l + 1)
                    for k in range(NK):
                        i = nc.vector.tensor_tensor(xc[:, k, :], src[k], bank[2][:, :], ALU.subtract)
                    i.then_inc(s["ln_xc"], 1)
                    dve.wait_ge(s["ln_std"], l + 1)
                    step(nc.vector.reciprocal(rstd[:], std[:]))
                    for k in range(NK):
                        i = nc.vector.tensor_tensor(dst[k], like(dst[k], xc[:, k, :]), like(dst[k], rstd[:]), ALU.mult)
                    i.then_inc(s["ln_done"], 1)

                def like(dst, src):
                    if len(dst.shape) == 2:
                        return src
                    return src.rearrange("p (b s) -> p b s", s=S).unsqueeze(2).to_broadcast([P, CB, 2, S])

                step(nc.vector.memset(rows_a[:], 0.0))
                step(nc.vector.memset(rows_b[:], 0.0))
                nc.vector.memset(rows_a[32:33, :], 1.0).then_inc(s["vec"], 1)
                steps[0] += 1
                dve.wait_ge(x_in, 16)
                dve.wait_ge(w_in, 5 * 16)
                dve.wait_ge(c_in, 4 * 16)
                for c in range(NCH):
                    dve.wait_ge(s["x1_proj"], c + 1)
                    for k in range(NK):
                        nc.vector.scalar_tensor_tensor(x[:, k, toks(c)], bank[k][:, :], bo[:, k:k + 1], x[:, k, toks(c)],
                                                       ALU.add, ALU.add).then_inc(s["x1_done"], 1)
                    dve.wait_ge(s["x1_done"], NK * (c + 1))
                    norm(2 * c, [x[:, k, toks(c)] for k in range(NK)], [h[:, k] for k in range(NK)])
                    dve.wait_ge(s["e0_done"], c + 1)
                    step(nc.vector.tensor_scalar(mean[:], e0[:], 1.0, None, ALU.add))
                    step(nc.vector.reciprocal(near[:], mean[:]))
                    step(nc.vector.tensor_scalar(mean[:], near[:], float(S), None, ALU.mult))
                    step(nc.vector.tensor_scalar(near[:], mean[:], ROUND, None, ALU.add))
                    step(nc.vector.tensor_scalar(rows_a[0:H, :], near[:], -ROUND, float(S - 1), ALU.add, ALU.min))
                    dve.wait_ge(s["ln1_done"], c + 1)
                    step(nc.vector.scalar_tensor_tensor(rows_b[0:H, :], bank[1][0:H, :], 0.0, ln1[:], ALU.max, ALU.add))
                    step(nc.vector.scalar_tensor_tensor(near[:], mean[:], -2.0, rows_a[0:H, :], ALU.mult, ALU.add))
                    nc.vector.tensor_tensor(rows_b[32:32 + H, :], near[:], rows_b[0:H, :], ALU.mult).then_inc(s["rows_done"], 1)
                    for p in range(PAIRS):
                        n = PAIRS * c + p
                        dve.wait_ge(s["b_copied"], n + 1)
                        if n >= 2:
                            dve.wait_ge(s["ex_done"], n - 1)
                        nc.vector.tensor_tensor(dist[p % 2][:], bank[4 + 2 * (p % 2)][:, :], b_copy[p % 2][:],
                                                ALU.mult).then_inc(s["dist_done"], 1)
                    for b in range(CB):
                        n = CB * c + b
                        dve.wait_ge(s["val_ready"], n + 1)
                        if n >= 2:
                            dve.wait_ge(s["pv"], n - 1)
                        nc.vector.tensor_tensor(vbd[b % 2][:], bank[2 + b % 2][:, 0:D], head_cols[:], ALU.mult).then_inc(s["vbd_done"], 1)
                    dve.wait_ge(s["sums"], c + 1)
                    for k in range(NK):
                        step(nc.vector.reciprocal(rs[:, k, :], bank[6 + k][:, :]))
                    dve.wait_ge(s["pv"], CB * (c + 1))
                    for k in range(NK):
                        i = nc.vector.tensor_tensor(o2[:, k, :], bank[4 + k][:, :], rs[:, k, :], ALU.mult)
                    i.then_inc(s["o2_done"], 1)
                    dve.wait_ge(s["x2_proj"], c + 1)
                    for k in range(NK):
                        nc.vector.tensor_tensor(x[:, k, toks(c)], bank[k][:, :], x[:, k, toks(c)], ALU.add).then_inc(s["x2_done"], 1)
                    dve.wait_ge(s["x2_done"], NK * (c + 1))
                    norm(2 * c + 1, [x[:, k, toks(c)] for k in range(NK)], [h2[:, k, toks(c)] for k in range(NK)])
                dve.wait_ge(f_in, 10 * 16)
                step(nc.vector.tensor_scalar(bias_a[:], sb2[:], 0.5, None, ALU.mult))
                for c in range(E):
                    ea, eb = CLASS_EXPERTS[c]
                    step(nc.vector.tensor_tensor(bias_b[:], b2[:, ea, :], b2[:, eb, :], ALU.add))
                    step(nc.vector.scalar_tensor_tensor(class_bias[:, c, :], bias_b[:], 0.25, bias_a[:], ALU.mult, ALU.add))
                nc.vector.tensor_scalar(sw2[:], sw2[:], 2.0, None, ALU.mult).then_inc(prep, 1)

                def gates(c):
                    dve.wait_ge(s["f3"], c + 1)
                    dve.wait_ge(s["silu_done"], c + 1)
                    if c >= 2:
                        dve.wait_ge(s["f_out"], c - 1)
                    for m in range(HS // P):
                        i = nc.vector.scalar_tensor_tensor(gate[c % 2][:, m, :], bank[2 + m // 2][:, (m % 2) * NC:(m % 2 + 1) * NC],
                                                           sb3[:, m:m + 1], silu[c % 2][:, m, :], ALU.add, ALU.mult)
                    i.then_inc(s["gate_done"], 1)

                gates(0)
                for c in range(E):
                    for k in range(NK):
                        i = nc.vector.tensor_scalar(flat(xb[c % 2][:, k, :]), cls(x, k, c), class_bias[:, c, k:k + 1], None, ALU.add)
                        i.then_inc(s["xb_done"], 1)
                    if c + 1 < E:
                        gates(c + 1)
                    dve.wait_ge(s["f_out"], c + 1)
                    dve.wait_ge(s["xb_done"], NK * (c + 1))
                    for k in range(NK):
                        nc.vector.scalar_tensor_tensor(cls(x, k, c), flat(bank[6][:, k * NC:(k + 1) * NC]), 0.25, flat(xb[c % 2][:, k, :]),
                                                       ALU.mult, ALU.add).then_inc(s["f_done"], 1)

            @block.tensor
            def _(pe):
                def norm(l, src):
                    for k in range(NK):
                        i = nc.tensor.matmul(bank[2][:, :], mean_w[:], src[k], start=k == 0, stop=k == NK - 1)
                    i.then_inc(s["ln_mean"], 1)
                    pe.wait_ge(s["ln_sq"], l + 1)
                    for k in range(NK):
                        i = nc.tensor.matmul(bank[3][:, :], mean_w[:], sq[:, k, :], start=k == 0, stop=k == NK - 1)
                    i.then_inc(s["ln_var"], 1)

                def project(wt, src, done):
                    for m in range(NK):
                        for k in range(NK):
                            i = nc.tensor.matmul(bank[m][:, :], wt[:, k, m * P:(m + 1) * P], src[k], start=k == 0, stop=k == NK - 1)
                    i.then_inc(done, 1)

                pe.wait_ge(w_in, 5 * 16)
                pe.wait_ge(c_in, 4 * 16)
                for c in range(NCH):
                    if c:
                        pe.wait_ge(s["x2_done"], NK * c)
                    project(wo, [attn_out[:, k, toks(c)] for k in range(NK)], s["x1_proj"])
                    if c:
                        pe.wait_ge(s["ln_done"], 2 * c)
                    pe.wait_ge(s["x1_done"], NK * (c + 1))
                    norm(2 * c, [x[:, k, toks(c)] for k in range(NK)])
                    pe.wait_ge(s["ln_done"], 2 * c + 1)
                    for j in range(2):
                        for k in range(NK):
                            i = nc.tensor.matmul(bank[j][0:H, :].rearrange("p (b s) -> p b s", s=S), wspan[:, k, j * H:(j + 1) * H],
                                                 h[:, k, :, 0, :], start=k == 0, stop=k == NK - 1)
                    i.then_inc(s["span"], 1)
                    pe.wait_ge(s["rows_done"], c + 1)
                    if c:
                        pe.wait_ge(s["o2_done"], c)
                    for p in range(PAIRS):
                        n = PAIRS * c + p
                        if n >= 2:
                            pe.wait_ge(s["dist_done"], n - 1)
                        nc.tensor.matmul(bank[4 + 2 * (p % 2)][:, :], sel_a[:, p, :], rows_a[:], start=True, stop=True)
                        nc.tensor.matmul(bank[5 + 2 * (p % 2)][:, :], sel_b[:, p, :], rows_b[:], start=True,
                                         stop=True).then_inc(s["ab_ready"], 1)
                    pe.wait_ge(s["ex_done"], PAIRS * (c + 1))
                    for p in range(PAIRS):
                        t, g = p // GROUPS, p % GROUPS
                        i = nc.tensor.matmul(bank[6 + t][32 * g:32 * g + 32, :], head_ones[:], ex[:, p, :], start=True, stop=True)
                    i.then_inc(s["sums"], 1)

                    def value(b):
                        n = CB * c + b
                        if b >= 2:
                            pe.wait_ge(s["vbd_done"], n - 1)
                        for k in range(NK):
                            two = h[:, k, b].rearrange("p e s -> p (e s)")
                            i = nc.tensor.matmul(bank[2 + b % 2][:, 0:D], two, wval[:, k, :], start=k == 0, stop=k == NK - 1)
                        i.then_inc(s["val_ready"], 1)

                    value(0)
                    for b in range(CB):
                        if b + 1 < CB:
                            value(b + 1)
                        pe.wait_ge(s["vbd_done"], CB * c + b + 1)
                        for p in range(PAIRS):
                            t, g = p // GROUPS, p % GROUPS
                            i = nc.tensor.matmul(bank[4 + t][32 * g:32 * g + 32, b * S:(b + 1) * S], vbd[b % 2][:, 32 * p:32 * p + 32],
                                                 ex[:, p, b * S:(b + 1) * S], start=True, stop=True, skip_group_check=True)
                        i.then_inc(s["pv"], 1)
                    pe.wait_ge(s["o2_done"], c + 1)
                    project(wout, [o2[:, k, :] for k in range(NK)], s["x2_proj"])
                    pe.wait_ge(s["x2_done"], NK * (c + 1))
                    norm(2 * c + 1, [x[:, k, toks(c)] for k in range(NK)])
                pe.wait_ge(s["ln_done"], 2 * NCH)
                pe.wait_ge(f_in, 10 * 16)
                pe.wait_ge(prep, 1)

                def hidden(c, wt, banks, done, free, count):
                    if c:
                        pe.wait_ge(free, count)
                    for m in range(HS // P):
                        for k in range(NK):
                            i = nc.tensor.matmul(flat(bank[banks + m // 2][:, (m % 2) * NC:(m % 2 + 1) * NC]), wt[:, k, m * P:(m + 1) * P],
                                                 cls(h2, k, c), start=k == 0, stop=k == NK - 1)
                    i.then_inc(done, 1)

                def experts(c):
                    if c:
                        pe.wait_ge(s["gelu_done"], c)
                    for j, e in enumerate(CLASS_EXPERTS[c]):
                        for m in range(NK):
                            for k in range(NK):
                                i = nc.tensor.matmul(flat(bank[4 + j][:, m * NC:(m + 1) * NC]), w1[:, e, k, m * P:(m + 1) * P],
                                                     cls(h2, k, c), start=k == 0, stop=k == NK - 1)
                    i.then_inc(s["fe"], 1)

                def output(c):
                    pe.wait_ge(s["gate_done"], c + 1)
                    pe.wait_ge(s["gelu_done"], c + 1)
                    if c:
                        pe.wait_ge(s["f_done"], NK * c)
                    for m in range(NK):
                        terms = [(sw2[:, k, m * P:(m + 1) * P], gate[c % 2][:, k, :]) for k in range(HS // P)]
                        terms += [(w2[:, e, k, m * P:(m + 1) * P], gelu[c % 2][:, j, k, :])
                                  for j, e in enumerate(CLASS_EXPERTS[c]) for k in range(NK)]
                        for n, (lhs, rhs) in enumerate(terms):
                            i = nc.tensor.matmul(bank[6][:, m * NC:(m + 1) * NC], lhs, rhs, start=n == 0, stop=n == len(terms) - 1)
                    i.then_inc(s["f_out"], 1)

                for c in range(E + 1):
                    if c < E:
                        hidden(c, sw1, 0, s["f1"], s["silu_done"], c)
                        hidden(c, sw3, 2, s["f3"], s["gate_done"], c)
                        experts(c)
                    if c:
                        output(c - 1)


def constants():
    rows = np.arange(P)
    position = np.arange(S) % (S // E) * E + np.arange(S) // (S // E)
    even = np.stack([rows % 32 < DK, rows % 32 >= DK], 1).astype(np.float32)
    select = np.zeros((PAIRS, PAIRS, S2P), np.float16)
    sel_a = np.zeros((33, PAIRS, P), np.float32)
    sel_b = np.zeros((48, PAIRS, P), np.float32)
    for p in range(PAIRS):
        select[p, p] = SEL
        for e in range(2):
            part = slice(S * e, S * e + S)
            sel_a[2 * p + e, p, part] = -1.0
            sel_a[32, p, part] = position
            sel_b[2 * p + e, p, part] = position
            sel_b[32 + 2 * p + e, p, part] = 1.0
    half = rows[:, None] // S
    return {
        "c_ident": np.eye(P, dtype=np.float32),
        "c_even": even,
        "c_select": select.reshape(PAIRS, -1),
        "c_sel_a": sel_a.reshape(33, -1),
        "c_sel_b": sel_b.reshape(48, -1),
        "c_head_cols": (half == np.arange(D)[None] // DK % 2).astype(np.float32),
        "c_head_ones": (half == np.arange(32)[None] // DK).astype(np.float32),
    }


def kernel(**inputs):
    import concourse.bacc as bacc
    from concourse.bass_utils import run_bass_kernel_spmd

    a = {n: np.asarray(v) for n, v in inputs.items()}
    order = np.arange(S).reshape(S // E, E).T.reshape(-1)

    def cols(vec):
        return vec.reshape(-1, P).T

    span = a["L0_attn_W_span"]
    mask = a["mask_1x1xSxS2_bf1"][0, 0][order].view(np.uint8)
    maskT = np.ones((KT * P, S), np.uint8)
    maskT[:S2] = mask.T
    ctxT = np.zeros((B, D, S2P), np.float32)
    ctxT[:, :, :S2] = a["ctx_1024"].transpose(0, 2, 1)
    arrays = {
        "xT": a["x"][:, order].reshape(NTOK, D).T,
        "ctxT": ctxT,
        "maskQ": mask,
        "maskT": maskT,
        "wqT": a["L0_xattn_wq_w"].T, "wkT": a["L0_xattn_wk_w"].T, "wvT": a["L0_xattn_wv_w"].T, "woT": a["L0_xattn_wo_w"].T,
        "bq": cols(a["L0_xattn_wq_b"]), "bk": cols(a["L0_xattn_wk_b"]), "bv": cols(a["L0_xattn_wv_b"]), "bo": cols(a["L0_xattn_wo_b"]),
        "wspanT": np.concatenate([span[0::2], span[1::2]]).T,
        "wvalT": a["L0_attn_W_val"].T, "woutT": a["L0_attn_W_out"].T,
        "sw1": a["L0_ffn_sw1"], "sw3": a["L0_ffn_sw3"], "sw2": a["L0_ffn_sw2"],
        "sb1": cols(a["L0_ffn_sb1"]), "sb3": cols(a["L0_ffn_sb3"]), "sb2": cols(a["L0_ffn_sb2"]),
        "w1": a["L0_ffn_w1"], "w2": a["L0_ffn_w2"],
        "b1": cols(a["L0_ffn_b1"].reshape(-1)), "b2": cols(a["L0_ffn_b2"].reshape(-1)),
        **constants(),
    }
    arrays = {n: np.ascontiguousarray(v) for n, v in arrays.items()}

    nc = bacc.Bacc("TRN2", target_bir_lowering=False, num_devices=1)
    ins = {n: nc.dram_tensor(f"in_{n}", v.shape, mybir.dt.from_np(v.dtype), kind="ExternalInput").ap() for n, v in arrays.items()}
    out = nc.dram_tensor("out_yT", (D, NTOK), F32, kind="ExternalOutput").ap()
    build(nc, ins, out)
    r = run_bass_kernel_spmd(nc, [{f"in_{n}": v for n, v in arrays.items()}], core_ids=[0])
    yT = r.results[0]["out_yT"]
    return np.ascontiguousarray(yT.reshape(D, B, E, S // E).transpose(1, 3, 2, 0).reshape(B, S, D))
```

```python
from contextlib import ExitStack

import numpy as np

import concourse.bass as bass
from concourse import mybir

F32 = mybir.dt.float32
F32R = mybir.dt.float32r
BF16 = mybir.dt.bfloat16
F16 = mybir.dt.float16
U8 = mybir.dt.uint8
ALU = mybir.AluOpType
ACT = mybir.ActivationFunctionType
AX = mybir.AxisListType

P = 128
B, S, S2, D = 32, 64, 1601, 256
H = 16
DK = D // H
NTOK = B * S
NK = D // P
PAIRS = H // 2
GROUPS = 4
PW = 2 * S
KT = -(-S2 // P)
S2P = S2 + 1
KC = 4
CHUNKS = [(0, 400), (400, 400), (800, 400), (1200, 402)]
MAXCH = [(0, 400), (400, 400), (800, 400), (1200, 401)]
NCK = NK * KC
NMX = PAIRS * KC
NST = 2 * KT
NACC = KT - 1
NP = 5
SPLIT = NK * KC
UP = 32.0
SEL = 1024.0
MASKED = -float(2 ** 25)
KSTACK = 3 * 32
KROWS = KSTACK + PAIRS
EPS = 1e-5
HS = 512
E = 8
PRIME, HASH = 11, 7919
NCH = 4
CW = NTOK // NCH
CB = CW // S
SOFT_ROW = 32
SPAN_ROWS = SOFT_ROW + H
B_ROWS = 3 * 32 + H
FOLD_CHUNK = 0
ROUND = 1.5 * 2.0 ** 23

CLASS_EXPERTS = [[(c * PRIME + k * HASH) % E for k in range(2)] for c in range(E)]


def keys_of(kt):
    return min(P, S2 - kt * P)


class Batch:

    def __init__(self, n, slot, used):
        self.n, self.slot, self.used = n, slot, used


def at(n):
    return Batch(n, n % 2, n // 2 + 1)


def loop_batch(t, offset):
    return Batch(2 * t + offset, offset % 2, t + offset // 2 + 1)


def first(b):
    return isinstance(b.n, int) and b.n == 0


def last(b):
    return isinstance(b.n, int) and b.n == B - 1


def before(b):
    return Batch(b.n - 1, 1 - b.slot, None)


def need(eng, sem, value):
    if not isinstance(value, int) or value > 0:
        eng.wait_ge(sem, value)


def build(nc, ins, out_dram):
    ctx = ExitStack()
    with ctx:
        def sem(name):
            return ctx.enter_context(nc.semaphore(name))

        bank = [ctx.enter_context(nc.psum_tensor(f"bank{i}", [P, 512], F32)) for i in range(8)]
        attn_out = ctx.enter_context(nc.sbuf_tensor("attn_out", [P, NK, NTOK], F32))
        ident = ctx.enter_context(nc.sbuf_tensor("ident", [P, P], F32))
        mean_w = ctx.enter_context(nc.sbuf_tensor("mean_w", [P, P], F32))
        wo = ctx.enter_context(nc.sbuf_tensor("wo", [P, NK, D], F32))
        bo = ctx.enter_context(nc.sbuf_tensor("bo", [P, NK], F32))
        wo_in = sem("wo_in")
        eps_col = ctx.enter_context(nc.sbuf_tensor("eps_col", [P, 1], F32))
        q_parts = nc.dram_tensor("q_parts", (2, D, NTOK), F16).ap()
        with ExitStack() as attention:
            def sb(name, shape, dt):
                return attention.enter_context(nc.sbuf_tensor(name, shape, dt))
            w = dict(
                wk_hi=sb("wk_hi", [P, NK, D], F32R), wk_lo=sb("wk_lo", [P, NK, D], F32R),
                wv_hi=sb("wv_hi", [P, NK, D], F32R), wv_lo=sb("wv_lo", [P, NK, D], F32R),
                bk=sb("bk", [P, NK], F32), bv=sb("bv", [P, NK], F32),
                even_rows=sb("even_rows", [P, 2], F32),
                mask_q=sb("mask_q", [P, S2], BF16), mask_k=sb("mask_k", [P, KT, S], BF16),
                rows_all=sb("rows_all", [1, 1], mybir.dt.int32),
                ident_h=sb("ident_h", [P, P], BF16), ones=sb("ones", [P, 32], F32),
            )
            first_in = dict(
                raw=sb("ctx_raw", [P, NK, S2P], F32), c_hi=sb("ctx_hi", [P, NK, S2P], F32R), c_lo=sb("ctx_lo", [P, NK, S2P], F32R),
                kstack=[sb(f"kstack{i}", [P, PAIRS, S2P], F16) for i in range(2)],
                qstack=[sb(f"qstack{i}", [P, PAIRS, PW], F16) for i in range(2)],
                q_hi=[sb(f"q_hi{i}", [P, NK, CW], F16) for i in range(2)],
                q_lo=[sb(f"q_lo{i}", [P, NK, CW], F16) for i in range(2)],
                ctx_in=sem("ctx_in"),
                ctx_hi=sem("ctx_hi"),
                ctx_lo=sem("ctx_lo"),
                rows_in=sem("select_rows_in"), stack_zero=sem("stack_zero"),
            )
            before, ready = queries(nc, ins, bank, w, first_in, wo, bo, wo_in, ident, mean_w, eps_col, q_parts, sem)
            cross = cross_attention(nc, sb, ins, bank, w, first_in, ident, attn_out, q_parts, sem)

            def both(eng, name):
                before[name](eng)
                for done, count in ready:
                    eng.wait_ge(done, count)
                cross[name](eng)

            with nc.Block() as block:
                @block.sync
                def _(sp):
                    both(sp, "sync")

                @block.vector
                def _(dve):
                    both(dve, "vector")

                @block.gpsimd
                def _(pool):
                    both(pool, "gpsimd")

                @block.scalar
                def _(act):
                    both(act, "scalar")

                @block.tensor
                def _(pe):
                    both(pe, "tensor")
        tail(nc, ins, bank, attn_out, wo, bo, wo_in, mean_w, eps_col, out_dram, sem)


def run_periods(order, table):
    depth = max(late for late, _, _ in table.values())
    for period in range(NCH + depth):
        count = {}
        for step in order.split():
            late, do, arg = table[step]
            i = count.get(step, 0)
            count[step] = i + 1
            if 0 <= period - late < NCH:
                do(period - late, i if arg is None else arg)


def queries(nc, ins, bank, w, first_in, wo, bo, wo_in, ident, mean_w, eps_col, q_parts, sem):
    with ExitStack() as own:
        def sb(name, shape, dt=F32):
            return own.enter_context(nc.sbuf_tensor(name, shape, dt))

        x = sb("x0", [P, NK, NTOK])
        wq, wk, wv = (sb(n, [P, NK, D]) for n in ("wq", "wk", "wv"))
        bq, bk_raw, bq_up = sb("bq", [P, NK]), sb("bk_raw", [P, NK]), sb("bq_up", [P, NK])
        mask_u8 = sb("mask_u8", [P, S2], U8)
        maskT_u8 = sb("maskT_u8", [P, KT, S], U8)
        row_ok, row_all = sb("row_ok", [S, 1]), sb("row_all", [S, 1])
        row_diag = sb("row_diag", [S, S])
        row_live = sb("row_live", [P, S])
        ones_q = sb("ones_q", [S, P])
        xc = [sb(f"xc{i}", [P, NK, CW]) for i in range(2)]
        sq = [sb(f"sq{i}", [P, NK, CW]) for i in range(2)]
        rstd = [sb(f"rstd{i}", [P, CW]) for i in range(2)]
        xn = [sb(f"xn{i}", [P, NK, CW]) for i in range(2)]
        q = [sb(f"q{i}", [P, NK, CW]) for i in range(2)]
        q_hi, q_lo = first_in["q_hi"], first_in["q_lo"]
        mean_bank, var_bank, proj_bank, row_bank = bank[0:2], bank[2:4], bank[4:6], bank[6]

        x_in = [sem(f"q_x_in{c}") for c in range(NCH)]
        const_in, wq_in, w_in, mask_in = (sem("q_" + n) for n in ("const_in", "wq_in", "w_in", "mask_in"))
        memsets, up_done, parts_hi, consts, rows_seen, diag_ready, live_ready, live_done = (
            sem("q_" + n) for n in ("memsets", "up_done", "parts_hi", "consts", "rows_seen", "diag_ready", "live_ready", "live_done"))
        mean, xc_done, sq_done, var, lnv, rstd_done, xn_done, proj, biased, live, hi_done, lo_done = (
            sem("q_" + n) for n in "mean xc sq var lnv rstd xn proj biased live hi lo".split())
        q_out = [sem(f"q_out{i}") for i in range(2)]
        raw, c_hi, c_lo = first_in["raw"], first_in["c_hi"], first_in["c_lo"]

        PE_ORDER, DVE_ORDER, ACT_ORDER = "M V P", "C L N G X", "S H I B X"

        def toks(c):
            return slice(c * CW, (c + 1) * CW)

        def sync(sp):
            def load(tile, src, done):
                sp.dma_start(tile, src).then_inc(done, 16)

            def rows(name):
                return ins[name].rearrange("(k p) n -> p k n", p=P)

            load(x[:, :, toks(0)], rows("xT")[:, :, toks(0)], x_in[0])
            load(wq[:], rows("wqT"), wq_in)
            load(bq[:], ins["bq"], wq_in)
            load(x[:, :, toks(1)], rows("xT")[:, :, toks(1)], x_in[1])
            load(ident[:], ins["c_ident"], const_in)
            load(w["even_rows"][:], ins["c_even"], const_in)
            for e in range(2):
                load(mask_u8[S * e:S * e + S, :], ins["maskQ"], mask_in)
            load(maskT_u8[:], ins["maskT"].rearrange("(n p) q -> p n q", p=P), mask_in)
            for c in range(2, NCH):
                load(x[:, :, toks(c)], rows("xT")[:, :, toks(c)], x_in[c])
            load(wk[:], rows("wkT"), w_in)
            load(wv[:], rows("wvT"), w_in)
            load(bk_raw[:], ins["bk"], w_in)
            load(w["bv"][:], ins["bv"], w_in)
            load(raw[:], ins["ctxT"][0].rearrange("(k p) s -> p k s", p=P), first_in["ctx_in"])
            for i in range(2):
                load(first_in["kstack"][i][KSTACK:KROWS, :, :], ins["c_select"].rearrange("r (p s) -> r p s", s=S2P), first_in["rows_in"])
            load(wo[:], rows("woT"), wo_in)
            load(bo[:], ins["bo"], wo_in)
            for c in range(NCH):
                sp.wait_ge(lo_done, c + 1)
                for i, part in enumerate((q_hi, q_lo)):
                    sp.dma_start(q_parts[i].rearrange("(k p) t -> p k t", p=P)[:, :, toks(c)], part[c % 2][:]).then_inc(q_out[c % 2], 16)
            for i in range(2):
                sp.wait_ge(q_out[i], 2 * 16 * (NCH // 2))

        def vector(dve):
            def centre(c, _):
                dve.wait_ge(x_in[c], 16)
                dve.wait_ge(mean, c + 1)
                need(dve, xn_done, c - 1)
                for k in range(NK):
                    i = nc.vector.tensor_tensor(xc[c % 2][:, k, :], x[:, k, toks(c)], mean_bank[c % 2][:, :], ALU.subtract)
                i.then_inc(xc_done, 1)

            def normalize(c, _):
                dve.wait_ge(rstd_done, c + 1)
                dve.wait_ge(xc_done, c + 1)
                need(dve, proj, c - 1)
                for k in range(NK):
                    i = nc.vector.tensor_tensor(xn[c % 2][:, k, :], xc[c % 2][:, k, :], rstd[c % 2][:], ALU.mult)
                i.then_inc(xn_done, 1)
                if c == 0:
                    mask_rows()
                if c == 1:
                    dve.wait_ge(live_ready, 1)
                    nc.vector.tensor_copy(row_live[:], row_bank[:, 0:S]).then_inc(live_done, 1)
                    nc.vector.tensor_copy(w["rows_all"][:], row_bank[0:1, S:S + 1]).then_inc(live_done, 1)
                    dve.wait_ge(live_done, 2)

            def clear(c, _):
                dve.wait_ge(biased, c + 1)
                for k in range(NK):
                    qv = q[c % 2][:, k, :].rearrange("p (b s) -> p b s", s=S)
                    i = nc.vector.tensor_tensor(qv, qv, row_live[:, :].unsqueeze(1).to_broadcast([P, CB, S]), ALU.mult)
                i.then_inc(live, 1)

            def low(c, _):
                dve.wait_ge(hi_done, c + 1)
                need(dve, q_out[c % 2], 2 * 16 * (c // 2))
                nc.vector.tensor_tensor(q_lo[c % 2][:], q[c % 2][:], q_hi[c % 2][:], ALU.subtract).then_inc(lo_done, 1)

            def split_lo(c, _):
                s0, n = CHUNKS[c]
                if c == 0:
                    weights_lo()
                for k in range(NK):
                    dve.wait_ge(first_in["ctx_hi"], NK * c + k + 1)
                    nc.vector.tensor_tensor(c_lo[:, k, s0:s0 + n], raw[:, k, s0:s0 + n], c_hi[:, k, s0:s0 + n].bitcast(F32),
                                            ALU.subtract).then_inc(first_in["ctx_lo"], 1)

            def weights_lo():
                dve.wait_ge(w_in, 4 * 16)
                dve.wait_ge(parts_hi, 2)
                nc.vector.scalar_tensor_tensor(w["wk_lo"][:], wk[:], UP, w["wk_hi"][:].bitcast(F32),
                                               ALU.mult, ALU.subtract).then_inc(consts, 1)
                nc.vector.tensor_tensor(w["wv_lo"][:], wv[:], w["wv_hi"][:].bitcast(F32), ALU.subtract).then_inc(consts, 1)
                nc.vector.tensor_scalar(w["bk"][:], bk_raw[:], UP, None, ALU.mult).then_inc(consts, 1)

            def mask_rows():
                dve.wait_ge(const_in, 2 * 16)
                dve.wait_ge(mask_in, 3 * 16)
                nc.vector.tensor_reduce(row_all[:], mask_u8[0:S, :], AX.X, ALU.min).then_inc(rows_seen, 1)
                nc.vector.tensor_reduce(row_ok[:], mask_u8[0:S, :], AX.X, ALU.max).then_inc(rows_seen, 1)
                dve.wait_ge(rows_seen, 2)
                nc.vector.tensor_scalar(row_diag[:], ident[0:S, 0:S], row_ok[:, 0:1], None, ALU.mult).then_inc(diag_ready, 1)

            nc.vector.memset(mean_w[:], 1.0 / D).then_inc(memsets, 1)
            nc.vector.memset(eps_col[:], EPS).then_inc(memsets, 1)
            nc.vector.memset(ones_q[:], 1.0).then_inc(memsets, 1)
            nc.vector.memset(w["ones"][:], 1.0).then_inc(consts, 1)
            for i in range(2):
                nc.vector.memset(first_in["qstack"][i][:], 0.0).then_inc(first_in["stack_zero"], 1)
            dve.wait_ge(wq_in, 2 * 16)
            nc.vector.tensor_scalar(bq_up[:], bq[:], UP, None, ALU.mult).then_inc(up_done, 1)
            run_periods(DVE_ORDER, {"C": (0, centre, None), "N": (1, normalize, None), "G": (2, clear, None), "L": (3, low, None),
                                    "X": (2, split_lo, None)})

        def gpsimd(pool):
            pool.wait_ge(mask_in, 3 * 16)
            nc.gpsimd.tensor_scalar(w["mask_q"][:], mask_u8[:], -1.0, -MASKED, ALU.add, ALU.mult).then_inc(consts, 1)
            nc.gpsimd.tensor_scalar(w["mask_k"][:], maskT_u8[:], -1.0, -MASKED, ALU.add, ALU.mult).then_inc(consts, 1)
            pool.wait_ge(const_in, 2 * 16)
            nc.gpsimd.tensor_copy(w["ident_h"][:], ident[:]).then_inc(consts, 1)

        def scalar(act):
            def square(c, _):
                act.wait_ge(xc_done, c + 1)
                need(act, var, c - 1)
                nc.scalar.activation(sq[c % 2][:], xc[c % 2][:], ACT.Square).then_inc(sq_done, 1)

            def inverse(c, _):
                act.wait_ge(var, c + 1)
                need(act, xn_done, c - 1)
                nc.scalar.activation(rstd[c % 2][:], var_bank[c % 2][:, :], ACT.Ln, bias=eps_col[:, 0:1]).then_inc(lnv, 1)
                act.wait_ge(lnv, c + 1)
                nc.scalar.activation(rstd[c % 2][:], rstd[c % 2][:], ACT.Exp, scale=-0.5).then_inc(rstd_done, 1)

            def bias(c, _):
                act.wait_ge(proj, c + 1)
                need(act, lo_done, c - 1)
                for m in range(NK):
                    i = nc.scalar.activation(q[c % 2][:, m, :], proj_bank[m][:, :], ACT.Identity, bias=bq_up[:, m:m + 1], scale=UP)
                i.then_inc(biased, 1)

            def high(c, _):
                act.wait_ge(live, c + 1)
                need(act, q_out[c % 2], 2 * 16 * (c // 2))
                nc.scalar.activation(q_hi[c % 2][:], q[c % 2][:], ACT.Copy).then_inc(hi_done, 1)

            def split_hi(c, _):
                s0, n = CHUNKS[c]
                if c == 0:
                    act.wait_ge(w_in, 4 * 16)
                    nc.scalar.activation(w["wk_hi"][:], wk[:], ACT.Copy, scale=UP).then_inc(parts_hi, 1)
                    nc.scalar.activation(w["wv_hi"][:], wv[:], ACT.Copy).then_inc(parts_hi, 1)
                    act.wait_ge(first_in["ctx_in"], 16)
                for k in range(NK):
                    nc.scalar.activation(c_hi[:, k, s0:s0 + n], raw[:, k, s0:s0 + n], ACT.Copy).then_inc(first_in["ctx_hi"], 1)

            nc.scalar.preload_act_table_set("natural_log_exp_and_others")
            act.wait_ge(memsets, 2)
            act.wait_ge(up_done, 1)
            run_periods(ACT_ORDER, {"S": (0, square, None), "I": (1, inverse, None), "B": (2, bias, None), "H": (3, high, None),
                                    "X": (2, split_hi, None)})

        def tensor(pe):
            def means(c, _):
                pe.wait_ge(x_in[c], 16)
                need(pe, xc_done, c - 1)
                for k in range(NK):
                    i = nc.tensor.matmul(mean_bank[c % 2][:, :], mean_w[:], x[:, k, toks(c)], start=k == 0, stop=k == NK - 1)
                i.then_inc(mean, 1)

            def variances(c, _):
                pe.wait_ge(sq_done, c + 1)
                need(pe, lnv, c - 1)
                for k in range(NK):
                    i = nc.tensor.matmul(var_bank[c % 2][:, :], mean_w[:], sq[c % 2][:, k, :], start=k == 0, stop=k == NK - 1)
                i.then_inc(var, 1)
                if c == 1:
                    pe.wait_ge(diag_ready, 1)
                    nc.tensor.matmul(row_bank[:, 0:S], ones_q[:], row_diag[:], start=True, stop=True, skip_group_check=True)
                    nc.tensor.matmul(row_bank[0:1, S:S + 1], row_all[:], ones_q[:, 0:1], start=False, stop=True,
                                     skip_group_check=True).then_inc(live_ready, 1)

            def project(c, _):
                pe.wait_ge(xn_done, c + 1)
                need(pe, biased, c)
                for m in range(NK):
                    for k in range(NK):
                        i = nc.tensor.matmul(proj_bank[m][:, :], wq[:, k, m * P:(m + 1) * P], xn[c % 2][:, k, :],
                                             start=k == 0, stop=k == NK - 1)
                i.then_inc(proj, 1)

            pe.wait_ge(memsets, 3)
            pe.wait_ge(wq_in, 2 * 16)
            run_periods(PE_ORDER, {"M": (0, means, None), "V": (1, variances, None), "P": (2, project, None)})

        ready = [(consts, 7), (parts_hi, 2), (live_done, 2), (const_in, 2 * 16), (w_in, 4 * 16)]
        return {"sync": sync, "vector": vector, "gpsimd": gpsimd, "scalar": scalar, "tensor": tensor}, ready


def cross_attention(nc, sb, ins, bank, w, first_in, ident, attn_out, q_parts, sem):
    raw, c_hi, c_lo, kstack, qstack = (first_in[n] for n in ("raw", "c_hi", "c_lo", "kstack", "qstack"))
    ctx_in, ctx_hi, ctx_lo = (first_in[n] for n in ("ctx_in", "ctx_hi", "ctx_lo"))
    k_hi = sb("k_hi", [P, NK, S2P], F16)
    k_lo = sb("k_lo", [P, NK, S2P], F16)
    v = [sb(f"v{i}", [P, KT, D], F32) for i in range(2)]
    probs = [sb(f"probs{i}", [P, PAIRS, PW], F32) for i in range(NP)]
    acc = [sb(f"acc{i}", [P, PAIRS, PW], F32) for i in range(2)]
    junk = [sb(f"junk{i}", [P, 402], BF16) for i in range(2)]
    lead = sb("lead", [P, NMX], F32)
    part_max = sb("part_max", [P, PAIRS, KC], F32)
    row_max = sb("row_max", [P, PAIRS], F32)
    shift = sb("shift", [P, PAIRS], F32)
    rsum = sb("rsum", [P, NK, PW], F32)
    o_norm = sb("o_norm", [P, NK, PW], F32)
    o_even = sb("o_even", [P, NK, S], F32)

    pj = bank[0:2]
    st = bank[2:4]
    sm = bank[4:6]
    ob = bank[6:8]

    k_proj = sem("k_proj")
    v_proj = sem("v_proj")
    khi_done = sem("khi_done")
    klo_done = sem("klo_done")
    v_done = sem("v_done")
    kstack_in = [[sem(f"kstack_in{i}{p}") for p in range(PAIRS)] for i in range(2)]
    qstack_in = [sem(f"qstack_in{i}") for i in range(2)]
    sm_ready = sem("sm_ready")
    sm_done = sem("sm_done")
    max_found = sem("max_found")
    shift_ready = sem("shift_ready")
    shift_rows = sem("shift_rows")
    shift_done = sem("shift_done")
    st_ready = sem("st_ready")
    exp_done = sem("exp_done")
    pv_done = sem("pv_done")
    acc_done = sem("acc_done")
    sums_ready = sem("sums_ready")
    rsum_done = sem("rsum_done")
    o_read = sem("o_read")
    even_done = sem("even_done")
    out_done = sem("out_done")

    STACK_DMAS = 3
    QSTACK_DMAS = 6

    def acc_count(n, kt):
        return NACC * n + max(kt, 1)

    SLOTS = ["K S0 L S1 K", "S0 K S1 K P R", "S0 N K S1 K O P", "S0 K S1 K P",
             "S0 M V M S1 M V M P M", "S0 M V M S1 M V M P M", "S0 H M V M S1 M X V M P M", "S0 H M V M S1 M X V M P M",
             "S0 H M V S1 M V M X P M", "S0 H M X V S1 M V H M X P M", "S0 H M V M S1 M P M G X", "S0 S1 H X P T",
             "S0 S1 P H X"]
    slots, counts = [], {}
    for slot in SLOTS:
        slots.append([])
        for step in slot.split():
            if step in ("S0", "S1"):
                slots[-1].append(("S", int(step[1])))
            else:
                slots[-1].append((step, counts.get(step, 0)))
                counts[step] = counts.get(step, 0) + 1
    assert (counts["K"], counts["V"], counts["M"], counts["H"], counts["X"], counts["P"]) == (NCK, KT, NMX, SPLIT, SPLIT, KT - 1)

    def turns(eng, emit):
        def turn(n):
            def or_none(m):
                return at(m) if 0 <= m < B else None
            emit(or_none(n), or_none(n + 1), or_none(n + 2), or_none(n + 3))
        for n in (-1, 0, 1):
            turn(n)
        with eng.Fori(1, (B - 4) // 2) as t:
            for u in range(2):
                emit(loop_batch(t, u), loop_batch(t, u + 1), loop_batch(t, u + 2), loop_batch(t, u + 3))
        for n in range(B - 4, B):
            turn(n)

    def sync(sp):
        def load(b):
            need(sp, ctx_lo, SPLIT * b.n)
            src = ins["ctxT"][b.n] if isinstance(b.n, int) else ins["ctxT"][bass.ds(b.n, 1)].rearrange("a d s -> (a d) s")
            sp.dma_start(raw[:], src.rearrange("(k p) s -> p k s", p=P)).then_inc(ctx_in, 16)

        def lay_out_queries(b):
            need(sp, st_ready, NST * (b.n - 1))
            for i, part in enumerate((0, 0, 1)):
                for e in range(2):
                    tok = bass.ds(b.n * S, S)
                    src = q_parts[part, :, tok].rearrange("(p e d) s -> e d p s", e=2, d=DK)[e]
                    sp.dma_start(qstack[b.slot][32 * i + DK * e:32 * i + DK * (e + 1), :, S * e:S * (e + 1)],
                                 src).then_inc(qstack_in[b.slot], 16)

        def lay_out_keys(b, t):
            sp.wait_ge(klo_done, NCK * b.n + KC * (t + 1))
            for g in range(GROUPS):
                p = GROUPS * t + g
                for i, part in enumerate((k_hi, k_lo, k_hi)):
                    sp.dma_start(kstack[b.slot][32 * i:32 * i + 32, p, :],
                                 part[32 * g:32 * g + 32, t, :]).then_inc(kstack_in[b.slot][p], 16)

        sp.wait_ge(first_in["stack_zero"], 2)
        load(at(1))

        def turn(cur, nxt, split, third):
            if nxt:
                lay_out_queries(nxt)
                for t in range(NK):
                    lay_out_keys(nxt, t)
            if third:
                load(third)
        turns(sp, turn)

    def add_rows(eng, ops, b, kt):
        sums, m = acc[b.slot], keys_of(kt)
        eng.wait_ge(exp_done, NST * b.n + 2 * kt + 2)
        need(eng, acc_done, NACC * b.n + kt - 1)
        if kt == 1:
            need(eng, sums_ready, b.n - 1)
            ops.tensor_tensor(sums[:], probs[0][:], probs[1][:], ALU.add).then_inc(acc_done, 1)
        else:
            ops.tensor_tensor(sums[0:m], sums[0:m], probs[kt % NP][0:m], ALU.add).then_inc(acc_done, 1)

    def gpsimd(pool):
        def turn(cur, nxt, split, third):
            if cur and not last(cur):
                for kt in range(1, KT):
                    add_rows(pool, nc.gpsimd, cur, kt)
        turns(pool, turn)

    def scalar(act):
        def split_hi(b, i):
            k, (s0, n) = i % NK, CHUNKS[i // NK]
            if i == 0:
                act.wait_ge(ctx_in, 16 * (b.n + 1))
            if k == 0 and not first(b):
                act.wait_ge(v_proj, KT * (b.n - 1) + -(-min(s0 + n, S2) // P))
            nc.scalar.activation(c_hi[:, k, s0:s0 + n], raw[:, k, s0:s0 + n], ACT.Copy).then_inc(ctx_hi, 1)

        def exponentials(b, kt, h):
            m = keys_of(kt)
            if h == 0:
                if kt >= NP:
                    act.wait_ge(pv_done, KT * b.n + kt - NP + 1)
                    act.wait_ge(acc_done, acc_count(b.n, kt - NP))
                else:
                    old = max(x for x in range(KT) if x % NP == kt)
                    need(act, pv_done, KT * (b.n - 1) + old + 1)
                    need(act, acc_done, acc_count(b.n - 1, old))
            act.wait_ge(st_ready, NST * b.n + 2 * kt + h + 1)
            nc.scalar.activation(probs[kt % NP][0:m, GROUPS * h:GROUPS * (h + 1), :], st[h][0:m, :], ACT.Exp,
                                 scale=DK ** -0.5 / (UP * UP)).then_inc(exp_done, 1)

        def keys_hi(b, c):
            t, (s0, n) = c // KC, CHUNKS[c % KC]
            if c % KC == 0:
                for p in range(GROUPS * t, GROUPS * (t + 1)):
                    need(act, kstack_in[1 - b.slot][p], 16 * STACK_DMAS * (b.used - 1 + b.slot))
            act.wait_ge(k_proj, NCK * b.n + c + 1)
            nc.scalar.activation(k_hi[:, t, s0:s0 + n], pj[(b.slot + c) % 2][:, 0:n], ACT.Identity,
                                 bias=w["bk"][:, t:t + 1]).then_inc(khi_done, 1)

        def values(b, i):
            m = keys_of(i)
            if i == 0:
                need(act, pv_done, KT * (b.n - 1))
            act.wait_ge(v_proj, KT * b.n + i + 1)
            nc.scalar.activation(v[b.slot][0:m, i, :], pj[(b.slot + NCK + i) % 2][0:m, 0:D], ACT.Copy).then_inc(v_done, 1)

        def turn(cur, nxt, split, third):
            for kt in range(KT):
                for what, i in slots[kt]:
                    if what == "S" and cur:
                        exponentials(cur, kt, i)
                    if what == "K" and nxt:
                        keys_hi(nxt, i)
                    if what == "V" and nxt:
                        values(nxt, i)
                    if what == "H" and split:
                        split_hi(split, i)
        turns(act, turn)

    def vector(dve):
        def split_lo(b, i):
            k, (s0, n) = i % NK, CHUNKS[i // NK]
            dve.wait_ge(ctx_hi, SPLIT * b.n + i + 1)
            nc.vector.tensor_tensor(c_lo[:, k, s0:s0 + n], raw[:, k, s0:s0 + n],
                                    c_hi[:, k, s0:s0 + n].bitcast(F32), ALU.subtract).then_inc(ctx_lo, 1)

        def keys_lo(b, c):
            t, (s0, n) = c // KC, CHUNKS[c % KC]
            dve.wait_ge(khi_done, NCK * b.n + c + 1)
            nc.vector.scalar_tensor_tensor(k_lo[:, t, s0:s0 + n], pj[(b.slot + c) % 2][:, 0:n], w["bk"][:, t:t + 1],
                                           k_hi[:, t, s0:s0 + n], ALU.add, ALU.subtract).then_inc(klo_done, 1)

        def chunk_max(b, i):
            p, c = i // KC, i % KC
            s0, n = MAXCH[c]
            dve.wait_ge(sm_ready, NMX * b.n + i + 1)
            nc.vector.memset(lead[:, i:i + 1], 0.0)
            nc.vector.tensor_tensor_reduce(junk[(b.slot + i) % 2][:, 0:n], sm[(b.slot + i) % 2][:, 0:n], w["mask_q"][:, s0:s0 + n],
                                           1.0, -3.0e38, ALU.add, ALU.max, part_max[:, p, c:c + 1]).then_inc(sm_done, 1)

        def maxima(b):
            dve.wait_ge(sm_done, NMX * (b.n + 1))
            nc.vector.tensor_reduce(row_max[:], part_max[:], AX.X, ALU.max).then_inc(max_found, 1)
            dve.wait_ge(max_found, b.n + 1)
            nc.vector.tensor_scalar(shift[:], row_max[:], -1.0 / SEL, None, ALU.mult).then_inc(shift_ready, 1)

        def shift_in(b):
            dve.wait_ge(shift_rows, b.n + 1)
            rows = sm[b.slot][0:PAIRS, 0:PW].unsqueeze(1).to_broadcast([PAIRS, PAIRS, PW])
            nc.vector.tensor_copy(qstack[b.slot][KSTACK:KROWS, :, :], rows).then_inc(shift_done, 1)

        def normalizers(b):
            o = ob[b.slot]
            dve.wait_ge(sums_ready, b.n + 1)
            nc.vector.reciprocal(rsum[:], o[:, NK * PW:2 * NK * PW].rearrange("p (t c) -> p t c", t=NK)).then_inc(rsum_done, 1)

        def outputs(b):
            o = ob[b.slot]
            dve.wait_ge(rsum_done, b.n + 1)
            nc.vector.tensor_tensor(o_norm[:], o[:, 0:NK * PW].rearrange("p (t c) -> p t c", t=NK), rsum[:],
                                    ALU.mult).then_inc(o_read, 1)
            dve.wait_ge(o_read, b.n + 1)
            for t in range(NK):
                nc.vector.tensor_scalar(o_even[:, t, :], o_norm[:, t, 0:S], w["even_rows"][:, 0:1], w["bv"][:, t:t + 1],
                                        ALU.mult, ALU.add).then_inc(even_done, 1)
            dve.wait_ge(even_done, NK * (b.n + 1))
            nc.vector.scalar_tensor_tensor(attn_out[:, :, bass.ds(b.n * S, S)], o_norm[:, :, S:2 * S], w["even_rows"][:, 1:2],
                                           o_even[:], ALU.mult, ALU.add).then_inc(out_done, 1)

        def turn(cur, nxt, split, third):
            for kt in range(KT):
                for what, i in slots[kt]:
                    if what == "K" and nxt:
                        keys_lo(nxt, i)
                    if what == "M" and nxt:
                        chunk_max(nxt, i)
                    if what == "G" and nxt:
                        maxima(nxt)
                    if what == "T" and nxt:
                        shift_in(nxt)
                    if what == "X" and split:
                        split_lo(split, i)
                    if what == "N" and cur and not first(cur):
                        normalizers(before(cur))
                    if what == "O" and cur and not first(cur):
                        outputs(before(cur))
                    if what == "S" and i == 1 and cur and last(cur) and kt:
                        add_rows(dve, nc.vector, cur, kt)
        turns(dve, turn)
        normalizers(at(B - 1))
        outputs(at(B - 1))

    def tensor(pe):
        def piece_free(b, j):
            if j < 2:
                need(pe, v_done, KT * (b.n - 1) + KT - 1 + j)
            elif j - 2 < NCK:
                pe.wait_ge(klo_done, NCK * b.n + j - 1)
            else:
                pe.wait_ge(v_done, KT * b.n + j - 1 - NCK)

        def keys(b, c):
            t, (s0, n) = c // KC, CHUNKS[c % KC]
            if c < KC:
                pe.wait_ge(ctx_lo, SPLIT * b.n + NK * (c + 1))
            piece_free(b, c)
            o = pj[(b.slot + c) % 2][:, 0:n]
            terms = [(wp, cp, k) for k in range(NK) for wp, cp in (("wk_hi", c_hi), ("wk_lo", c_hi), ("wk_hi", c_lo))]
            for i, (wp, cp, k) in enumerate(terms):
                mm = nc.tensor.matmul(o, w[wp][:, k, t * P:(t + 1) * P], cp[:, k, s0:s0 + n],
                                      start=i == 0, stop=i == len(terms) - 1)
            mm.then_inc(k_proj, 1)

        def values(b, j):
            m = keys_of(j)
            piece_free(b, NCK + j)
            o = pj[(b.slot + NCK + j) % 2][0:m, 0:D]
            terms = [(wp, cp, k) for k in range(NK) for wp, cp in (("wv_hi", c_hi), ("wv_lo", c_hi), ("wv_hi", c_lo))]
            for i, (wp, cp, k) in enumerate(terms):
                mm = nc.tensor.matmul(o, cp[:, k, j * P:j * P + m], w[wp][:, k, :],
                                      start=i == 0, stop=i == len(terms) - 1)
            mm.then_inc(v_proj, 1)

        def chunk_scores(b, i):
            p, (s0, n) = i // KC, MAXCH[i % KC]
            if i == 0:
                pe.wait_ge(qstack_in[b.slot], 16 * QSTACK_DMAS * b.used)
            if i % KC == 0:
                pe.wait_ge(kstack_in[b.slot][p], 16 * STACK_DMAS * b.used)
            if i == 1:
                need(pe, shift_done, b.n)
            elif i == 0:
                need(pe, sm_done, NMX * b.n)
            else:
                pe.wait_ge(sm_done, NMX * b.n + i - 1)
            nc.tensor.matmul(sm[(b.slot + i) % 2][:, 0:n], qstack[b.slot][0:KSTACK, p, :],
                             kstack[b.slot][0:KSTACK, p, s0:s0 + n], start=True, stop=True).then_inc(sm_ready, 1)

        def turn_shift(b):
            pe.wait_ge(shift_ready, b.n + 1)
            nc.tensor.transpose(sm[b.slot][0:PAIRS, 0:P], shift[:], ident[:]).then_inc(shift_rows, 1)

        def scores(b, kt, h, masked):
            m = keys_of(kt)
            if kt == 0 and h == 0:
                pe.wait_ge(shift_done, b.n + 1)
            need(pe, exp_done, NST * b.n + 2 * kt + h - 1)
            if masked:
                mask = w["mask_k"][0:m, kt, :].unsqueeze(1).to_broadcast([m, 2 * GROUPS, S])
                nc.tensor.matmul(st[h][0:m, :], w["ident_h"][0:m, 0:m], mask, start=True, stop=True, skip_group_check=True)
            for g in range(GROUPS):
                p = GROUPS * h + g
                mm = nc.tensor.matmul(st[h][0:m, g * PW:(g + 1) * PW], kstack[b.slot][0:KROWS, p, kt * P:kt * P + m],
                                      qstack[b.slot][0:KROWS, p, :], start=not masked and g == 0, stop=True, skip_group_check=True)
            mm.then_inc(st_ready, 1)

        def products(b, kt):
            m = keys_of(kt)
            if kt == 0:
                pe.wait_ge(v_done, KT * (b.n + 1))
                need(pe, o_read, b.n - 1)
            pe.wait_ge(exp_done, NST * b.n + 2 * kt + 2)
            for t in range(NK):
                for g in range(GROUPS):
                    p = GROUPS * t + g
                    mm = nc.tensor.matmul(ob[b.slot][32 * g:32 * g + 32, t * PW:(t + 1) * PW],
                                          v[b.slot][0:m, kt, 32 * p:32 * p + 32], probs[kt % NP][0:m, p, :],
                                          start=kt == 0 and t == 0, stop=kt == KT - 1, skip_group_check=True)
            mm.then_inc(pv_done, 1)

        def row_sums(b):
            pe.wait_ge(acc_done, NACC * (b.n + 1))
            for t in range(NK):
                for g in range(GROUPS):
                    c0 = (NK + t) * PW
                    mm = nc.tensor.matmul(ob[b.slot][32 * g:32 * g + 32, c0:c0 + PW], w["ones"][:],
                                          acc[b.slot][:, GROUPS * t + g, :], start=False, stop=True, skip_group_check=True)
            mm.then_inc(sums_ready, 1)

        pe.wait_ge(first_in["rows_in"], 2 * 16)

        def run(masked):
            def turn(cur, nxt, split, third):
                for kt in range(KT):
                    for what, i in slots[kt]:
                        if cur:
                            if what == "S":
                                scores(cur, kt, i, masked)
                            if what == "P":
                                products(cur, i)
                            if what == "L" and not first(cur):
                                products(before(cur), KT - 1)
                            if what == "R" and not first(cur):
                                row_sums(before(cur))
                        if nxt:
                            if what == "K":
                                keys(nxt, i)
                            if what == "V":
                                values(nxt, i)
                            if what == "M":
                                chunk_scores(nxt, i)
                            if what == "T":
                                turn_shift(nxt)
            turns(pe, turn)
            products(at(B - 1), KT - 1)
            row_sums(at(B - 1))

        rows_all = pe.value_load(w["rows_all"][0:1, 0:1], min_val=0, max_val=S)
        with pe.If(rows_all == S):
            run(masked=False)
        with pe.Else():
            run(masked=True)

    return {"sync": sync, "vector": vector, "gpsimd": gpsimd, "scalar": scalar, "tensor": tensor}


def tail(nc, ins, bank, attn_out, wo, bo, wo_in, mean_w, eps_col, out_dram, sem):
    with ExitStack() as own:
        def sb(name, shape, dt=F32):
            return own.enter_context(nc.sbuf_tensor(name, shape, dt))

        x = sb("x", [P, NK, NTOK])
        h2 = sb("h2", [P, NK, NTOK])
        wval, wout = (sb(n, [P, NK, D]) for n in ("wval", "wout"))
        wspan = sb("wspan", [P, NK, SPAN_ROWS])
        sel_a, sel_b = sb("sel_a", [33, PAIRS, P], F32R), sb("sel_b", [B_ROWS, PAIRS, P], F32R)
        head_ones = sb("head_ones", [P, 32])
        sw1, sw3 = sb("sw1", [P, NK, HS]), sb("sw3", [P, NK, HS])
        sw2 = sb("sw2", [P, HS // P, D])
        w1, w2 = sb("w1", [P, E, NK, D]), sb("w2", [P, E, NK, D])
        sb1, sb3 = sb("sb1", [P, HS // P]), sb("sb3", [P, HS // P])
        sb2, b1, b2 = sb("sb2", [P, NK]), sb("b1", [P, E, NK]), sb("b2", [P, E, NK])
        class_bias = sb("class_bias", [P, E, NK])
        bias_a, bias_b = sb("bias_a", [P, NK]), sb("bias_b", [P, NK])
        x_in = [sem(f"t_x_in{c}") for c in range(NCH)]
        w_in, sel_in, f_in, y_out, prep = (sem("t_" + n) for n in ("w_in", "sel_in", "f_in", "y_out", "prep"))
        h2_done, f_done = sem("t_h2_done"), sem("t_f_done")

        def toks(c):
            return slice(c * CW, (c + 1) * CW)

        with nc.Block() as block:
            @block.sync
            def _(sp):
                def load(tile, src, done):
                    sp.dma_start(tile, src).then_inc(done, 16)

                def rows(name):
                    return ins[name].rearrange("(k p) n -> p k n", p=P)

                load(x[:, :, toks(0)], rows("xT")[:, :, toks(0)], x_in[0])
                for name, tile in (("wspanT", wspan), ("wvalT", wval), ("woutT", wout)):
                    load(tile[:], rows(name), w_in)
                load(head_ones[:], ins["c_head_ones"], w_in)
                for c in range(1, NCH):
                    load(x[:, :, toks(c)], rows("xT")[:, :, toks(c)], x_in[c])
                for name, tile in (("sw1", sw1), ("sw3", sw3), ("sw2", sw2)):
                    load(tile[:], rows(name), f_in)
                for name, tile in (("w1", w1), ("w2", w2)):
                    load(tile[:], ins[name].rearrange("e (k p) n -> p e k n", p=P), f_in)
                for name, tile in (("sb1", sb1), ("sb3", sb3), ("sb2", sb2)):
                    load(tile[:], ins[name], f_in)
                for name, tile in (("b1", b1), ("b2", b2)):
                    load(tile[:], ins[name].rearrange("p (e k) -> p e k", k=NK), f_in)
                sp.wait_ge(f_done, NK * E)
                sp.dma_start(out_dram.rearrange("(k p) t -> p k t", p=P), x[:]).then_inc(y_out, 16)
                sp.wait_ge(y_out, 16)

            @block.gpsimd
            def _(pool):
                for name, tile in (("c_sel_a", sel_a), ("c_sel_b", sel_b)):
                    pool.dma_start(tile[:], ins[name].rearrange("r (p m) -> r p m", m=P)).then_inc(sel_in, 16)

            with ExitStack() as span:
                spans = span_attention(nc, span, bank, sem, mean_w, eps_col, attn_out, x, h2, wo, bo, wspan, wval, wout,
                                       sel_a, sel_b, head_ones, x_in, wo_in, w_in, sel_in, h2_done)
            mlps = expert_mlps(nc, own, bank, sem, x, h2, sw1, sw2, sw3, w1, w2, sb1, sb3, b1, class_bias, prep, f_in, h2_done, f_done)

            @block.scalar
            def _(act):
                nc.scalar.preload_act_table_set("natural_log_exp_and_others")
                spans["scalar"](act)
                mlps["scalar"](act)

            @block.vector
            def _(dve):
                def fold():
                    bias_steps = sem("t_bias_steps")
                    done = [0]

                    def step(instruction):
                        instruction.then_inc(bias_steps, 1)
                        done[0] += 1
                        dve.wait_ge(bias_steps, done[0])
                    dve.wait_ge(f_in, 10 * 16)
                    step(nc.vector.tensor_scalar(bias_a[:], sb2[:], 0.5, None, ALU.mult))
                    for c in range(E):
                        ea, eb = CLASS_EXPERTS[c]
                        step(nc.vector.tensor_tensor(bias_b[:], b2[:, ea, :], b2[:, eb, :], ALU.add))
                        step(nc.vector.scalar_tensor_tensor(class_bias[:, c, :], bias_b[:], 0.25, bias_a[:], ALU.mult, ALU.add))
                    nc.vector.tensor_scalar(sw2[:], sw2[:], 2.0, None, ALU.mult).then_inc(prep, 1)
                spans["vector"](dve, fold)
                mlps["vector"](dve)

            @block.tensor
            def _(pe):
                spans["tensor"](pe)
                mlps["tensor"](pe)


def span_attention(nc, own, bank, sem, mean_w, eps_col, attn_out, x, h2, wo, bo, wspan, wval, wout,
                   sel_a, sel_b, head_ones, x_in, wo_in, w_in, sel_in, h2_done):
    def sb(name, shape, dt=F32):
        return own.enter_context(nc.sbuf_tensor(name, shape, dt))

    UNITS = PAIRS
    QUADS = CB // 2
    xc = [sb(f"t_xc{i}", [P, NK, CW]) for i in range(2)]
    sq = [sb(f"t_sq{i}", [P, NK, CW]) for i in range(2)]
    rstd = [sb(f"t_rstd{i}", [P, CW]) for i in range(2)]
    h = [sb(f"t_h{i}", [P, NK, CW]) for i in range(2)]
    e0, lnx, near = sb("e0", [H, CW]), sb("lnx", [SPAN_ROWS, CW]), sb("near", [H, CW])
    soft, gap = sb("soft", [H, CW]), sb("gap", [H, CW])
    rows_a = [sb(f"rows_a{i}", [33, CW], F32R) for i in range(2)]
    rows_b = [sb(f"rows_b{i}", [B_ROWS, CW], F32R) for i in range(2)]
    b_copy = [sb(f"b_copy{i}", [P, CW]) for i in range(2)]
    dist = [sb(f"dist{i}", [P, CW]) for i in range(2)]
    ex = sb("ex", [P, PAIRS, CW])
    vbd = sb("vbd", [P, CB, D])
    rs, o2 = sb("rs", [P, NK, CW]), sb("o2", [P, NK, CW])

    proj, ln_bank, ab, vb = bank[0:2], bank[2:4], bank[4:6], bank[6:8]
    factors = [ab, vb]
    names = ("x1_proj x1_done x2_proj x2_done span e0_done lnx_abs lnx_exp lnx_done vec rows_zero vbd_zero rows_done ab_ready b_copied "
             "dist_done ex_done sums lns_done rs_done val_ready vbd_done pv o2_done h_done").split()
    s = {n: sem("t_" + n) for n in names}
    s["h2_done"] = h2_done
    mean, xc_done, sq_done, var, lnv, rstd_done = ([sem(f"t_{n}{i}") for i in range(2)]
                                                   for n in ("mean", "xc", "sq", "var", "lnv", "rstd"))
    norm_done = [s["h_done"], h2_done]
    src_done = [s["x1_done"], s["x2_done"]]

    PE_ORDER = "W Z M0 A M1 A V0 A V1 A A A S A A X X X X U O"
    DVE_ORDER = "W Z C0 A C1 A A N0 A A A N1 A A R O"
    ACT_ORDER = "A Q0 A Q1 A I0 A A A I1 A A S E X X X X U"

    NOW, NEXT, LAST = 0, 1, 2

    def norm_steps(table, letter, do):
        table[letter + "0"], table[letter + "1"] = (NOW, do, 0), (LAST, do, 1)
        return table

    def scalar(act):
        def square(c, j):
            act.wait_ge(xc_done[j], c + 1)
            need(act, var[j], c)
            nc.scalar.activation(sq[j][:], xc[j][:], ACT.Square).then_inc(sq_done[j], 1)

        def inverse(c, j):
            act.wait_ge(var[j], c + 1)
            need(act, norm_done[j], c)
            nc.scalar.activation(rstd[j][:], ln_bank[j][:, :], ACT.Ln, bias=eps_col[:, 0:1]).then_inc(lnv[j], 1)
            act.wait_ge(lnv[j], c + 1)
            nc.scalar.activation(rstd[j][:], rstd[j][:], ACT.Exp, scale=-0.5).then_inc(rstd_done[j], 1)

        def spans(c, _):
            act.wait_ge(s["span"], c + 1)
            need(act, s["rows_done"], c)
            nc.scalar.activation(e0[:], ln_bank[0][0:H, :], ACT.Exp, scale=-1.0).then_inc(s["e0_done"], 1)
            x_rows = lnx[SOFT_ROW:SOFT_ROW + H, :]
            nc.scalar.activation(x_rows, ln_bank[0][SOFT_ROW:SOFT_ROW + H, :], ACT.Abs).then_inc(s["lnx_abs"], 1)
            act.wait_ge(s["lnx_abs"], c + 1)
            nc.scalar.activation(x_rows, x_rows, ACT.Exp, scale=-1.0).then_inc(s["lnx_exp"], 1)
            act.wait_ge(s["lnx_exp"], c + 1)
            nc.scalar.activation(x_rows, x_rows, ACT.Ln, bias=1.0).then_inc(s["lnx_done"], 1)

        def exponential(c, i):
            n = UNITS * c + i
            act.wait_ge(s["dist_done"], n + 1)
            if i == 0:
                need(act, s["pv"], c)
            nc.scalar.activation(ex[:, i, :], dist[i % 2][:], ACT.Exp, scale=-1.0).then_inc(s["ex_done"], 1)

        def unit(c, i):
            n = UNITS * c + i
            act.wait_ge(s["ab_ready"], n + 1)
            need(act, s["dist_done"], n - 1)
            nc.scalar.activation(b_copy[i % 2][:], factors[i % 2][1][:, :], ACT.Copy).then_inc(s["b_copied"], 1)
            if i:
                exponential(c, i - 1)

        def values(c, q):
            act.wait_ge(s["val_ready"], QUADS * c + q + 1)
            if q == 0:
                act.wait_ge(s["vbd_zero"], 1)
                need(act, s["pv"], c)
            for r in range(2):
                for e in range(2):
                    i = nc.scalar.activation(heads(vbd[S * e:S * (e + 1), 2 * q + r, :], e),
                                             heads(vb[q % 2][S * r:S * (r + 1), 0:D], e), ACT.Copy)
            i.then_inc(s["vbd_done"], 1)

        def sums(c, _):
            act.wait_ge(s["sums"], c + 1)
            need(act, s["o2_done"], c)
            for t in range(NK):
                i = nc.scalar.activation(rs[:, t, :], ab[t][:, :], ACT.Ln)
            i.then_inc(s["lns_done"], 1)
            act.wait_ge(s["lns_done"], c + 1)
            nc.scalar.activation(rs[:], rs[:], ACT.Exp, scale=-1.0).then_inc(s["rs_done"], 1)

        table = {"S": (NOW, spans, None), "A": (NEXT, unit, None), "E": (NEXT, exponential, UNITS - 1), "X": (NEXT, values, None),
                 "U": (NEXT, sums, None)}
        run_periods(ACT_ORDER, norm_steps(norm_steps(table, "Q", square), "I", inverse))

    def heads(ap, e):
        return ap.rearrange("p (q e d) -> p q e d", e=2, d=DK)[:, :, e, :]

    def vector(dve, between):
        steps = [0]

        def step(instruction):
            instruction.then_inc(s["vec"], 1)
            steps[0] += 1
            dve.wait_ge(s["vec"], steps[0])

        def residual(c, j):
            if j == 0:
                if c == 0:
                    dve.wait_ge(wo_in, 2 * 16)
                dve.wait_ge(x_in[c], 16)
                dve.wait_ge(s["x1_proj"], c + 1)
                for k in range(NK):
                    nc.vector.scalar_tensor_tensor(x[:, k, toks(c)], proj[k][:, :], bo[:, k:k + 1], x[:, k, toks(c)],
                                                   ALU.add, ALU.add).then_inc(s["x1_done"], 1)
            else:
                dve.wait_ge(s["x2_proj"], c + 1)
                for k in range(NK):
                    nc.vector.tensor_tensor(x[:, k, toks(c)], ab[k][:, :], x[:, k, toks(c)], ALU.add).then_inc(s["x2_done"], 1)

        def centre(c, j):
            dve.wait_ge(mean[j], c + 1)
            dve.wait_ge(src_done[j], NK * (c + 1))
            need(dve, norm_done[j], c)
            for k in range(NK):
                i = nc.vector.tensor_tensor(xc[j][:, k, :], x[:, k, toks(c)], ln_bank[j][:, :], ALU.subtract)
            i.then_inc(xc_done[j], 1)

        def normalize(c, j):
            dve.wait_ge(rstd_done[j], c + 1)
            dve.wait_ge(xc_done[j], c + 1)
            if j == 0:
                need(dve, s["val_ready"], QUADS * (c - 1))
            for k in range(NK):
                dst = h[c % 2][:, k, :] if j == 0 else h2[:, k, toks(c)]
                i = nc.vector.tensor_tensor(dst, xc[j][:, k, :], rstd[j][:], ALU.mult)
            i.then_inc(norm_done[j], 1)

        def span_rows(c, _):
            ra, rb = rows_a[c % 2], rows_b[c % 2]
            dve.wait_ge(s["e0_done"], c + 1)
            need(dve, s["ab_ready"], UNITS * (c - 1))
            step(nc.vector.tensor_scalar(e0[:], e0[:], 1.0, None, ALU.add))
            step(nc.vector.reciprocal(gap[:], e0[:]))
            step(nc.vector.tensor_scalar(near[:], gap[:], float(S), ROUND, ALU.mult, ALU.add))
            step(nc.vector.tensor_scalar(ra[0:H, :], near[:], -ROUND, float(S - 1), ALU.add, ALU.min))
            dve.wait_ge(s["lnx_done"], c + 1)
            soft_rows = slice(SOFT_ROW, SOFT_ROW + H)
            step(nc.vector.scalar_tensor_tensor(soft[:], ln_bank[0][soft_rows, :], 0.0, lnx[soft_rows, :], ALU.max, ALU.add))
            step(nc.vector.scalar_tensor_tensor(near[:], gap[:], -2.0 * S, ra[0:H, :].bitcast(F32), ALU.mult, ALU.add))
            step(nc.vector.tensor_tensor(gap[:], near[:], soft[:], ALU.mult))
            for part, src in enumerate((soft, gap)):
                hi, lo = (rb[64 * part + 32 * i:64 * part + 32 * i + H, :] for i in range(2))
                step(nc.vector.tensor_copy(hi, src[:]))
                step(nc.vector.tensor_tensor(lo, src[:], hi.bitcast(F32), ALU.subtract))
            nc.vector.memset(done_mark[:], 0.0).then_inc(s["rows_done"], 1)

        def unit(c, i):
            n = UNITS * c + i
            dve.wait_ge(s["b_copied"], n + 1)
            need(dve, s["ex_done"], n - 1)
            nc.vector.tensor_tensor(dist[i % 2][:], factors[i % 2][0][:, :], b_copy[i % 2][:], ALU.mult).then_inc(s["dist_done"], 1)

        def outputs(c, _):
            dve.wait_ge(s["rs_done"], c + 1)
            dve.wait_ge(s["pv"], c + 1)
            need(dve, s["x2_proj"], c)
            for k in range(NK):
                i = nc.vector.tensor_tensor(o2[:, k, :], vb[k][:, :], rs[:, k, :], ALU.mult)
            i.then_inc(s["o2_done"], 1)
            if c == FOLD_CHUNK:
                between()

        for i in range(2):
            nc.vector.memset(rows_a[i][:].bitcast(F32), 0.0).then_inc(s["rows_zero"], 1)
            nc.vector.memset(rows_b[i][:].bitcast(F32), 0.0).then_inc(s["rows_zero"], 1)
        nc.vector.memset(vbd[:], 0.0).then_inc(s["vbd_zero"], 1)
        dve.wait_ge(s["rows_zero"], 4)
        for i in range(2):
            nc.vector.memset(rows_a[i][32:33, :].bitcast(F32), 1.0).then_inc(s["rows_zero"], 1)
        table = {"W": (NOW, residual, 0), "Z": (LAST, residual, 1), "R": (NOW, span_rows, None), "A": (NEXT, unit, None),
                 "O": (NEXT, outputs, None)}
        run_periods(DVE_ORDER, norm_steps(norm_steps(table, "C", centre), "N", normalize))

    def tensor(pe):
        def project(wt, src, dst, done):
            for m in range(NK):
                for k in range(NK):
                    i = nc.tensor.matmul(dst[m][:, :], wt[:, k, m * P:(m + 1) * P], src[k], start=k == 0, stop=k == NK - 1)
            i.then_inc(done, 1)

        def output_a(c, _):
            if c == 0:
                pe.wait_ge(wo_in, 2 * 16)
            need(pe, s["x1_done"], NK * c)
            project(wo, [attn_out[:, k, toks(c)] for k in range(NK)], proj, s["x1_proj"])

        def output_l(c, _):
            pe.wait_ge(s["o2_done"], c + 1)
            project(wout, [o2[:, k, :] for k in range(NK)], ab, s["x2_proj"])

        def means(c, j):
            pe.wait_ge(src_done[j], NK * (c + 1))
            need(pe, s["rows_done"] if j == 0 else rstd_done[1], c)
            for k in range(NK):
                i = nc.tensor.matmul(ln_bank[j][:, :], mean_w[:], x[:, k, toks(c)], start=k == 0, stop=k == NK - 1)
            i.then_inc(mean[j], 1)

        def variances(c, j):
            pe.wait_ge(sq_done[j], c + 1)
            for k in range(NK):
                i = nc.tensor.matmul(ln_bank[j][:, :], mean_w[:], sq[j][:, k, :], start=k == 0, stop=k == NK - 1)
            i.then_inc(var[j], 1)

        def spans(c, _):
            if c == 0:
                pe.wait_ge(w_in, 4 * 16)
                pe.wait_ge(sel_in, 2 * 16)
            pe.wait_ge(s["h_done"], c + 1)
            for k in range(NK):
                i = nc.tensor.matmul(ln_bank[0][0:SPAN_ROWS, :], wspan[:, k, :], h[c % 2][:, k, :], start=k == 0, stop=k == NK - 1)
            i.then_inc(s["span"], 1)

        def unit(c, i):
            n = UNITS * c + i
            if i == 0:
                pe.wait_ge(s["rows_zero"], 6)
                pe.wait_ge(s["rows_done"], c + 1)
                need(pe, s["x2_done"], NK * c)
            if i == 1:
                need(pe, s["o2_done"], c)
            need(pe, s["dist_done"], n - 1)
            nc.tensor.matmul(factors[i % 2][0][:, :], sel_a[:, i, :], rows_a[c % 2][:], start=True, stop=True)
            nc.tensor.matmul(factors[i % 2][1][:, :], sel_b[:, i, :], rows_b[c % 2][:], start=True,
                             stop=True).then_inc(s["ab_ready"], 1)

        def values(c, q):
            if q >= 2:
                pe.wait_ge(s["vbd_done"], QUADS * c + q - 1)
            else:
                pe.wait_ge(s["dist_done"], UNITS * (c + 1))
            for k in range(NK):
                i = nc.tensor.matmul(vb[q % 2][:, 0:D], h[c % 2][:, k, q * 2 * S:(q + 1) * 2 * S], wval[:, k, :],
                                     start=k == 0, stop=k == NK - 1)
            i.then_inc(s["val_ready"], 1)

        def sums(c, _):
            pe.wait_ge(s["ex_done"], UNITS * (c + 1))
            for p in range(PAIRS):
                t, g = p // GROUPS, p % GROUPS
                i = nc.tensor.matmul(ab[t][32 * g:32 * g + 32, :], head_ones[:], ex[:, p, :], start=True, stop=True)
            i.then_inc(s["sums"], 1)

        def products(c, _):
            pe.wait_ge(s["vbd_done"], QUADS * (c + 1))
            for b in range(CB):
                for p in range(PAIRS):
                    t, g = p // GROUPS, p % GROUPS
                    i = nc.tensor.matmul(vb[t][32 * g:32 * g + 32, b * S:(b + 1) * S], vbd[:, b, 32 * p:32 * p + 32],
                                         ex[:, p, b * S:(b + 1) * S], start=True, stop=True, skip_group_check=True)
            i.then_inc(s["pv"], 1)

        table = {"W": (NOW, output_a, None), "Z": (LAST, output_l, None), "S": (NOW, spans, None), "A": (NEXT, unit, None),
                 "X": (NEXT, values, None), "U": (NEXT, sums, None), "O": (NEXT, products, None)}
        run_periods(PE_ORDER, norm_steps(norm_steps(table, "M", means), "V", variances))

    def toks(c):
        return slice(c * CW, (c + 1) * CW)

    done_mark = sb("done_mark", [P, 1])
    return {"scalar": scalar, "vector": vector, "tensor": tensor}


def expert_mlps(nc, own, bank, sem, x, h2, sw1, sw2, sw3, w1, w2, sb1, sb3, b1, class_bias, prep, f_in, h2_done, f_done):
    def sb(name, shape, dt=F32):
        return own.enter_context(nc.sbuf_tensor(name, shape, dt))

    NC = NTOK // E
    silu = [sb(f"silu{i}", [P, HS // P, NC]) for i in range(2)]
    gate = [sb(f"gate{i}", [P, HS // P, NC]) for i in range(2)]
    gelu = [sb(f"gelu{i}", [P, 2, NK, NC]) for i in range(2)]
    xb = [sb(f"xb{i}", [P, NK, NC]) for i in range(2)]
    s = {n: sem("t_" + n) for n in "f1 f3 fe silu_done gate_done gelu_done f_out xb_done".split()}
    s["f_done"] = f_done

    def cls(tile, k, c):
        return tile[:, k, :].rearrange("p (b c n) -> p b c n", c=E, n=S // E)[:, :, c, :]

    def flat(ap):
        return ap.rearrange("p (b n) -> p b n", n=S // E)

    def scalar(act):
        for c in range(E):
            act.wait_ge(s["f1"], c + 1)
            if c >= 2:
                act.wait_ge(s["gate_done"], c - 1)
            for m in range(HS // P):
                i = nc.scalar.activation(silu[c % 2][:, m, :], bank[m // 2][:, (m % 2) * NC:(m % 2 + 1) * NC], ACT.Silu,
                                         bias=sb1[:, m:m + 1])
            i.then_inc(s["silu_done"], 1)
            act.wait_ge(s["fe"], c + 1)
            if c >= 2:
                act.wait_ge(s["f_out"], c - 1)
            for k in range(2):
                for m in range(NK):
                    e = CLASS_EXPERTS[c][k]
                    i = nc.scalar.activation(gelu[c % 2][:, k, m, :], bank[4 + k][:, m * NC:(m + 1) * NC], ACT.Gelu,
                                             bias=b1[:, e, m:m + 1])
            i.then_inc(s["gelu_done"], 1)

    def vector(dve):
        def gates(c):
            dve.wait_ge(s["f3"], c + 1)
            dve.wait_ge(s["silu_done"], c + 1)
            if c >= 2:
                dve.wait_ge(s["f_out"], c - 1)
            for m in range(HS // P):
                i = nc.vector.scalar_tensor_tensor(gate[c % 2][:, m, :], bank[2 + m // 2][:, (m % 2) * NC:(m % 2 + 1) * NC],
                                                   sb3[:, m:m + 1], silu[c % 2][:, m, :], ALU.add, ALU.mult)
            i.then_inc(s["gate_done"], 1)

        gates(0)
        for c in range(E):
            for k in range(NK):
                i = nc.vector.tensor_scalar(flat(xb[c % 2][:, k, :]), cls(x, k, c), class_bias[:, c, k:k + 1], None, ALU.add)
                i.then_inc(s["xb_done"], 1)
            if c + 1 < E:
                gates(c + 1)
            dve.wait_ge(s["f_out"], c + 1)
            dve.wait_ge(s["xb_done"], NK * (c + 1))
            for k in range(NK):
                nc.vector.scalar_tensor_tensor(cls(x, k, c), flat(bank[6][:, k * NC:(k + 1) * NC]), 0.25, flat(xb[c % 2][:, k, :]),
                                               ALU.mult, ALU.add).then_inc(s["f_done"], 1)

    def tensor(pe):
        pe.wait_ge(h2_done, NCH)
        pe.wait_ge(f_in, 10 * 16)
        pe.wait_ge(prep, 1)

        def hidden(c, wt, banks, done, free, count):
            if c:
                pe.wait_ge(free, count)
            for m in range(HS // P):
                for k in range(NK):
                    i = nc.tensor.matmul(flat(bank[banks + m // 2][:, (m % 2) * NC:(m % 2 + 1) * NC]), wt[:, k, m * P:(m + 1) * P],
                                         cls(h2, k, c), start=k == 0, stop=k == NK - 1)
            i.then_inc(done, 1)

        def experts(c):
            if c:
                pe.wait_ge(s["gelu_done"], c)
            for j, e in enumerate(CLASS_EXPERTS[c]):
                for m in range(NK):
                    for k in range(NK):
                        i = nc.tensor.matmul(flat(bank[4 + j][:, m * NC:(m + 1) * NC]), w1[:, e, k, m * P:(m + 1) * P],
                                             cls(h2, k, c), start=k == 0, stop=k == NK - 1)
            i.then_inc(s["fe"], 1)

        def output(c):
            pe.wait_ge(s["gate_done"], c + 1)
            pe.wait_ge(s["gelu_done"], c + 1)
            if c:
                pe.wait_ge(s["f_done"], NK * c)
            for m in range(NK):
                terms = [(sw2[:, k, m * P:(m + 1) * P], gate[c % 2][:, k, :]) for k in range(HS // P)]
                terms += [(w2[:, e, k, m * P:(m + 1) * P], gelu[c % 2][:, j, k, :])
                          for j, e in enumerate(CLASS_EXPERTS[c]) for k in range(NK)]
                for n, (lhs, rhs) in enumerate(terms):
                    i = nc.tensor.matmul(bank[6][:, m * NC:(m + 1) * NC], lhs, rhs, start=n == 0, stop=n == len(terms) - 1)
            i.then_inc(s["f_out"], 1)

        for c in range(E + 1):
            if c < E:
                hidden(c, sw1, 0, s["f1"], s["silu_done"], c)
                hidden(c, sw3, 2, s["f3"], s["gate_done"], c)
                experts(c)
            if c:
                output(c - 1)

    return {"scalar": scalar, "vector": vector, "tensor": tensor}


def constants():
    rows = np.arange(P)
    position = np.arange(S) % (S // E) * E + np.arange(S) // (S // E)
    even = np.stack([rows % 32 < DK, rows % 32 >= DK], 1).astype(np.float32)
    select = np.zeros((PAIRS, PAIRS, S2P), np.float16)
    sel_a = np.zeros((33, PAIRS, P), np.float32)
    sel_b = np.zeros((B_ROWS, PAIRS, P), np.float32)
    for p in range(PAIRS):
        select[p, p] = SEL
        for e in range(2):
            part = slice(S * e, S * e + S)
            sel_a[2 * p + e, p, part] = -1.0
            sel_a[32, p, part] = position
            for i in range(2):
                sel_b[32 * i + 2 * p + e, p, part] = position
                sel_b[64 + 32 * i + 2 * p + e, p, part] = 1.0
    half = rows[:, None] // S
    return {
        "c_ident": np.eye(P, dtype=np.float32),
        "c_even": even,
        "c_select": select.reshape(PAIRS, -1),
        "c_sel_a": sel_a.reshape(33, -1),
        "c_sel_b": sel_b.reshape(B_ROWS, -1),
        "c_head_ones": (half == np.arange(32)[None] // DK).astype(np.float32),
    }


def kernel(**inputs):
    import concourse.bacc as bacc
    from concourse.bass_utils import run_bass_kernel_spmd

    a = {n: np.asarray(v) for n, v in inputs.items()}
    order = np.arange(S).reshape(S // E, E).T.reshape(-1)

    def cols(vec):
        return vec.reshape(-1, P).T

    span = a["L0_attn_W_span"]
    mask = a["mask_1x1xSxS2_bf1"][0, 0][order].view(np.uint8)
    maskT = np.ones((KT * P, S), np.uint8)
    maskT[:S2] = mask.T
    ctxT = np.zeros((B, D, S2P), np.float32)
    ctxT[:, :, :S2] = a["ctx_1024"].transpose(0, 2, 1)
    arrays = {
        "xT": a["x"][:, order].reshape(NTOK, D).T,
        "ctxT": ctxT,
        "maskQ": mask,
        "maskT": maskT,
        "wqT": a["L0_xattn_wq_w"].T, "wkT": a["L0_xattn_wk_w"].T, "wvT": a["L0_xattn_wv_w"].T, "woT": a["L0_xattn_wo_w"].T,
        "bq": cols(a["L0_xattn_wq_b"]), "bk": cols(a["L0_xattn_wk_b"]), "bv": cols(a["L0_xattn_wv_b"]), "bo": cols(a["L0_xattn_wo_b"]),
        "wspanT": np.concatenate([span[0::2], np.zeros((SOFT_ROW - H, D), np.float32), span[1::2]]).T,
        "wvalT": a["L0_attn_W_val"].T, "woutT": a["L0_attn_W_out"].T,
        "sw1": a["L0_ffn_sw1"], "sw3": a["L0_ffn_sw3"], "sw2": a["L0_ffn_sw2"],
        "sb1": cols(a["L0_ffn_sb1"]), "sb3": cols(a["L0_ffn_sb3"]), "sb2": cols(a["L0_ffn_sb2"]),
        "w1": a["L0_ffn_w1"], "w2": a["L0_ffn_w2"],
        "b1": cols(a["L0_ffn_b1"].reshape(-1)), "b2": cols(a["L0_ffn_b2"].reshape(-1)),
        **constants(),
    }
    arrays = {n: np.ascontiguousarray(v) for n, v in arrays.items()}

    nc = bacc.Bacc("TRN2", target_bir_lowering=False, num_devices=1)
    ins = {n: nc.dram_tensor(f"in_{n}", v.shape, mybir.dt.from_np(v.dtype), kind="ExternalInput").ap() for n, v in arrays.items()}
    out = nc.dram_tensor("out_yT", (D, NTOK), F32, kind="ExternalOutput").ap()
    build(nc, ins, out)
    r = run_bass_kernel_spmd(nc, [{f"in_{n}": v for n, v in arrays.items()}], core_ids=[0])
    yT = r.results[0]["out_yT"]
    return np.ascontiguousarray(yT.reshape(D, B, E, S // E).transpose(1, 3, 2, 0).reshape(B, S, D))
```

```python
from contextlib import ExitStack

import numpy as np

import concourse.bass as bass
from concourse import mybir

F32 = mybir.dt.float32
F32R = mybir.dt.float32r
BF16 = mybir.dt.bfloat16
F16 = mybir.dt.float16
U8 = mybir.dt.uint8
ALU = mybir.AluOpType
ACT = mybir.ActivationFunctionType
AX = mybir.AxisListType

P = 128
B, S, S2, D = 32, 64, 1601, 256
H = 16
DK = D // H
NTOK = B * S
NK = D // P
PAIRS = H // 2
GROUPS = 4
PW = 2 * S
KT = -(-S2 // P)
S2P = S2 + 1
KC = 4
CHUNKS = [(0, 400), (400, 400), (800, 400), (1200, 402)]
MAXCH = [(0, 400), (400, 400), (800, 400), (1200, 401)]
NCK = NK * KC
NMX = PAIRS * KC
NST = 2 * KT
NACC = KT - 1
NP = 5
SPLIT = NK * KC
UP = 32.0
SEL = 1024.0
MASKED = -float(2 ** 25)
KSTACK = 3 * 32
KROWS = KSTACK + PAIRS
EPS = 1e-5
HS = 512
E = 8
PRIME, HASH = 11, 7919
NCH = 4
CW = NTOK // NCH
CB = CW // S
SOFT_ROW = 32
SPAN_ROWS = SOFT_ROW + H
B_ROWS = 3 * 32 + H
W_SLOTS = 4
FOLD_CHUNK = 0
ROUND = 1.5 * 2.0 ** 23

CLASS_EXPERTS = [[(c * PRIME + k * HASH) % E for k in range(2)] for c in range(E)]


def keys_of(kt):
    return min(P, S2 - kt * P)


class Batch:

    def __init__(self, n, slot, used):
        self.n, self.slot, self.used = n, slot, used


def at(n):
    return Batch(n, n % 2, n // 2 + 1)


def loop_batch(t, offset):
    return Batch(2 * t + offset, offset % 2, t + offset // 2 + 1)


def first(b):
    return isinstance(b.n, int) and b.n == 0


def last(b):
    return isinstance(b.n, int) and b.n == B - 1


def before(b):
    return Batch(b.n - 1, 1 - b.slot, None)


def need(eng, sem, value):
    if not isinstance(value, int) or value > 0:
        eng.wait_ge(sem, value)


def build(nc, ins, out_dram):
    ctx = ExitStack()
    with ctx:
        def sem(name):
            return ctx.enter_context(nc.semaphore(name))

        bank = [ctx.enter_context(nc.psum_tensor(f"bank{i}", [P, 512], F32)) for i in range(8)]
        attn_out = ctx.enter_context(nc.sbuf_tensor("attn_out", [P, NK, NTOK], F32))
        ident = ctx.enter_context(nc.sbuf_tensor("ident", [P, P], F32))
        mean_w = ctx.enter_context(nc.sbuf_tensor("mean_w", [P, P], F32))
        wo = ctx.enter_context(nc.sbuf_tensor("wo", [P, NK, D], F32))
        bo = ctx.enter_context(nc.sbuf_tensor("bo", [P, NK], F32))
        wo_in = sem("wo_in")
        eps_col = ctx.enter_context(nc.sbuf_tensor("eps_col", [P, 1], F32))
        q_parts = nc.dram_tensor("q_parts", (2, D, NTOK), F16).ap()
        with ExitStack() as attention:
            def sb(name, shape, dt):
                return attention.enter_context(nc.sbuf_tensor(name, shape, dt))
            w = dict(
                wk_hi=sb("wk_hi", [P, NK, D], F32R), wk_lo=sb("wk_lo", [P, NK, D], F32R),
                wv_hi=sb("wv_hi", [P, NK, D], F32R), wv_lo=sb("wv_lo", [P, NK, D], F32R),
                bk=sb("bk", [P, NK], F32), bv=sb("bv", [P, NK], F32),
                even_rows=sb("even_rows", [P, 2], F32),
                mask_q=sb("mask_q", [P, S2], BF16), mask_k=sb("mask_k", [P, KT, S], BF16),
                rows_all=sb("rows_all", [1, 1], mybir.dt.int32),
                ident_h=sb("ident_h", [P, P], BF16), ones=sb("ones", [P, 32], F32),
            )
            first_in = dict(
                raw=sb("ctx_raw", [P, NK, S2P], F32), c_hi=sb("ctx_hi", [P, NK, S2P], F32R), c_lo=sb("ctx_lo", [P, NK, S2P], F32R),
                kstack=[sb(f"kstack{i}", [P, PAIRS, S2P], F16) for i in range(2)],
                qstack=[sb(f"qstack{i}", [P, PAIRS, PW], F16) for i in range(2)],
                q_hi=[sb(f"q_hi{i}", [P, NK, CW], F16) for i in range(2)],
                q_lo=[sb(f"q_lo{i}", [P, NK, CW], F16) for i in range(2)],
                ctx_in=sem("ctx_in"),
                ctx_hi=sem("ctx_hi"),
                ctx_lo=sem("ctx_lo"),
                rows_in=sem("select_rows_in"), stack_zero=sem("stack_zero"),
            )
            before, ready = queries(nc, ins, bank, w, first_in, wo, bo, wo_in, ident, mean_w, eps_col, q_parts, sem)
            cross = cross_attention(nc, sb, ins, bank, w, first_in, ident, attn_out, q_parts, sem)

            def both(eng, name):
                before[name](eng)
                for done, count in ready:
                    eng.wait_ge(done, count)
                cross[name](eng)

            with nc.Block() as block:
                @block.sync
                def _(sp):
                    both(sp, "sync")

                @block.vector
                def _(dve):
                    both(dve, "vector")

                @block.gpsimd
                def _(pool):
                    both(pool, "gpsimd")

                @block.scalar
                def _(act):
                    both(act, "scalar")

                @block.tensor
                def _(pe):
                    both(pe, "tensor")
        tail(nc, ins, bank, attn_out, wo, bo, wo_in, mean_w, eps_col, out_dram, sem)


def run_periods(order, table):
    depth = max(late for late, _, _ in table.values())
    for period in range(NCH + depth):
        count = {}
        for step in order.split():
            late, do, arg = table[step]
            i = count.get(step, 0)
            count[step] = i + 1
            if 0 <= period - late < NCH:
                do(period - late, i if arg is None else arg)


def queries(nc, ins, bank, w, first_in, wo, bo, wo_in, ident, mean_w, eps_col, q_parts, sem):
    with ExitStack() as own:
        def sb(name, shape, dt=F32):
            return own.enter_context(nc.sbuf_tensor(name, shape, dt))

        x = sb("x0", [P, NK, NTOK])
        wq, wk, wv = (sb(n, [P, NK, D]) for n in ("wq", "wk", "wv"))
        bq, bk_raw, bq_up = sb("bq", [P, NK]), sb("bk_raw", [P, NK]), sb("bq_up", [P, NK])
        mask_u8 = sb("mask_u8", [P, S2], U8)
        maskT_u8 = sb("maskT_u8", [P, KT, S], U8)
        row_ok, row_all = sb("row_ok", [S, 1]), sb("row_all", [S, 1])
        row_diag = sb("row_diag", [S, S])
        row_live = sb("row_live", [P, S])
        ones_q = sb("ones_q", [S, P])
        xc = [sb(f"xc{i}", [P, NK, CW]) for i in range(2)]
        sq = [sb(f"sq{i}", [P, NK, CW]) for i in range(2)]
        rstd = [sb(f"rstd{i}", [P, CW]) for i in range(2)]
        xn = [sb(f"xn{i}", [P, NK, CW]) for i in range(2)]
        q = [sb(f"q{i}", [P, NK, CW]) for i in range(2)]
        q_hi, q_lo = first_in["q_hi"], first_in["q_lo"]
        mean_bank, var_bank, proj_bank, row_bank = bank[0:2], bank[2:4], bank[4:6], bank[6]

        x_in = [sem(f"q_x_in{c}") for c in range(NCH)]
        const_in, wq_in, w_in, mask_in = (sem("q_" + n) for n in ("const_in", "wq_in", "w_in", "mask_in"))
        memsets, up_done, parts_hi, consts, rows_seen, diag_ready, live_ready, live_done = (
            sem("q_" + n) for n in ("memsets", "up_done", "parts_hi", "consts", "rows_seen", "diag_ready", "live_ready", "live_done"))
        mean, xc_done, sq_done, var, lnv, rstd_done, xn_done, proj, biased, live, hi_done, lo_done = (
            sem("q_" + n) for n in "mean xc sq var lnv rstd xn proj biased live hi lo".split())
        q_out = [sem(f"q_out{i}") for i in range(2)]
        raw, c_hi, c_lo = first_in["raw"], first_in["c_hi"], first_in["c_lo"]

        PE_ORDER, DVE_ORDER, ACT_ORDER = "M V P", "C L N G X", "S H I B X"

        def toks(c):
            return slice(c * CW, (c + 1) * CW)

        def sync(sp):
            def load(tile, src, done):
                sp.dma_start(tile, src).then_inc(done, 16)

            def rows(name):
                return ins[name].rearrange("(k p) n -> p k n", p=P)

            load(x[:, :, toks(0)], rows("xT")[:, :, toks(0)], x_in[0])
            load(wq[:], rows("wqT"), wq_in)
            load(bq[:], ins["bq"], wq_in)
            load(x[:, :, toks(1)], rows("xT")[:, :, toks(1)], x_in[1])
            load(ident[:], ins["c_ident"], const_in)
            load(w["even_rows"][:], ins["c_even"], const_in)
            for e in range(2):
                load(mask_u8[S * e:S * e + S, :], ins["maskQ"], mask_in)
            load(maskT_u8[:], ins["maskT"].rearrange("(n p) q -> p n q", p=P), mask_in)
            for c in range(2, NCH):
                load(x[:, :, toks(c)], rows("xT")[:, :, toks(c)], x_in[c])
            load(wk[:], rows("wkT"), w_in)
            load(wv[:], rows("wvT"), w_in)
            load(bk_raw[:], ins["bk"], w_in)
            load(w["bv"][:], ins["bv"], w_in)
            load(raw[:], ins["ctxT"][0].rearrange("(k p) s -> p k s", p=P), first_in["ctx_in"])
            for i in range(2):
                load(first_in["kstack"][i][KSTACK:KROWS, :, :], ins["c_select"].rearrange("r (p s) -> r p s", s=S2P), first_in["rows_in"])
            load(wo[:], rows("woT"), wo_in)
            load(bo[:], ins["bo"], wo_in)
            for c in range(NCH):
                sp.wait_ge(lo_done, c + 1)
                for i, part in enumerate((q_hi, q_lo)):
                    sp.dma_start(q_parts[i].rearrange("(k p) t -> p k t", p=P)[:, :, toks(c)], part[c % 2][:]).then_inc(q_out[c % 2], 16)
            for i in range(2):
                sp.wait_ge(q_out[i], 2 * 16 * (NCH // 2))

        def vector(dve):
            def centre(c, _):
                dve.wait_ge(x_in[c], 16)
                dve.wait_ge(mean, c + 1)
                need(dve, xn_done, c - 1)
                for k in range(NK):
                    i = nc.vector.tensor_tensor(xc[c % 2][:, k, :], x[:, k, toks(c)], mean_bank[c % 2][:, :], ALU.subtract)
                i.then_inc(xc_done, 1)

            def normalize(c, _):
                dve.wait_ge(rstd_done, c + 1)
                dve.wait_ge(xc_done, c + 1)
                need(dve, proj, c - 1)
                for k in range(NK):
                    i = nc.vector.tensor_tensor(xn[c % 2][:, k, :], xc[c % 2][:, k, :], rstd[c % 2][:], ALU.mult)
                i.then_inc(xn_done, 1)
                if c == 0:
                    mask_rows()
                if c == 1:
                    dve.wait_ge(live_ready, 1)
                    nc.vector.tensor_copy(row_live[:], row_bank[:, 0:S]).then_inc(live_done, 1)
                    nc.vector.tensor_copy(w["rows_all"][:], row_bank[0:1, S:S + 1]).then_inc(live_done, 1)
                    dve.wait_ge(live_done, 2)

            def clear(c, _):
                dve.wait_ge(biased, c + 1)
                for k in range(NK):
                    qv = q[c % 2][:, k, :].rearrange("p (b s) -> p b s", s=S)
                    i = nc.vector.tensor_tensor(qv, qv, row_live[:, :].unsqueeze(1).to_broadcast([P, CB, S]), ALU.mult)
                i.then_inc(live, 1)

            def low(c, _):
                dve.wait_ge(hi_done, c + 1)
                need(dve, q_out[c % 2], 2 * 16 * (c // 2))
                nc.vector.tensor_tensor(q_lo[c % 2][:], q[c % 2][:], q_hi[c % 2][:], ALU.subtract).then_inc(lo_done, 1)

            def split_lo(c, _):
                s0, n = CHUNKS[c]
                if c == 0:
                    weights_lo()
                for k in range(NK):
                    dve.wait_ge(first_in["ctx_hi"], NK * c + k + 1)
                    nc.vector.tensor_tensor(c_lo[:, k, s0:s0 + n], raw[:, k, s0:s0 + n], c_hi[:, k, s0:s0 + n].bitcast(F32),
                                            ALU.subtract).then_inc(first_in["ctx_lo"], 1)

            def weights_lo():
                dve.wait_ge(w_in, 4 * 16)
                dve.wait_ge(parts_hi, 2)
                nc.vector.scalar_tensor_tensor(w["wk_lo"][:], wk[:], UP, w["wk_hi"][:].bitcast(F32),
                                               ALU.mult, ALU.subtract).then_inc(consts, 1)
                nc.vector.tensor_tensor(w["wv_lo"][:], wv[:], w["wv_hi"][:].bitcast(F32), ALU.subtract).then_inc(consts, 1)
                nc.vector.tensor_scalar(w["bk"][:], bk_raw[:], UP, None, ALU.mult).then_inc(consts, 1)

            def mask_rows():
                dve.wait_ge(const_in, 2 * 16)
                dve.wait_ge(mask_in, 3 * 16)
                nc.vector.tensor_reduce(row_all[:], mask_u8[0:S, :], AX.X, ALU.min).then_inc(rows_seen, 1)
                nc.vector.tensor_reduce(row_ok[:], mask_u8[0:S, :], AX.X, ALU.max).then_inc(rows_seen, 1)
                dve.wait_ge(rows_seen, 2)
                nc.vector.tensor_scalar(row_diag[:], ident[0:S, 0:S], row_ok[:, 0:1], None, ALU.mult).then_inc(diag_ready, 1)

            nc.vector.memset(mean_w[:], 1.0 / D).then_inc(memsets, 1)
            nc.vector.memset(eps_col[:], EPS).then_inc(memsets, 1)
            nc.vector.memset(ones_q[:], 1.0).then_inc(memsets, 1)
            nc.vector.memset(w["ones"][:], 1.0).then_inc(consts, 1)
            for i in range(2):
                nc.vector.memset(first_in["qstack"][i][:], 0.0).then_inc(first_in["stack_zero"], 1)
            dve.wait_ge(wq_in, 2 * 16)
            nc.vector.tensor_scalar(bq_up[:], bq[:], UP, None, ALU.mult).then_inc(up_done, 1)
            run_periods(DVE_ORDER, {"C": (0, centre, None), "N": (1, normalize, None), "G": (2, clear, None), "L": (3, low, None),
                                    "X": (2, split_lo, None)})

        def gpsimd(pool):
            pool.wait_ge(mask_in, 3 * 16)
            nc.gpsimd.tensor_scalar(w["mask_q"][:], mask_u8[:], -1.0, -MASKED, ALU.add, ALU.mult).then_inc(consts, 1)
            nc.gpsimd.tensor_scalar(w["mask_k"][:], maskT_u8[:], -1.0, -MASKED, ALU.add, ALU.mult).then_inc(consts, 1)
            pool.wait_ge(const_in, 2 * 16)
            nc.gpsimd.tensor_copy(w["ident_h"][:], ident[:]).then_inc(consts, 1)

        def scalar(act):
            def square(c, _):
                act.wait_ge(xc_done, c + 1)
                need(act, var, c - 1)
                nc.scalar.activation(sq[c % 2][:], xc[c % 2][:], ACT.Square).then_inc(sq_done, 1)

            def inverse(c, _):
                act.wait_ge(var, c + 1)
                need(act, xn_done, c - 1)
                nc.scalar.activation(rstd[c % 2][:], var_bank[c % 2][:, :], ACT.Ln, bias=eps_col[:, 0:1]).then_inc(lnv, 1)
                act.wait_ge(lnv, c + 1)
                nc.scalar.activation(rstd[c % 2][:], rstd[c % 2][:], ACT.Exp, scale=-0.5).then_inc(rstd_done, 1)

            def bias(c, _):
                act.wait_ge(proj, c + 1)
                need(act, lo_done, c - 1)
                for m in range(NK):
                    i = nc.scalar.activation(q[c % 2][:, m, :], proj_bank[m][:, :], ACT.Identity, bias=bq_up[:, m:m + 1], scale=UP)
                i.then_inc(biased, 1)

            def high(c, _):
                act.wait_ge(live, c + 1)
                need(act, q_out[c % 2], 2 * 16 * (c // 2))
                nc.scalar.activation(q_hi[c % 2][:], q[c % 2][:], ACT.Copy).then_inc(hi_done, 1)

            def split_hi(c, _):
                s0, n = CHUNKS[c]
                if c == 0:
                    act.wait_ge(w_in, 4 * 16)
                    nc.scalar.activation(w["wk_hi"][:], wk[:], ACT.Copy, scale=UP).then_inc(parts_hi, 1)
                    nc.scalar.activation(w["wv_hi"][:], wv[:], ACT.Copy).then_inc(parts_hi, 1)
                    act.wait_ge(first_in["ctx_in"], 16)
                for k in range(NK):
                    nc.scalar.activation(c_hi[:, k, s0:s0 + n], raw[:, k, s0:s0 + n], ACT.Copy).then_inc(first_in["ctx_hi"], 1)

            nc.scalar.preload_act_table_set("natural_log_exp_and_others")
            act.wait_ge(memsets, 2)
            act.wait_ge(up_done, 1)
            run_periods(ACT_ORDER, {"S": (0, square, None), "I": (1, inverse, None), "B": (2, bias, None), "H": (3, high, None),
                                    "X": (2, split_hi, None)})

        def tensor(pe):
            def means(c, _):
                pe.wait_ge(x_in[c], 16)
                need(pe, xc_done, c - 1)
                for k in range(NK):
                    i = nc.tensor.matmul(mean_bank[c % 2][:, :], mean_w[:], x[:, k, toks(c)], start=k == 0, stop=k == NK - 1)
                i.then_inc(mean, 1)

            def variances(c, _):
                pe.wait_ge(sq_done, c + 1)
                need(pe, lnv, c - 1)
                for k in range(NK):
                    i = nc.tensor.matmul(var_bank[c % 2][:, :], mean_w[:], sq[c % 2][:, k, :], start=k == 0, stop=k == NK - 1)
                i.then_inc(var, 1)
                if c == 1:
                    pe.wait_ge(diag_ready, 1)
                    nc.tensor.matmul(row_bank[:, 0:S], ones_q[:], row_diag[:], start=True, stop=True, skip_group_check=True)
                    nc.tensor.matmul(row_bank[0:1, S:S + 1], row_all[:], ones_q[:, 0:1], start=False, stop=True,
                                     skip_group_check=True).then_inc(live_ready, 1)

            def project(c, _):
                pe.wait_ge(xn_done, c + 1)
                need(pe, biased, c)
                for m in range(NK):
                    for k in range(NK):
                        i = nc.tensor.matmul(proj_bank[m][:, :], wq[:, k, m * P:(m + 1) * P], xn[c % 2][:, k, :],
                                             start=k == 0, stop=k == NK - 1)
                i.then_inc(proj, 1)

            pe.wait_ge(memsets, 3)
            pe.wait_ge(wq_in, 2 * 16)
            run_periods(PE_ORDER, {"M": (0, means, None), "V": (1, variances, None), "P": (2, project, None)})

        ready = [(consts, 7), (parts_hi, 2), (live_done, 2), (const_in, 2 * 16), (w_in, 4 * 16)]
        return {"sync": sync, "vector": vector, "gpsimd": gpsimd, "scalar": scalar, "tensor": tensor}, ready


def cross_attention(nc, sb, ins, bank, w, first_in, ident, attn_out, q_parts, sem):
    raw, c_hi, c_lo, kstack, qstack = (first_in[n] for n in ("raw", "c_hi", "c_lo", "kstack", "qstack"))
    ctx_in, ctx_hi, ctx_lo = (first_in[n] for n in ("ctx_in", "ctx_hi", "ctx_lo"))
    k_hi = sb("k_hi", [P, NK, S2P], F16)
    k_lo = sb("k_lo", [P, NK, S2P], F16)
    v = [sb(f"v{i}", [P, KT, D], F32) for i in range(2)]
    probs = [sb(f"probs{i}", [P, PAIRS, PW], F32) for i in range(NP)]
    acc = [sb(f"acc{i}", [P, PAIRS, PW], F32) for i in range(2)]
    junk = [sb(f"junk{i}", [P, 402], BF16) for i in range(2)]
    lead = sb("lead", [P, NMX], F32)
    part_max = sb("part_max", [P, PAIRS, KC], F32)
    row_max = sb("row_max", [P, PAIRS], F32)
    shift = sb("shift", [P, PAIRS], F32)
    rsum = sb("rsum", [P, NK, PW], F32)
    o_norm = sb("o_norm", [P, NK, PW], F32)
    o_even = sb("o_even", [P, NK, S], F32)

    pj = bank[0:2]
    st = bank[2:4]
    sm = bank[4:6]
    ob = bank[6:8]

    k_proj = sem("k_proj")
    v_proj = sem("v_proj")
    khi_done = sem("khi_done")
    klo_done = sem("klo_done")
    v_done = sem("v_done")
    kstack_in = [[sem(f"kstack_in{i}{p}") for p in range(PAIRS)] for i in range(2)]
    qstack_in = [sem(f"qstack_in{i}") for i in range(2)]
    sm_ready = sem("sm_ready")
    sm_done = sem("sm_done")
    max_found = sem("max_found")
    shift_ready = sem("shift_ready")
    shift_rows = sem("shift_rows")
    shift_done = sem("shift_done")
    st_ready = sem("st_ready")
    exp_done = sem("exp_done")
    pv_done = sem("pv_done")
    acc_done = sem("acc_done")
    sums_ready = sem("sums_ready")
    rsum_done = sem("rsum_done")
    o_read = sem("o_read")
    even_done = sem("even_done")
    out_done = sem("out_done")

    STACK_DMAS = 3
    QSTACK_DMAS = 6

    def acc_count(n, kt):
        return NACC * n + max(kt, 1)

    SLOTS = ["K S0 L S1 K", "S0 K S1 K P R", "S0 N K S1 K O P", "S0 K S1 K P",
             "S0 M V M S1 M V M P M", "S0 M V M S1 M V M P M", "S0 H M V M S1 M X V M P M", "S0 H M V M S1 M X V M P M",
             "S0 H M V S1 M V M X P M", "S0 H M X V S1 M V H M X P M", "S0 H M V M S1 M P M G X", "S0 S1 H X P T",
             "S0 S1 P H X"]
    slots, counts = [], {}
    for slot in SLOTS:
        slots.append([])
        for step in slot.split():
            if step in ("S0", "S1"):
                slots[-1].append(("S", int(step[1])))
            else:
                slots[-1].append((step, counts.get(step, 0)))
                counts[step] = counts.get(step, 0) + 1
    assert (counts["K"], counts["V"], counts["M"], counts["H"], counts["X"], counts["P"]) == (NCK, KT, NMX, SPLIT, SPLIT, KT - 1)

    def turns(eng, emit):
        def turn(n):
            def or_none(m):
                return at(m) if 0 <= m < B else None
            emit(or_none(n), or_none(n + 1), or_none(n + 2), or_none(n + 3))
        for n in (-1, 0, 1):
            turn(n)
        with eng.Fori(1, (B - 4) // 2) as t:
            for u in range(2):
                emit(loop_batch(t, u), loop_batch(t, u + 1), loop_batch(t, u + 2), loop_batch(t, u + 3))
        for n in range(B - 4, B):
            turn(n)

    def sync(sp):
        def load(b):
            need(sp, ctx_lo, SPLIT * b.n)
            src = ins["ctxT"][b.n] if isinstance(b.n, int) else ins["ctxT"][bass.ds(b.n, 1)].rearrange("a d s -> (a d) s")
            sp.dma_start(raw[:], src.rearrange("(k p) s -> p k s", p=P)).then_inc(ctx_in, 16)

        def lay_out_queries(b):
            need(sp, st_ready, NST * (b.n - 1))
            for i, part in enumerate((0, 0, 1)):
                for e in range(2):
                    tok = bass.ds(b.n * S, S)
                    src = q_parts[part, :, tok].rearrange("(p e d) s -> e d p s", e=2, d=DK)[e]
                    sp.dma_start(qstack[b.slot][32 * i + DK * e:32 * i + DK * (e + 1), :, S * e:S * (e + 1)],
                                 src).then_inc(qstack_in[b.slot], 16)

        def lay_out_keys(b, t):
            sp.wait_ge(klo_done, NCK * b.n + KC * (t + 1))
            for g in range(GROUPS):
                p = GROUPS * t + g
                for i, part in enumerate((k_hi, k_lo, k_hi)):
                    sp.dma_start(kstack[b.slot][32 * i:32 * i + 32, p, :],
                                 part[32 * g:32 * g + 32, t, :]).then_inc(kstack_in[b.slot][p], 16)

        sp.wait_ge(first_in["stack_zero"], 2)
        load(at(1))

        def turn(cur, nxt, split, third):
            if nxt:
                lay_out_queries(nxt)
                for t in range(NK):
                    lay_out_keys(nxt, t)
            if third:
                load(third)
        turns(sp, turn)

    def add_rows(eng, ops, b, kt):
        sums, m = acc[b.slot], keys_of(kt)
        eng.wait_ge(exp_done, NST * b.n + 2 * kt + 2)
        need(eng, acc_done, NACC * b.n + kt - 1)
        if kt == 1:
            need(eng, sums_ready, b.n - 1)
            ops.tensor_tensor(sums[:], probs[0][:], probs[1][:], ALU.add).then_inc(acc_done, 1)
        else:
            ops.tensor_tensor(sums[0:m], sums[0:m], probs[kt % NP][0:m], ALU.add).then_inc(acc_done, 1)

    def gpsimd(pool):
        def turn(cur, nxt, split, third):
            if cur and not last(cur):
                for kt in range(1, KT):
                    add_rows(pool, nc.gpsimd, cur, kt)
        turns(pool, turn)

    def scalar(act):
        def split_hi(b, i):
            k, (s0, n) = i % NK, CHUNKS[i // NK]
            if i == 0:
                act.wait_ge(ctx_in, 16 * (b.n + 1))
            if k == 0 and not first(b):
                act.wait_ge(v_proj, KT * (b.n - 1) + -(-min(s0 + n, S2) // P))
            nc.scalar.activation(c_hi[:, k, s0:s0 + n], raw[:, k, s0:s0 + n], ACT.Copy).then_inc(ctx_hi, 1)

        def exponentials(b, kt, h):
            m = keys_of(kt)
            if h == 0:
                if kt >= NP:
                    act.wait_ge(pv_done, KT * b.n + kt - NP + 1)
                    act.wait_ge(acc_done, acc_count(b.n, kt - NP))
                else:
                    old = max(x for x in range(KT) if x % NP == kt)
                    need(act, pv_done, KT * (b.n - 1) + old + 1)
                    need(act, acc_done, acc_count(b.n - 1, old))
            act.wait_ge(st_ready, NST * b.n + 2 * kt + h + 1)
            nc.scalar.activation(probs[kt % NP][0:m, GROUPS * h:GROUPS * (h + 1), :], st[h][0:m, :], ACT.Exp,
                                 scale=DK ** -0.5 / (UP * UP)).then_inc(exp_done, 1)

        def keys_hi(b, c):
            t, (s0, n) = c // KC, CHUNKS[c % KC]
            if c % KC == 0:
                for p in range(GROUPS * t, GROUPS * (t + 1)):
                    need(act, kstack_in[1 - b.slot][p], 16 * STACK_DMAS * (b.used - 1 + b.slot))
            act.wait_ge(k_proj, NCK * b.n + c + 1)
            nc.scalar.activation(k_hi[:, t, s0:s0 + n], pj[(b.slot + c) % 2][:, 0:n], ACT.Identity,
                                 bias=w["bk"][:, t:t + 1]).then_inc(khi_done, 1)

        def values(b, i):
            m = keys_of(i)
            if i == 0:
                need(act, pv_done, KT * (b.n - 1))
            act.wait_ge(v_proj, KT * b.n + i + 1)
            nc.scalar.activation(v[b.slot][0:m, i, :], pj[(b.slot + NCK + i) % 2][0:m, 0:D], ACT.Copy).then_inc(v_done, 1)

        def turn(cur, nxt, split, third):
            for kt in range(KT):
                for what, i in slots[kt]:
                    if what == "S" and cur:
                        exponentials(cur, kt, i)
                    if what == "K" and nxt:
                        keys_hi(nxt, i)
                    if what == "V" and nxt:
                        values(nxt, i)
                    if what == "H" and split:
                        split_hi(split, i)
        turns(act, turn)

    def vector(dve):
        def split_lo(b, i):
            k, (s0, n) = i % NK, CHUNKS[i // NK]
            dve.wait_ge(ctx_hi, SPLIT * b.n + i + 1)
            nc.vector.tensor_tensor(c_lo[:, k, s0:s0 + n], raw[:, k, s0:s0 + n],
                                    c_hi[:, k, s0:s0 + n].bitcast(F32), ALU.subtract).then_inc(ctx_lo, 1)

        def keys_lo(b, c):
            t, (s0, n) = c // KC, CHUNKS[c % KC]
            dve.wait_ge(khi_done, NCK * b.n + c + 1)
            nc.vector.scalar_tensor_tensor(k_lo[:, t, s0:s0 + n], pj[(b.slot + c) % 2][:, 0:n], w["bk"][:, t:t + 1],
                                           k_hi[:, t, s0:s0 + n], ALU.add, ALU.subtract).then_inc(klo_done, 1)

        def chunk_max(b, i):
            p, c = i // KC, i % KC
            s0, n = MAXCH[c]
            dve.wait_ge(sm_ready, NMX * b.n + i + 1)
            nc.vector.memset(lead[:, i:i + 1], 0.0)
            nc.vector.tensor_tensor_reduce(junk[(b.slot + i) % 2][:, 0:n], sm[(b.slot + i) % 2][:, 0:n], w["mask_q"][:, s0:s0 + n],
                                           1.0, -3.0e38, ALU.add, ALU.max, part_max[:, p, c:c + 1]).then_inc(sm_done, 1)

        def maxima(b):
            dve.wait_ge(sm_done, NMX * (b.n + 1))
            nc.vector.tensor_reduce(row_max[:], part_max[:], AX.X, ALU.max).then_inc(max_found, 1)
            dve.wait_ge(max_found, b.n + 1)
            nc.vector.tensor_scalar(shift[:], row_max[:], -1.0 / SEL, None, ALU.mult).then_inc(shift_ready, 1)

        def shift_in(b):
            dve.wait_ge(shift_rows, b.n + 1)
            rows = sm[b.slot][0:PAIRS, 0:PW].unsqueeze(1).to_broadcast([PAIRS, PAIRS, PW])
            nc.vector.tensor_copy(qstack[b.slot][KSTACK:KROWS, :, :], rows).then_inc(shift_done, 1)

        def normalizers(b):
            o = ob[b.slot]
            dve.wait_ge(sums_ready, b.n + 1)
            nc.vector.reciprocal(rsum[:], o[:, NK * PW:2 * NK * PW].rearrange("p (t c) -> p t c", t=NK)).then_inc(rsum_done, 1)

        def outputs(b):
            o = ob[b.slot]
            dve.wait_ge(rsum_done, b.n + 1)
            nc.vector.tensor_tensor(o_norm[:], o[:, 0:NK * PW].rearrange("p (t c) -> p t c", t=NK), rsum[:],
                                    ALU.mult).then_inc(o_read, 1)
            dve.wait_ge(o_read, b.n + 1)
            for t in range(NK):
                nc.vector.tensor_scalar(o_even[:, t, :], o_norm[:, t, 0:S], w["even_rows"][:, 0:1], w["bv"][:, t:t + 1],
                                        ALU.mult, ALU.add).then_inc(even_done, 1)
            dve.wait_ge(even_done, NK * (b.n + 1))
            nc.vector.scalar_tensor_tensor(attn_out[:, :, bass.ds(b.n * S, S)], o_norm[:, :, S:2 * S], w["even_rows"][:, 1:2],
                                           o_even[:], ALU.mult, ALU.add).then_inc(out_done, 1)

        def turn(cur, nxt, split, third):
            for kt in range(KT):
                for what, i in slots[kt]:
                    if what == "K" and nxt:
                        keys_lo(nxt, i)
                    if what == "M" and nxt:
                        chunk_max(nxt, i)
                    if what == "G" and nxt:
                        maxima(nxt)
                    if what == "T" and nxt:
                        shift_in(nxt)
                    if what == "X" and split:
                        split_lo(split, i)
                    if what == "N" and cur and not first(cur):
                        normalizers(before(cur))
                    if what == "O" and cur and not first(cur):
                        outputs(before(cur))
                    if what == "S" and i == 1 and cur and last(cur) and kt:
                        add_rows(dve, nc.vector, cur, kt)
        turns(dve, turn)
        normalizers(at(B - 1))
        outputs(at(B - 1))

    def tensor(pe):
        def piece_free(b, j):
            if j < 2:
                need(pe, v_done, KT * (b.n - 1) + KT - 1 + j)
            elif j - 2 < NCK:
                pe.wait_ge(klo_done, NCK * b.n + j - 1)
            else:
                pe.wait_ge(v_done, KT * b.n + j - 1 - NCK)

        def keys(b, c):
            t, (s0, n) = c // KC, CHUNKS[c % KC]
            if c < KC:
                pe.wait_ge(ctx_lo, SPLIT * b.n + NK * (c + 1))
            piece_free(b, c)
            o = pj[(b.slot + c) % 2][:, 0:n]
            terms = [(wp, cp, k) for k in range(NK) for wp, cp in (("wk_hi", c_hi), ("wk_lo", c_hi), ("wk_hi", c_lo))]
            for i, (wp, cp, k) in enumerate(terms):
                mm = nc.tensor.matmul(o, w[wp][:, k, t * P:(t + 1) * P], cp[:, k, s0:s0 + n],
                                      start=i == 0, stop=i == len(terms) - 1)
            mm.then_inc(k_proj, 1)

        def values(b, j):
            m = keys_of(j)
            piece_free(b, NCK + j)
            o = pj[(b.slot + NCK + j) % 2][0:m, 0:D]
            terms = [(wp, cp, k) for k in range(NK) for wp, cp in (("wv_hi", c_hi), ("wv_lo", c_hi), ("wv_hi", c_lo))]
            for i, (wp, cp, k) in enumerate(terms):
                mm = nc.tensor.matmul(o, cp[:, k, j * P:j * P + m], w[wp][:, k, :],
                                      start=i == 0, stop=i == len(terms) - 1)
            mm.then_inc(v_proj, 1)

        def chunk_scores(b, i):
            p, (s0, n) = i // KC, MAXCH[i % KC]
            if i == 0:
                pe.wait_ge(qstack_in[b.slot], 16 * QSTACK_DMAS * b.used)
            if i % KC == 0:
                pe.wait_ge(kstack_in[b.slot][p], 16 * STACK_DMAS * b.used)
            if i == 1:
                need(pe, shift_done, b.n)
            elif i == 0:
                need(pe, sm_done, NMX * b.n)
            else:
                pe.wait_ge(sm_done, NMX * b.n + i - 1)
            nc.tensor.matmul(sm[(b.slot + i) % 2][:, 0:n], qstack[b.slot][0:KSTACK, p, :],
                             kstack[b.slot][0:KSTACK, p, s0:s0 + n], start=True, stop=True).then_inc(sm_ready, 1)

        def turn_shift(b):
            pe.wait_ge(shift_ready, b.n + 1)
            nc.tensor.transpose(sm[b.slot][0:PAIRS, 0:P], shift[:], ident[:]).then_inc(shift_rows, 1)

        def scores(b, kt, h, masked):
            m = keys_of(kt)
            if kt == 0 and h == 0:
                pe.wait_ge(shift_done, b.n + 1)
            need(pe, exp_done, NST * b.n + 2 * kt + h - 1)
            if masked:
                mask = w["mask_k"][0:m, kt, :].unsqueeze(1).to_broadcast([m, 2 * GROUPS, S])
                nc.tensor.matmul(st[h][0:m, :], w["ident_h"][0:m, 0:m], mask, start=True, stop=True, skip_group_check=True)
            for g in range(GROUPS):
                p = GROUPS * h + g
                mm = nc.tensor.matmul(st[h][0:m, g * PW:(g + 1) * PW], kstack[b.slot][0:KROWS, p, kt * P:kt * P + m],
                                      qstack[b.slot][0:KROWS, p, :], start=not masked and g == 0, stop=True, skip_group_check=True)
            mm.then_inc(st_ready, 1)

        def products(b, kt):
            m = keys_of(kt)
            if kt == 0:
                pe.wait_ge(v_done, KT * (b.n + 1))
                need(pe, o_read, b.n - 1)
            pe.wait_ge(exp_done, NST * b.n + 2 * kt + 2)
            for t in range(NK):
                for g in range(GROUPS):
                    p = GROUPS * t + g
                    mm = nc.tensor.matmul(ob[b.slot][32 * g:32 * g + 32, t * PW:(t + 1) * PW],
                                          v[b.slot][0:m, kt, 32 * p:32 * p + 32], probs[kt % NP][0:m, p, :],
                                          start=kt == 0 and t == 0, stop=kt == KT - 1, skip_group_check=True)
            mm.then_inc(pv_done, 1)

        def row_sums(b):
            pe.wait_ge(acc_done, NACC * (b.n + 1))
            for t in range(NK):
                for g in range(GROUPS):
                    c0 = (NK + t) * PW
                    mm = nc.tensor.matmul(ob[b.slot][32 * g:32 * g + 32, c0:c0 + PW], w["ones"][:],
                                          acc[b.slot][:, GROUPS * t + g, :], start=False, stop=True, skip_group_check=True)
            mm.then_inc(sums_ready, 1)

        pe.wait_ge(first_in["rows_in"], 2 * 16)

        def run(masked):
            def turn(cur, nxt, split, third):
                for kt in range(KT):
                    for what, i in slots[kt]:
                        if cur:
                            if what == "S":
                                scores(cur, kt, i, masked)
                            if what == "P":
                                products(cur, i)
                            if what == "L" and not first(cur):
                                products(before(cur), KT - 1)
                            if what == "R" and not first(cur):
                                row_sums(before(cur))
                        if nxt:
                            if what == "K":
                                keys(nxt, i)
                            if what == "V":
                                values(nxt, i)
                            if what == "M":
                                chunk_scores(nxt, i)
                            if what == "T":
                                turn_shift(nxt)
            turns(pe, turn)
            products(at(B - 1), KT - 1)
            row_sums(at(B - 1))

        rows_all = pe.value_load(w["rows_all"][0:1, 0:1], min_val=0, max_val=S)
        with pe.If(rows_all == S):
            run(masked=False)
        with pe.Else():
            run(masked=True)

    return {"sync": sync, "vector": vector, "gpsimd": gpsimd, "scalar": scalar, "tensor": tensor}


def tail(nc, ins, bank, attn_out, wo, bo, wo_in, mean_w, eps_col, out_dram, sem):
    with ExitStack() as own:
        def sb(name, shape, dt=F32):
            return own.enter_context(nc.sbuf_tensor(name, shape, dt))

        x = sb("x", [P, NK, NTOK])
        h2 = sb("h2", [P, NK, NTOK])
        wval, wout = (sb(n, [P, NK, D]) for n in ("wval", "wout"))
        wspan = sb("wspan", [P, NK, SPAN_ROWS])
        sel_a, sel_b = sb("sel_a", [33, PAIRS, P], F32R), sb("sel_b", [B_ROWS, PAIRS, P], F32R)
        head_ones = sb("head_ones", [P, 32])
        sw1, sw3 = ([sb(n + part, [P, NK, HS], F32R) for part in ("_hi", "_lo")] for n in ("sw1", "sw3"))
        w1 = [[sb(f"w1_{part}{i}", [P, NK, D], F32R) for part in ("hi", "lo")] for i in range(W_SLOTS)]
        weight = [sb(f"weight{i}", [P, NK * HS]) for i in range(2)]
        sb1, sb3 = sb("sb1", [P, HS // P]), sb("sb3", [P, HS // P])
        sb2, b1, b2 = sb("sb2", [P, NK]), sb("b1", [P, E, NK]), sb("b2", [P, E, NK])
        class_bias = sb("class_bias", [P, E, NK])
        bias_a, bias_b = sb("bias_a", [P, NK]), sb("bias_b", [P, NK])
        x_in = [sem(f"t_x_in{c}") for c in range(NCH)]
        w_in, sel_in, f_in, y_out = (sem("t_" + n) for n in ("w_in", "sel_in", "f_in", "y_out"))
        h2_done, f_done = sem("t_h2_done"), sem("t_f_done")

        def toks(c):
            return slice(c * CW, (c + 1) * CW)

        with nc.Block() as block:
            with ExitStack() as span:
                spans = span_attention(nc, span, bank, sem, mean_w, eps_col, attn_out, x, h2, wo, bo, wspan, wval, wout,
                                       sel_a, sel_b, head_ones, x_in, wo_in, w_in, sel_in, h2_done)
            mlps = expert_mlps(nc, own, bank, sem, ins, x, h2, weight, sw1, sw3, w1, sb1, sb3, b1, class_bias, f_in, h2_done, f_done)

            @block.sync
            def _(sp):
                def load(tile, src, done):
                    sp.dma_start(tile, src).then_inc(done, 16)

                def rows(name):
                    return ins[name].rearrange("(k p) n -> p k n", p=P)

                load(x[:, :, toks(0)], rows("xT")[:, :, toks(0)], x_in[0])
                for name, tile in (("wspanT", wspan), ("wvalT", wval), ("woutT", wout)):
                    load(tile[:], rows(name), w_in)
                load(head_ones[:], ins["c_head_ones"], w_in)
                for c in range(1, NCH):
                    load(x[:, :, toks(c)], rows("xT")[:, :, toks(c)], x_in[c])
                for name, tile in (("sb1", sb1), ("sb3", sb3), ("sb2", sb2)):
                    load(tile[:], ins[name], f_in)
                for name, tile in (("b1", b1), ("b2", b2)):
                    load(tile[:], ins[name].rearrange("p (e k) -> p e k", k=NK), f_in)
                mlps["sync"](sp)
                sp.wait_ge(f_done, NK * E)
                sp.dma_start(out_dram.rearrange("(k p) t -> p k t", p=P), x[:]).then_inc(y_out, 16)
                sp.wait_ge(y_out, 16)

            @block.gpsimd
            def _(pool):
                for name, tile in (("c_sel_a", sel_a), ("c_sel_b", sel_b)):
                    pool.dma_start(tile[:], ins[name].rearrange("r (p m) -> r p m", m=P)).then_inc(sel_in, 16)
                mlps["gpsimd"](pool)

            @block.scalar
            def _(act):
                nc.scalar.preload_act_table_set("natural_log_exp_and_others")
                spans["scalar"](act)
                mlps["scalar"](act)

            @block.vector
            def _(dve):
                def fold():
                    bias_steps = sem("t_bias_steps")
                    done = [0]

                    def step(instruction):
                        instruction.then_inc(bias_steps, 1)
                        done[0] += 1
                        dve.wait_ge(bias_steps, done[0])
                    dve.wait_ge(f_in, 5 * 16)
                    step(nc.vector.tensor_scalar(bias_a[:], sb2[:], 0.5, None, ALU.mult))
                    for c in range(E):
                        ea, eb = CLASS_EXPERTS[c]
                        step(nc.vector.tensor_tensor(bias_b[:], b2[:, ea, :], b2[:, eb, :], ALU.add))
                        step(nc.vector.scalar_tensor_tensor(class_bias[:, c, :], bias_b[:], 0.25, bias_a[:], ALU.mult, ALU.add))
                spans["vector"](dve, fold)
                mlps["vector"](dve)

            @block.tensor
            def _(pe):
                spans["tensor"](pe)
                mlps["tensor"](pe)


def span_attention(nc, own, bank, sem, mean_w, eps_col, attn_out, x, h2, wo, bo, wspan, wval, wout,
                   sel_a, sel_b, head_ones, x_in, wo_in, w_in, sel_in, h2_done):
    def sb(name, shape, dt=F32):
        return own.enter_context(nc.sbuf_tensor(name, shape, dt))

    UNITS = PAIRS
    QUADS = CB // 2
    xc = [sb(f"t_xc{i}", [P, NK, CW]) for i in range(2)]
    sq = [sb(f"t_sq{i}", [P, NK, CW]) for i in range(2)]
    rstd = [sb(f"t_rstd{i}", [P, CW]) for i in range(2)]
    h = [sb(f"t_h{i}", [P, NK, CW]) for i in range(2)]
    e0, lnx, near = sb("e0", [H, CW]), sb("lnx", [SPAN_ROWS, CW]), sb("near", [H, CW])
    soft, gap = sb("soft", [H, CW]), sb("gap", [H, CW])
    rows_a = [sb(f"rows_a{i}", [33, CW], F32R) for i in range(2)]
    rows_b = [sb(f"rows_b{i}", [B_ROWS, CW], F32R) for i in range(2)]
    b_copy = [sb(f"b_copy{i}", [P, CW]) for i in range(2)]
    dist = [sb(f"dist{i}", [P, CW]) for i in range(2)]
    ex = sb("ex", [P, PAIRS, CW])
    vbd = sb("vbd", [P, CB, D])
    rs, o2 = sb("rs", [P, NK, CW]), sb("o2", [P, NK, CW])

    proj, ln_bank, ab, vb = bank[0:2], bank[2:4], bank[4:6], bank[6:8]
    factors = [ab, vb]
    names = ("x1_proj x1_done x2_proj x2_done span e0_done lnx_abs lnx_exp lnx_done vec rows_zero vbd_zero rows_done spans_read ab_ready b_copied "
             "dist_done ex_done sums lns_done rs_done val_ready vbd_done pv o2_done h_done").split()
    s = {n: sem("t_" + n) for n in names}
    s["h2_done"] = h2_done
    mean, xc_done, sq_done, var, lnv, rstd_done = ([sem(f"t_{n}{i}") for i in range(2)]
                                                   for n in ("mean", "xc", "sq", "var", "lnv", "rstd"))
    norm_done = [s["h_done"], h2_done]
    src_done = [s["x1_done"], s["x2_done"]]

    PE_ORDER = "M0 Z A M1 A V0 A V1 A A A S A A W X X X X U O"
    DVE_ORDER = "C0 Z A C1 A A N0 A A A N1 A A W R O"
    ACT_ORDER = "A Q0 A Q1 A I0 A A A I1 A A S E X X X X U"

    SOON, NOW, NEXT, LAST = 0, 1, 2, 3

    def norm_steps(table, letter, do):
        table[letter + "0"], table[letter + "1"] = (NOW, do, 0), (LAST, do, 1)
        return table

    def scalar(act):
        def square(c, j):
            act.wait_ge(xc_done[j], c + 1)
            need(act, var[j], c)
            nc.scalar.activation(sq[j][:], xc[j][:], ACT.Square).then_inc(sq_done[j], 1)

        def inverse(c, j):
            act.wait_ge(var[j], c + 1)
            need(act, norm_done[j], c)
            nc.scalar.activation(rstd[j][:], ln_bank[j][:, :], ACT.Ln, bias=eps_col[:, 0:1]).then_inc(lnv[j], 1)
            act.wait_ge(lnv[j], c + 1)
            nc.scalar.activation(rstd[j][:], rstd[j][:], ACT.Exp, scale=-0.5).then_inc(rstd_done[j], 1)

        def spans(c, _):
            act.wait_ge(s["span"], c + 1)
            need(act, s["rows_done"], c)
            nc.scalar.activation(e0[:], ln_bank[0][0:H, :], ACT.Exp, scale=-1.0).then_inc(s["e0_done"], 1)
            x_rows = lnx[SOFT_ROW:SOFT_ROW + H, :]
            nc.scalar.activation(x_rows, ln_bank[0][SOFT_ROW:SOFT_ROW + H, :], ACT.Abs).then_inc(s["lnx_abs"], 1)
            act.wait_ge(s["lnx_abs"], c + 1)
            nc.scalar.activation(x_rows, x_rows, ACT.Exp, scale=-1.0).then_inc(s["lnx_exp"], 1)
            act.wait_ge(s["lnx_exp"], c + 1)
            nc.scalar.activation(x_rows, x_rows, ACT.Ln, bias=1.0).then_inc(s["lnx_done"], 1)

        def exponential(c, i):
            n = UNITS * c + i
            act.wait_ge(s["dist_done"], n + 1)
            if i == 0:
                need(act, s["pv"], c)
            nc.scalar.activation(ex[:, i, :], dist[i % 2][:], ACT.Exp, scale=-1.0).then_inc(s["ex_done"], 1)

        def unit(c, i):
            n = UNITS * c + i
            act.wait_ge(s["ab_ready"], n + 1)
            need(act, s["dist_done"], n - 1)
            nc.scalar.activation(b_copy[i % 2][:], factors[i % 2][1][:, :], ACT.Copy).then_inc(s["b_copied"], 1)
            if i:
                exponential(c, i - 1)

        def values(c, q):
            act.wait_ge(s["val_ready"], QUADS * c + q + 1)
            if q == 0:
                act.wait_ge(s["vbd_zero"], 1)
                need(act, s["pv"], c)
            for r in range(2):
                for e in range(2):
                    i = nc.scalar.activation(heads(vbd[S * e:S * (e + 1), 2 * q + r, :], e),
                                             heads(vb[q % 2][S * r:S * (r + 1), 0:D], e), ACT.Copy)
            i.then_inc(s["vbd_done"], 1)

        def sums(c, _):
            act.wait_ge(s["sums"], c + 1)
            need(act, s["o2_done"], c)
            for t in range(NK):
                i = nc.scalar.activation(rs[:, t, :], ab[t][:, :], ACT.Ln)
            i.then_inc(s["lns_done"], 1)
            act.wait_ge(s["lns_done"], c + 1)
            nc.scalar.activation(rs[:], rs[:], ACT.Exp, scale=-1.0).then_inc(s["rs_done"], 1)

        table = {"S": (NOW, spans, None), "A": (NEXT, unit, None), "E": (NEXT, exponential, UNITS - 1), "X": (NEXT, values, None),
                 "U": (NEXT, sums, None)}
        run_periods(ACT_ORDER, norm_steps(norm_steps(table, "Q", square), "I", inverse))

    def heads(ap, e):
        return ap.rearrange("p (q e d) -> p q e d", e=2, d=DK)[:, :, e, :]

    def vector(dve, between):
        steps = [0]

        def step(instruction):
            instruction.then_inc(s["vec"], 1)
            steps[0] += 1
            dve.wait_ge(s["vec"], steps[0])

        def residual(c, j):
            if j == 0:
                if c == 0:
                    dve.wait_ge(wo_in, 2 * 16)
                dve.wait_ge(x_in[c], 16)
                dve.wait_ge(s["x1_proj"], c + 1)
                for k in range(NK):
                    nc.vector.scalar_tensor_tensor(x[:, k, toks(c)], proj[k][:, :], bo[:, k:k + 1], x[:, k, toks(c)],
                                                   ALU.add, ALU.add).then_inc(s["x1_done"], 1)
            else:
                dve.wait_ge(s["x2_proj"], c + 1)
                for k in range(NK):
                    nc.vector.tensor_tensor(x[:, k, toks(c)], ab[k][:, :], x[:, k, toks(c)], ALU.add).then_inc(s["x2_done"], 1)

        def centre(c, j):
            dve.wait_ge(mean[j], c + 1)
            dve.wait_ge(src_done[j], NK * (c + 1))
            need(dve, norm_done[j], c)
            for k in range(NK):
                i = nc.vector.tensor_tensor(xc[j][:, k, :], x[:, k, toks(c)], ln_bank[j][:, :], ALU.subtract)
            i.then_inc(xc_done[j], 1)

        def normalize(c, j):
            dve.wait_ge(rstd_done[j], c + 1)
            dve.wait_ge(xc_done[j], c + 1)
            if j == 0:
                need(dve, s["val_ready"], QUADS * (c - 1))
            for k in range(NK):
                dst = h[c % 2][:, k, :] if j == 0 else h2[:, k, toks(c)]
                i = nc.vector.tensor_tensor(dst, xc[j][:, k, :], rstd[j][:], ALU.mult)
            i.then_inc(norm_done[j], 1)

        def span_rows(c, _):
            ra, rb = rows_a[c % 2], rows_b[c % 2]
            dve.wait_ge(s["lnx_done"], c + 1)
            soft_rows = slice(SOFT_ROW, SOFT_ROW + H)
            nc.vector.scalar_tensor_tensor(soft[:], ln_bank[0][soft_rows, :], 0.0, lnx[soft_rows, :], ALU.max,
                                           ALU.add).then_inc(s["spans_read"], 1)
            dve.wait_ge(s["e0_done"], c + 1)
            need(dve, s["ab_ready"], UNITS * (c - 1))
            step(nc.vector.tensor_scalar(e0[:], e0[:], 1.0, None, ALU.add))
            dve.wait_ge(s["spans_read"], c + 1)
            step(nc.vector.reciprocal(gap[:], e0[:]))
            step(nc.vector.tensor_scalar(near[:], gap[:], float(S), ROUND, ALU.mult, ALU.add))
            step(nc.vector.tensor_scalar(ra[0:H, :], near[:], -ROUND, float(S - 1), ALU.add, ALU.min))
            step(nc.vector.scalar_tensor_tensor(near[:], gap[:], -2.0 * S, ra[0:H, :].bitcast(F32), ALU.mult, ALU.add))
            step(nc.vector.tensor_tensor(gap[:], near[:], soft[:], ALU.mult))
            for part, src in enumerate((soft, gap)):
                hi, lo = (rb[64 * part + 32 * i:64 * part + 32 * i + H, :] for i in range(2))
                step(nc.vector.tensor_copy(hi, src[:]))
                step(nc.vector.tensor_tensor(lo, src[:], hi.bitcast(F32), ALU.subtract))
            nc.vector.memset(done_mark[:], 0.0).then_inc(s["rows_done"], 1)

        def unit(c, i):
            n = UNITS * c + i
            dve.wait_ge(s["b_copied"], n + 1)
            need(dve, s["ex_done"], n - 1)
            nc.vector.tensor_tensor(dist[i % 2][:], factors[i % 2][0][:, :], b_copy[i % 2][:], ALU.mult).then_inc(s["dist_done"], 1)

        def outputs(c, _):
            dve.wait_ge(s["rs_done"], c + 1)
            dve.wait_ge(s["pv"], c + 1)
            need(dve, s["x2_proj"], c)
            for k in range(NK):
                i = nc.vector.tensor_tensor(o2[:, k, :], vb[k][:, :], rs[:, k, :], ALU.mult)
            i.then_inc(s["o2_done"], 1)
            if c == FOLD_CHUNK:
                between()

        for i in range(2):
            nc.vector.memset(rows_a[i][:].bitcast(F32), 0.0).then_inc(s["rows_zero"], 1)
            nc.vector.memset(rows_b[i][:].bitcast(F32), 0.0).then_inc(s["rows_zero"], 1)
        nc.vector.memset(vbd[:], 0.0).then_inc(s["vbd_zero"], 1)
        dve.wait_ge(s["rows_zero"], 4)
        for i in range(2):
            nc.vector.memset(rows_a[i][32:33, :].bitcast(F32), 1.0).then_inc(s["rows_zero"], 1)
        table = {"W": (SOON, residual, 0), "Z": (LAST, residual, 1), "R": (NOW, span_rows, None), "A": (NEXT, unit, None),
                 "O": (NEXT, outputs, None)}
        run_periods(DVE_ORDER, norm_steps(norm_steps(table, "C", centre), "N", normalize))

    def tensor(pe):
        def project(wt, src, dst, done):
            for m in range(NK):
                for k in range(NK):
                    i = nc.tensor.matmul(dst[m][:, :], wt[:, k, m * P:(m + 1) * P], src[k], start=k == 0, stop=k == NK - 1)
            i.then_inc(done, 1)

        def output_a(c, _):
            if c == 0:
                pe.wait_ge(wo_in, 2 * 16)
            need(pe, s["x1_done"], NK * c)
            project(wo, [attn_out[:, k, toks(c)] for k in range(NK)], proj, s["x1_proj"])

        def output_l(c, _):
            pe.wait_ge(s["o2_done"], c + 1)
            project(wout, [o2[:, k, :] for k in range(NK)], ab, s["x2_proj"])

        def means(c, j):
            pe.wait_ge(src_done[j], NK * (c + 1))
            need(pe, s["spans_read"] if j == 0 else rstd_done[1], c)
            for k in range(NK):
                i = nc.tensor.matmul(ln_bank[j][:, :], mean_w[:], x[:, k, toks(c)], start=k == 0, stop=k == NK - 1)
            i.then_inc(mean[j], 1)

        def variances(c, j):
            pe.wait_ge(sq_done[j], c + 1)
            for k in range(NK):
                i = nc.tensor.matmul(ln_bank[j][:, :], mean_w[:], sq[j][:, k, :], start=k == 0, stop=k == NK - 1)
            i.then_inc(var[j], 1)

        def spans(c, _):
            if c == 0:
                pe.wait_ge(w_in, 4 * 16)
                pe.wait_ge(sel_in, 2 * 16)
            pe.wait_ge(s["h_done"], c + 1)
            for k in range(NK):
                i = nc.tensor.matmul(ln_bank[0][0:SPAN_ROWS, :], wspan[:, k, :], h[c % 2][:, k, :], start=k == 0, stop=k == NK - 1)
            i.then_inc(s["span"], 1)

        def unit(c, i):
            n = UNITS * c + i
            if i == 0:
                pe.wait_ge(s["rows_zero"], 6)
                pe.wait_ge(s["rows_done"], c + 1)
                need(pe, s["x2_done"], NK * c)
            if i == 1:
                need(pe, s["o2_done"], c)
            need(pe, s["dist_done"], n - 1)
            nc.tensor.matmul(factors[i % 2][0][:, :], sel_a[:, i, :], rows_a[c % 2][:], start=True, stop=True)
            nc.tensor.matmul(factors[i % 2][1][:, :], sel_b[:, i, :], rows_b[c % 2][:], start=True,
                             stop=True).then_inc(s["ab_ready"], 1)

        def values(c, q):
            if q >= 2:
                pe.wait_ge(s["vbd_done"], QUADS * c + q - 1)
            else:
                pe.wait_ge(s["dist_done"], UNITS * (c + 1))
            for k in range(NK):
                i = nc.tensor.matmul(vb[q % 2][:, 0:D], h[c % 2][:, k, q * 2 * S:(q + 1) * 2 * S], wval[:, k, :],
                                     start=k == 0, stop=k == NK - 1)
            i.then_inc(s["val_ready"], 1)

        def sums(c, _):
            pe.wait_ge(s["ex_done"], UNITS * (c + 1))
            for p in range(PAIRS):
                t, g = p // GROUPS, p % GROUPS
                i = nc.tensor.matmul(ab[t][32 * g:32 * g + 32, :], head_ones[:], ex[:, p, :], start=True, stop=True)
            i.then_inc(s["sums"], 1)

        def products(c, _):
            pe.wait_ge(s["vbd_done"], QUADS * (c + 1))
            for b in range(CB):
                for p in range(PAIRS):
                    t, g = p // GROUPS, p % GROUPS
                    i = nc.tensor.matmul(vb[t][32 * g:32 * g + 32, b * S:(b + 1) * S], vbd[:, b, 32 * p:32 * p + 32],
                                         ex[:, p, b * S:(b + 1) * S], start=True, stop=True, skip_group_check=True)
            i.then_inc(s["pv"], 1)

        table = {"W": (SOON, output_a, None), "Z": (LAST, output_l, None), "S": (NOW, spans, None), "A": (NEXT, unit, None),
                 "X": (NEXT, values, None), "U": (NEXT, sums, None), "O": (NEXT, products, None)}
        run_periods(PE_ORDER, norm_steps(norm_steps(table, "M", means), "V", variances))

    def toks(c):
        return slice(c * CW, (c + 1) * CW)

    done_mark = sb("done_mark", [P, 1])
    return {"scalar": scalar, "vector": vector, "tensor": tensor}


def expert_mlps(nc, own, bank, sem, ins, x, h2, weight, sw1, sw3, w1, sb1, sb3, b1, class_bias, f_in, h2_done, f_done):
    def sb(name, shape, dt=F32):
        return own.enter_context(nc.sbuf_tensor(name, shape, dt))

    NC = NTOK // E
    FT = HS // P
    gate = [sb(f"gate{i}", [P, FT, NC]) for i in range(2)]
    gelu = sb("gelu", [P, 2, NK, NC])
    xb = [sb(f"xb{i}", [P, NK, NC]) for i in range(2)]

    def parts(name, shape, count):
        return [[sb(f"{name}_{part}{i}", shape, F32R) for part in ("hi", "lo")] for i in range(count)]

    tokens, gate_parts, gelu_parts = (parts(n, shape, 2) for n, shape in
                                      (("tokens", [P, NK, NC]), ("gate", [P, FT, NC]), ("gelu", [P, 2, NK, NC])))
    sw2, = parts("sw2", [P, FT, D], 1)
    w2 = parts("w2", [P, NK, D], W_SLOTS)
    s = {n: sem("t_" + n) for n in ("f1 f3 fe silu_done gate_done gelu_done f_out xb_done h_hi_done h_lo_done gate_hi_done "
                                    "gate_lo_done gelu_hi_done gelu_lo_done w_doubled w_hi_done w_lo_done").split()}
    s["f_done"] = f_done
    w_in = [sem(f"t_weight_in{i}") for i in range(2)]

    order, arrival = [0], list(CLASS_EXPERTS[0])
    while len(order) < E:
        c = next(c for c in range(E) if c not in order and arrival[-1] in CLASS_EXPERTS[c])
        order.append(c)
        arrival.append(next(e for e in CLASS_EXPERTS[c] if e != arrival[-1]))

    pieces = ["sw1", "sw3"] + [("w1", i) for i in range(W_SLOTS)]
    NFIRST = len(pieces)
    pieces += ["sw2"] + [("w2", i) for i in range(W_SLOTS)] + [(w, i) for i in range(W_SLOTS, E + 1) for w in ("w1", "w2")]

    def split_count(w, n):
        return pieces.index((w, n + 1)) + 1

    def slot_of(w, n, e):
        return {"w1": w1, "w2": w2}[w][(n if arrival[n] == e else n + 1) % W_SLOTS]

    def width(piece):
        return FT * D if isinstance(piece, str) else NK * D

    def cls(tile, k, c):
        return tile[:, k, :].rearrange("p (b c n) -> p b c n", c=E, n=S // E)[:, :, c, :]

    def flat(ap):
        return ap.rearrange("p (b n) -> p b n", n=S // E)

    def sync(sp):
        for n, piece in enumerate(pieces):
            if n >= 2:
                sp.wait_ge(s["w_lo_done"], n - 1)
            src = ins[piece] if isinstance(piece, str) else ins[piece[0]][arrival[piece[1]]]
            dst = weight[n % 2][:, 0:width(piece)].rearrange("p (k n) -> p k n", n=src.shape[-1])
            sp.dma_start(dst, src.rearrange("(k p) n -> p k n", p=P)).then_inc(w_in[n % 2], 16)

    def gpsimd(pool):
        for n, piece in enumerate(pieces):
            if n == NFIRST:
                pool.wait_ge(h2_done, NCH)
            whole = weight[n % 2][:, 0:width(piece)]
            pool.wait_ge(w_in[n % 2], 16 * (n // 2 + 1))
            if isinstance(piece, str):
                hi, lo = {"sw1": sw1, "sw2": sw2, "sw3": sw3}[piece]
            else:
                w, i = piece
                hi, lo = (w1 if w == "w1" else w2)[i % W_SLOTS]
                if i >= W_SLOTS:
                    pool.wait_ge(s["fe"] if w == "w1" else s["f_out"], i - W_SLOTS + 1)
            if piece == "sw2":
                nc.gpsimd.tensor_scalar(whole, whole, 2.0, None, ALU.mult).then_inc(s["w_doubled"], 1)
                pool.wait_ge(s["w_doubled"], 1)
            hi, lo = (part[:].rearrange("p k n -> p (k n)") for part in (hi, lo))
            nc.gpsimd.tensor_copy(hi, whole).then_inc(s["w_hi_done"], 1)
            pool.wait_ge(s["w_hi_done"], n + 1)
            nc.gpsimd.tensor_tensor(lo, whole, hi.bitcast(F32), ALU.subtract).then_inc(s["w_lo_done"], 1)

    def scalar(act):
        def tokens_hi(n):
            if n == 0:
                act.wait_ge(h2_done, NCH)
            if n >= 2:
                act.wait_ge(s["fe"], n - 1)
            for k in range(NK):
                i = nc.scalar.activation(flat(tokens[n % 2][0][:, k, :]), cls(h2, k, order[n]), ACT.Copy)
            i.then_inc(s["h_hi_done"], 1)

        tokens_hi(0)
        for n, c in enumerate(order):
            if n + 1 < E:
                tokens_hi(n + 1)
            act.wait_ge(s["f1"], n + 1)
            if n >= 2:
                act.wait_ge(s["gate_lo_done"], n - 1)
            for m in range(FT):
                i = nc.scalar.activation(gate[n % 2][:, m, :], bank[m // 2][:, (m % 2) * NC:(m % 2 + 1) * NC], ACT.Silu,
                                         bias=sb1[:, m:m + 1])
            i.then_inc(s["silu_done"], 1)
            act.wait_ge(s["fe"], n + 1)
            if n:
                act.wait_ge(s["gelu_lo_done"], n)
            for k in range(2):
                for m in range(NK):
                    e = CLASS_EXPERTS[c][k]
                    i = nc.scalar.activation(gelu[:, k, m, :], bank[4 + k][:, m * NC:(m + 1) * NC], ACT.Gelu, bias=b1[:, e, m:m + 1])
            i.then_inc(s["gelu_done"], 1)
            if n >= 2:
                act.wait_ge(s["f_out"], n - 1)
            act.wait_ge(s["gate_done"], n + 1)
            nc.scalar.activation(gate_parts[n % 2][0][:], gate[n % 2][:], ACT.Copy).then_inc(s["gate_hi_done"], 1)
            act.wait_ge(s["gelu_done"], n + 1)
            nc.scalar.activation(gelu_parts[n % 2][0][:], gelu[:], ACT.Copy).then_inc(s["gelu_hi_done"], 1)

    def vector(dve):
        def tokens_lo(n):
            dve.wait_ge(s["h_hi_done"], n + 1)
            if n >= 2:
                dve.wait_ge(s["fe"], n - 1)
            for k in range(NK):
                i = nc.vector.tensor_tensor(flat(tokens[n % 2][1][:, k, :]), cls(h2, k, order[n]),
                                            flat(tokens[n % 2][0][:, k, :].bitcast(F32)), ALU.subtract)
            i.then_inc(s["h_lo_done"], 1)

        def gates(n):
            dve.wait_ge(s["f3"], n + 1)
            dve.wait_ge(s["silu_done"], n + 1)
            for m in range(FT):
                i = nc.vector.scalar_tensor_tensor(gate[n % 2][:, m, :], bank[2 + m // 2][:, (m % 2) * NC:(m % 2 + 1) * NC],
                                                   sb3[:, m:m + 1], gate[n % 2][:, m, :], ALU.add, ALU.mult)
            i.then_inc(s["gate_done"], 1)

        def rest(whole, parts, n, hi_done, done):
            dve.wait_ge(hi_done, n + 1)
            nc.vector.tensor_tensor(parts[1][:], whole[:], parts[0][:].bitcast(F32), ALU.subtract).then_inc(done, 1)

        def result(n):
            dve.wait_ge(s["f_out"], n + 1)
            dve.wait_ge(s["xb_done"], NK * (n + 1))
            for k in range(NK):
                nc.vector.scalar_tensor_tensor(cls(x, k, order[n]), flat(bank[6][:, k * NC:(k + 1) * NC]), 0.25,
                                               flat(xb[n % 2][:, k, :]), ALU.mult, ALU.add).then_inc(s["f_done"], 1)

        tokens_lo(0)
        for n, c in enumerate(order):
            if n + 1 < E:
                tokens_lo(n + 1)
            gates(n)
            for k in range(NK):
                need(dve, f_done, NK * (n - 1))
                i = nc.vector.tensor_scalar(flat(xb[n % 2][:, k, :]), cls(x, k, c), class_bias[:, c, k:k + 1], None, ALU.add)
                i.then_inc(s["xb_done"], 1)
            rest(gate[n % 2], gate_parts[n % 2], n, s["gate_hi_done"], s["gate_lo_done"])
            rest(gelu, gelu_parts[n % 2], n, s["gelu_hi_done"], s["gelu_lo_done"])
            if n:
                result(n - 1)
        result(E - 1)

    def tensor(pe):
        def accumulate(dst, terms):
            passes = [p for (w_hi, w_lo), (x_hi, x_lo) in terms for p in ((w_hi, x_hi), (w_hi, x_lo), (w_lo, x_hi))]
            for n, (lhs, rhs) in enumerate(passes):
                i = nc.tensor.matmul(dst, lhs, rhs, start=n == 0, stop=n == len(passes) - 1)
            return i

        def columns(parts, k, m):
            return [part[:, k, m * P:(m + 1) * P] for part in parts]

        def row(parts, *k):
            return [part[(slice(None),) + k] for part in parts]

        def hidden(n, weights, banks, done, free):
            if n:
                pe.wait_ge(free, n)
            for m in range(FT):
                i = accumulate(bank[banks + m // 2][:, (m % 2) * NC:(m % 2 + 1) * NC],
                               [(columns(weights, k, m), row(tokens[n % 2], k)) for k in range(NK)])
            i.then_inc(done, 1)

        def experts(n):
            if n:
                pe.wait_ge(s["gelu_done"], n)
            pe.wait_ge(s["w_lo_done"], split_count("w1", n))
            for j, e in enumerate(CLASS_EXPERTS[order[n]]):
                for m in range(NK):
                    i = accumulate(bank[4 + j][:, m * NC:(m + 1) * NC],
                                   [(columns(slot_of("w1", n, e), k, m), row(tokens[n % 2], k)) for k in range(NK)])
            i.then_inc(s["fe"], 1)

        def output(n):
            pe.wait_ge(s["w_lo_done"], split_count("w2", n))
            pe.wait_ge(s["gate_lo_done"], n + 1)
            pe.wait_ge(s["gelu_lo_done"], n + 1)
            if n:
                pe.wait_ge(s["f_done"], NK * n)
            for m in range(NK):
                terms = [(columns(sw2, k, m), row(gate_parts[n % 2], k)) for k in range(FT)]
                terms += [(columns(slot_of("w2", n, e), k, m), row(gelu_parts[n % 2], j, k))
                          for j, e in enumerate(CLASS_EXPERTS[order[n]]) for k in range(NK)]
                i = accumulate(bank[6][:, m * NC:(m + 1) * NC], terms)
            i.then_inc(s["f_out"], 1)

        pe.wait_ge(s["w_lo_done"], 2)
        for n in range(E + 1):
            if n < E:
                pe.wait_ge(s["h_lo_done"], n + 1)
                hidden(n, sw1, 0, s["f1"], s["silu_done"])
                hidden(n, sw3, 2, s["f3"], s["gate_done"])
                experts(n)
            if n:
                output(n - 1)

    return {"sync": sync, "gpsimd": gpsimd, "scalar": scalar, "vector": vector, "tensor": tensor}


def constants():
    rows = np.arange(P)
    position = np.arange(S) % (S // E) * E + np.arange(S) // (S // E)
    even = np.stack([rows % 32 < DK, rows % 32 >= DK], 1).astype(np.float32)
    select = np.zeros((PAIRS, PAIRS, S2P), np.float16)
    sel_a = np.zeros((33, PAIRS, P), np.float32)
    sel_b = np.zeros((B_ROWS, PAIRS, P), np.float32)
    for p in range(PAIRS):
        select[p, p] = SEL
        for e in range(2):
            part = slice(S * e, S * e + S)
            sel_a[2 * p + e, p, part] = -1.0
            sel_a[32, p, part] = position
            for i in range(2):
                sel_b[32 * i + 2 * p + e, p, part] = position
                sel_b[64 + 32 * i + 2 * p + e, p, part] = 1.0
    half = rows[:, None] // S
    return {
        "c_ident": np.eye(P, dtype=np.float32),
        "c_even": even,
        "c_select": select.reshape(PAIRS, -1),
        "c_sel_a": sel_a.reshape(33, -1),
        "c_sel_b": sel_b.reshape(B_ROWS, -1),
        "c_head_ones": (half == np.arange(32)[None] // DK).astype(np.float32),
    }


def kernel(**inputs):
    import concourse.bacc as bacc
    from concourse.bass_utils import run_bass_kernel_spmd

    a = {n: np.asarray(v) for n, v in inputs.items()}
    order = np.arange(S).reshape(S // E, E).T.reshape(-1)

    def cols(vec):
        return vec.reshape(-1, P).T

    span = a["L0_attn_W_span"]
    mask = a["mask_1x1xSxS2_bf1"][0, 0][order].view(np.uint8)
    maskT = np.ones((KT * P, S), np.uint8)
    maskT[:S2] = mask.T
    ctxT = np.zeros((B, D, S2P), np.float32)
    ctxT[:, :, :S2] = a["ctx_1024"].transpose(0, 2, 1)
    arrays = {
        "xT": a["x"][:, order].reshape(NTOK, D).T,
        "ctxT": ctxT,
        "maskQ": mask,
        "maskT": maskT,
        "wqT": a["L0_xattn_wq_w"].T, "wkT": a["L0_xattn_wk_w"].T, "wvT": a["L0_xattn_wv_w"].T, "woT": a["L0_xattn_wo_w"].T,
        "bq": cols(a["L0_xattn_wq_b"]), "bk": cols(a["L0_xattn_wk_b"]), "bv": cols(a["L0_xattn_wv_b"]), "bo": cols(a["L0_xattn_wo_b"]),
        "wspanT": np.concatenate([span[0::2], np.zeros((SOFT_ROW - H, D), np.float32), span[1::2]]).T,
        "wvalT": a["L0_attn_W_val"].T, "woutT": a["L0_attn_W_out"].T,
        "sw1": a["L0_ffn_sw1"], "sw3": a["L0_ffn_sw3"], "sw2": a["L0_ffn_sw2"],
        "sb1": cols(a["L0_ffn_sb1"]), "sb3": cols(a["L0_ffn_sb3"]), "sb2": cols(a["L0_ffn_sb2"]),
        "w1": a["L0_ffn_w1"], "w2": a["L0_ffn_w2"],
        "b1": cols(a["L0_ffn_b1"].reshape(-1)), "b2": cols(a["L0_ffn_b2"].reshape(-1)),
        **constants(),
    }
    arrays = {n: np.ascontiguousarray(v) for n, v in arrays.items()}

    nc = bacc.Bacc("TRN2", target_bir_lowering=False, num_devices=1)
    ins = {n: nc.dram_tensor(f"in_{n}", v.shape, mybir.dt.from_np(v.dtype), kind="ExternalInput").ap() for n, v in arrays.items()}
    out = nc.dram_tensor("out_yT", (D, NTOK), F32, kind="ExternalOutput").ap()
    build(nc, ins, out)
    r = run_bass_kernel_spmd(nc, [{f"in_{n}": v for n, v in arrays.items()}], core_ids=[0])
    yT = r.results[0]["out_yT"]
    return np.ascontiguousarray(yT.reshape(D, B, E, S // E).transpose(1, 3, 2, 0).reshape(B, S, D))
```
